# Optimizing a Trainium2 kernel written in Bass

```python
import numpy as np
import jax
import jax.numpy as jnp

def _softmax(x, axis=-1):
    return jax.nn.softmax(x, axis=axis)

def _gelu(x):
    return jax.nn.gelu(x, approximate=True)

def _silu(x):
    return jax.nn.silu(x)

def _sigmoid(x):
    return jax.nn.sigmoid(x)

def _layernorm(x, axis=-1, eps=1e-05):
    m = jnp.mean(x, axis=axis, keepdims=True)
    v = jnp.var(x, axis=axis, keepdims=True)
    return (x - m) / jnp.sqrt(v + eps)

def _scatter_add(tgt, idx, src, axis=0):
    return tgt.at[idx].add(src)

def _segment_sum(src, seg, n):
    return jax.ops.segment_sum(src, seg, n)
kernel_name = 'mk_flamingo_gated_d1_seqx_r2_4cf26c'

def setup_inputs(seed: int=0):
    np.random.seed(seed)
    _w = jnp.asarray

    def _rec_inputs():
        import jax
        import jax.numpy as jnp
        _rk = jax.random.key(seed)
        x = -0.0002928 + 1 * jax.random.normal(jax.random.fold_in(_rk, 1), (8, 512, 512), jnp.float32)
        _lenS = 512 - jax.random.randint(jax.random.fold_in(_rk, 7), (8,), 0, max(1, 512 // 4) + 1, jnp.int32)
        _lenS2 = 512 - jax.random.randint(jax.random.fold_in(_rk, 8), (8,), 0, max(1, 512 // 4) + 1, jnp.int32)
        _ctx_1024P = jax.random.normal(jax.random.fold_in(_rk, 11), (8, 16, 512), jnp.float32)
        _ctx_1024c = jax.random.dirichlet(jax.random.fold_in(_rk, 511), 0.3 * jnp.ones((16,), jnp.float32), (8, 512))
        _ctx_1024t = jnp.einsum('bsk,bkd->bsd', _ctx_1024c, _ctx_1024P)
        _ctx_1024t = _ctx_1024t * jax.lax.rsqrt(jnp.mean(jnp.square(_ctx_1024t)) + 1e-12) * 0.953939
        ctx_1024 = -1.39393e-06 + 0.999914 * (_ctx_1024t + 0.3 * jax.random.normal(jax.random.fold_in(_rk, 611), (8, 512, 512), jnp.float32))
        _validS = jnp.arange(512)[None, :] < _lenS[:, None]
        _validS2 = jnp.arange(512)[None, :] < _lenS2[:, None]
        _causal = jnp.tril(jnp.ones((512, 512), dtype=bool))
        mask_BxS2_bf0 = jnp.logical_not(jnp.ones((8, 512), dtype=bool))
        _g = jax.random.normal(jax.random.fold_in(_rk, 9001), (2, 1), jnp.float32)
        _g = jnp.sign(_g) * jnp.maximum(jnp.abs(_g), 1.0) + (_g == 0) * 1.0
        g_xattn = _g[0]
        g_ffn = _g[1]
        return (x, ctx_1024, mask_BxS2_bf0, g_xattn, g_ffn)
    x, ctx_1024, mask_BxS2_bf0, g_xattn, g_ffn = _rec_inputs()

    def _L0_xattn_setup():
        import jax, jax.numpy as jnp
        import numpy as np
        import math
        D_MODEL = 512
        NUM_HEADS = 16
        D_K = D_MODEL // NUM_HEADS
        MAX_REL = 64
        B, L = (2, 1024)
        key = jax.random.key(seed)
        ks = jax.random.split(key, 12)
        s = 1.0 / math.sqrt(D_MODEL)
        inp = {'query': jax.random.normal(ks[0], (B, L, D_MODEL), jnp.float32), 'key': jax.random.normal(ks[1], (B, L, D_MODEL), jnp.float32), 'value': jax.random.normal(ks[2], (B, L, D_MODEL), jnp.float32), 'key_padding_mask': jnp.zeros((B, L), dtype=bool), 'Wq': jax.random.normal(ks[3], (D_MODEL, D_MODEL), jnp.float32) * s, 'bq': jnp.zeros((D_MODEL,), jnp.float32), 'Wk': jax.random.normal(ks[4], (D_MODEL, D_MODEL), jnp.float32) * s, 'bk': jnp.zeros((D_MODEL,), jnp.float32), 'Wv': jax.random.normal(ks[5], (D_MODEL, D_MODEL), jnp.float32) * s, 'bv': jnp.zeros((D_MODEL,), jnp.float32), 'Wo': jax.random.normal(ks[6], (D_MODEL, D_MODEL), jnp.float32) * s, 'bo': jnp.zeros((D_MODEL,), jnp.float32), 'rel_bias': jax.random.normal(ks[7], (NUM_HEADS, 2 * MAX_REL - 1), jnp.float32) * 0.1}
        return inp
    _L0_xattn_all = _L0_xattn_setup()
    _L0_xattn_in = {k: v for k, v in _L0_xattn_all.items() if k in ('Wq', 'bq', 'Wk', 'bk', 'Wv', 'bv', 'Wo', 'bo', 'rel_bias')}
    del _L0_xattn_all

    def _L0_ffn_setup():
        import jax, jax.numpy as jnp
        import numpy as np
        B, T, C = (2, 1024, 512)
        H, D = (16, 64)
        CR = 8
        R = C // CR
        ROPE = D // 2
        NOPE = D - ROPE
        E, K, I, S = (8, 2, 256, 1)
        THETA = 100000.0
        EPS = 1e-05

        def _rmsnorm(x, w):
            rms = jnp.sqrt(jnp.mean(x * x, axis=-1, keepdims=True) + EPS)
            return w * (x / rms)

        def _rope(xh):
            d = xh.shape[-1]
            t = jnp.arange(xh.shape[2], dtype=jnp.float32)
            freqs = 1.0 / THETA ** (jnp.arange(0, d, 2, dtype=jnp.float32) / d)
            ang = jnp.outer(t, freqs)
            cos, sin = (jnp.cos(ang), jnp.sin(ang))
            xr = xh.reshape(xh.shape[:-1] + (d // 2, 2))
            x0, x1 = (xr[..., 0], xr[..., 1])
            rot = jnp.stack([x0 * cos - x1 * sin, x0 * sin + x1 * cos], axis=-1)
            return rot.reshape(xh.shape)

        def _attention(x, Wq, Wkva, Wkvb, Wo):
            b, t, _ = x.shape
            q = (x @ Wq).reshape(b, t, H, D).transpose(0, 2, 1, 3)
            ckv = x @ Wkva
            kv_latent, k_rope = (ckv[:, :, :R], ckv[:, :, R:])
            kv = (kv_latent @ Wkvb).reshape(b, t, H, NOPE).transpose(0, 2, 1, 3)
            k_rope = jnp.broadcast_to(k_rope[:, None, :, :], (b, H, t, ROPE))
            q_nope, q_rope = (q[..., :NOPE], q[..., NOPE:])
            q = jnp.concatenate([q_nope, _rope(q_rope)], axis=-1)
            k = jnp.concatenate([kv, _rope(k_rope)], axis=-1)
            v = jnp.concatenate([kv, jnp.zeros_like(k_rope)], axis=-1)
            att = jnp.einsum('bhqd,bhkd->bhqk', q, k) / jnp.sqrt(jnp.float32(D))
            mask = jnp.tril(jnp.ones((t, t), dtype=bool))
            att = jnp.where(mask, att, jnp.float32(-jnp.inf))
            att = jax.nn.softmax(att, axis=-1)
            y = jnp.einsum('bhqk,bhkd->bhqd', att, v)
            y = y.transpose(0, 2, 1, 3).reshape(b, t, H * D)
            return y @ Wo

        def _experts(x_flat, Wg, Wu, Wd):
            g = jax.nn.silu(jnp.einsum('nc,eci->nei', x_flat, Wg))
            u = jnp.einsum('nc,eci->nei', x_flat, Wu)
            return jnp.einsum('nei,eic->nec', g * u, Wd)

        def _moe(x, Wgate, expert_bias, Wg, Wu, Wd, sWg, sWu, sWd):
            b, t, c = x.shape
            xf = x.reshape(-1, c)
            shared = jnp.mean(_experts(xf, sWg, sWu, sWd), axis=1)
            logits = xf @ Wgate + expert_bias
            probs = jax.nn.softmax(logits, axis=-1)
            topk_p, topk_i = jax.lax.top_k(probs, K)
            topk_p = topk_p / jnp.sum(topk_p, axis=-1, keepdims=True)
            comb = jnp.sum(jax.nn.one_hot(topk_i, E, dtype=xf.dtype) * topk_p[..., None], axis=1)
            routed = jnp.einsum('ne,nec->nc', comb, _experts(xf, Wg, Wu, Wd))
            return (shared + routed).reshape(b, t, c)
        key = jax.random.key(seed)
        ks = jax.random.split(key, 16)
        w = lambda k, shp: jax.random.normal(k, shp, dtype=jnp.float32) * 0.02
        return {'x': jax.random.normal(ks[0], (B, T, C), dtype=jnp.float32), 'w_ln1': jnp.ones((C,), jnp.float32), 'Wq': w(ks[1], (C, H * D)), 'Wkva': w(ks[2], (C, R + ROPE)), 'Wkvb': w(ks[3], (R, H * NOPE)), 'Wo': w(ks[4], (H * D, C)), 'w_ln2': jnp.ones((C,), jnp.float32), 'Wgate': w(ks[5], (C, E)), 'expert_bias': jnp.zeros((E,), jnp.float32), 'Wg': w(ks[6], (E, C, I)), 'Wu': w(ks[7], (E, C, I)), 'Wd': w(ks[8], (E, I, C)), 'sWg': w(ks[9], (S, C, I)), 'sWu': w(ks[10], (S, C, I)), 'sWd': w(ks[11], (S, I, C))}
    _L0_ffn_all = _L0_ffn_setup()
    _L0_ffn_in = {k: v for k, v in _L0_ffn_all.items() if k in ('w_ln1', 'Wq', 'Wkva', 'Wkvb', 'Wo', 'w_ln2', 'Wgate', 'expert_bias', 'Wg', 'Wu', 'Wd', 'sWg', 'sWu', 'sWd')}
    del _L0_ffn_all
    return {'x': x, 'ctx_1024': ctx_1024, 'mask_BxS2_bf0': mask_BxS2_bf0, 'g_xattn': g_xattn, 'g_ffn': g_ffn, 'L0_xattn_Wq': _L0_xattn_in['Wq'], 'L0_xattn_bq': _L0_xattn_in['bq'], 'L0_xattn_Wk': _L0_xattn_in['Wk'], 'L0_xattn_bk': _L0_xattn_in['bk'], 'L0_xattn_Wv': _L0_xattn_in['Wv'], 'L0_xattn_bv': _L0_xattn_in['bv'], 'L0_xattn_Wo': _L0_xattn_in['Wo'], 'L0_xattn_bo': _L0_xattn_in['bo'], 'L0_xattn_rel_bias': _L0_xattn_in['rel_bias'], 'L0_ffn_w_ln1': _L0_ffn_in['w_ln1'], 'L0_ffn_Wq': _L0_ffn_in['Wq'], 'L0_ffn_Wkva': _L0_ffn_in['Wkva'], 'L0_ffn_Wkvb': _L0_ffn_in['Wkvb'], 'L0_ffn_Wo': _L0_ffn_in['Wo'], 'L0_ffn_w_ln2': _L0_ffn_in['w_ln2'], 'L0_ffn_Wgate': _L0_ffn_in['Wgate'], 'L0_ffn_expert_bias': _L0_ffn_in['expert_bias'], 'L0_ffn_Wg': _L0_ffn_in['Wg'], 'L0_ffn_Wu': _L0_ffn_in['Wu'], 'L0_ffn_Wd': _L0_ffn_in['Wd'], 'L0_ffn_sWg': _L0_ffn_in['sWg'], 'L0_ffn_sWu': _L0_ffn_in['sWu'], 'L0_ffn_sWd': _L0_ffn_in['sWd']}

def reference(x, ctx_1024, mask_BxS2_bf0, g_xattn, g_ffn, L0_xattn_Wq, L0_xattn_bq, L0_xattn_Wk, L0_xattn_bk, L0_xattn_Wv, L0_xattn_bv, L0_xattn_Wo, L0_xattn_bo, L0_xattn_rel_bias, L0_ffn_w_ln1, L0_ffn_Wq, L0_ffn_Wkva, L0_ffn_Wkvb, L0_ffn_Wo, L0_ffn_w_ln2, L0_ffn_Wgate, L0_ffn_expert_bias, L0_ffn_Wg, L0_ffn_Wu, L0_ffn_Wd, L0_ffn_sWg, L0_ffn_sWu, L0_ffn_sWd):
    import jax
    import jax.numpy as jnp

    def _L0_xattn_ref(query, key, value, key_padding_mask, Wq, bq, Wk, bk, Wv, bv, Wo, bo, rel_bias):
        import jax, jax.numpy as jnp
        import numpy as np
        import math
        D_MODEL = 512
        NUM_HEADS = 16
        D_K = D_MODEL // NUM_HEADS
        MAX_REL = 64
        B, L = (2, 1024)
        Bsz, S, _ = query.shape
        Q = (query @ Wq + bq).reshape(Bsz, S, NUM_HEADS, D_K)
        K = (key @ Wk + bk).reshape(Bsz, S, NUM_HEADS, D_K)
        V = (value @ Wv + bv).reshape(Bsz, S, NUM_HEADS, D_K)
        scores = jnp.einsum('bqhd,bkhd->bhqk', Q, K) / math.sqrt(D_K)
        r = jnp.arange(S)
        rel_pos = jnp.clip(r[:, None] - r[None, :], -MAX_REL + 1, MAX_REL - 1) + MAX_REL - 1
        bias = rel_bias[:, rel_pos]
        scores = scores + bias[None]
        scores = jnp.where(key_padding_mask[:, None, None, :], -jnp.inf, scores)
        attn = jax.nn.softmax(scores, axis=-1)
        out = jnp.einsum('bhqk,bkhd->bqhd', attn, V).reshape(Bsz, S, D_MODEL)
        return out @ Wo + bo

    def _L0_ffn_ref(x, w_ln1, Wq, Wkva, Wkvb, Wo, w_ln2, Wgate, expert_bias, Wg, Wu, Wd, sWg, sWu, sWd):
        import jax, jax.numpy as jnp
        import numpy as np
        B, T, C = (2, 1024, 512)
        H, D = (16, 64)
        CR = 8
        R = C // CR
        ROPE = D // 2
        NOPE = D - ROPE
        E, K, I, S = (8, 2, 256, 1)
        THETA = 100000.0
        EPS = 1e-05

        def _rmsnorm(x, w):
            rms = jnp.sqrt(jnp.mean(x * x, axis=-1, keepdims=True) + EPS)
            return w * (x / rms)

        def _rope(xh):
            d = xh.shape[-1]
            t = jnp.arange(xh.shape[2], dtype=jnp.float32)
            freqs = 1.0 / THETA ** (jnp.arange(0, d, 2, dtype=jnp.float32) / d)
            ang = jnp.outer(t, freqs)
            cos, sin = (jnp.cos(ang), jnp.sin(ang))
            xr = xh.reshape(xh.shape[:-1] + (d // 2, 2))
            x0, x1 = (xr[..., 0], xr[..., 1])
            rot = jnp.stack([x0 * cos - x1 * sin, x0 * sin + x1 * cos], axis=-1)
            return rot.reshape(xh.shape)

        def _attention(x, Wq, Wkva, Wkvb, Wo):
            b, t, _ = x.shape
            q = (x @ Wq).reshape(b, t, H, D).transpose(0, 2, 1, 3)
            ckv = x @ Wkva
            kv_latent, k_rope = (ckv[:, :, :R], ckv[:, :, R:])
            kv = (kv_latent @ Wkvb).reshape(b, t, H, NOPE).transpose(0, 2, 1, 3)
            k_rope = jnp.broadcast_to(k_rope[:, None, :, :], (b, H, t, ROPE))
            q_nope, q_rope = (q[..., :NOPE], q[..., NOPE:])
            q = jnp.concatenate([q_nope, _rope(q_rope)], axis=-1)
            k = jnp.concatenate([kv, _rope(k_rope)], axis=-1)
            v = jnp.concatenate([kv, jnp.zeros_like(k_rope)], axis=-1)
            att = jnp.einsum('bhqd,bhkd->bhqk', q, k) / jnp.sqrt(jnp.float32(D))
            mask = jnp.tril(jnp.ones((t, t), dtype=bool))
            att = jnp.where(mask, att, jnp.float32(-jnp.inf))
            att = jax.nn.softmax(att, axis=-1)
            y = jnp.einsum('bhqk,bhkd->bhqd', att, v)
            y = y.transpose(0, 2, 1, 3).reshape(b, t, H * D)
            return y @ Wo

        def _experts(x_flat, Wg, Wu, Wd):
            g = jax.nn.silu(jnp.einsum('nc,eci->nei', x_flat, Wg))
            u = jnp.einsum('nc,eci->nei', x_flat, Wu)
            return jnp.einsum('nei,eic->nec', g * u, Wd)

        def _moe(x, Wgate, expert_bias, Wg, Wu, Wd, sWg, sWu, sWd):
            b, t, c = x.shape
            xf = x.reshape(-1, c)
            shared = jnp.mean(_experts(xf, sWg, sWu, sWd), axis=1)
            logits = xf @ Wgate + expert_bias
            probs = jax.nn.softmax(logits, axis=-1)
            topk_p, topk_i = jax.lax.top_k(probs, K)
            topk_p = topk_p / jnp.sum(topk_p, axis=-1, keepdims=True)
            comb = jnp.sum(jax.nn.one_hot(topk_i, E, dtype=xf.dtype) * topk_p[..., None], axis=1)
            routed = jnp.einsum('ne,nec->nc', comb, _experts(xf, Wg, Wu, Wd))
            return (shared + routed).reshape(b, t, c)
        x = x + _attention(_rmsnorm(x, w_ln1), Wq, Wkva, Wkvb, Wo)
        residual = x
        xn = _rmsnorm(x, w_ln2)
        x_out = _moe(xn, Wgate, expert_bias, Wg, Wu, Wd, sWg, sWu, sWd)
        return residual + x_out
    x = x + jnp.tanh(g_xattn[0]) * _L0_xattn_ref(_layernorm(x, axis=-1), ctx_1024, ctx_1024, mask_BxS2_bf0, L0_xattn_Wq, L0_xattn_bq, L0_xattn_Wk, L0_xattn_bk, L0_xattn_Wv, L0_xattn_bv, L0_xattn_Wo, L0_xattn_bo, L0_xattn_rel_bias)
    x = x + jnp.tanh(g_ffn[0]) * _L0_ffn_ref(_layernorm(x, axis=-1), L0_ffn_w_ln1, L0_ffn_Wq, L0_ffn_Wkva, L0_ffn_Wkvb, L0_ffn_Wo, L0_ffn_w_ln2, L0_ffn_Wgate, L0_ffn_expert_bias, L0_ffn_Wg, L0_ffn_Wu, L0_ffn_Wd, L0_ffn_sWg, L0_ffn_sWu, L0_ffn_sWd)
    return x

_drawn_inputs = setup_inputs


def setup_inputs(seed=0):
    import zlib

    import numpy as np

    out = dict(_drawn_inputs(seed))
    spreads = {'L0_xattn_bq': (0.0, 0.321),
     'L0_xattn_bk': (0.0, 0.8),
     'L0_xattn_bv': (0.0, 0.1),
     'L0_xattn_bo': (0.0, 0.1),
     'L0_ffn_w_ln1': (1.0, 0.6),
     'L0_ffn_w_ln2': (1.0, 0.2),
     'L0_ffn_expert_bias': (0.0, 0.1)}
    factors = {'L0_xattn_rel_bias': 7.663, 'L0_ffn_Wq': 8.0}
    for name, (base, spread) in spreads.items():
        noise = np.random.default_rng([zlib.crc32(name.encode()), seed]).standard_normal(out[name].shape)
        drawn = base * np.exp(spread * noise) if base else spread * noise
        out[name] = jnp.asarray(drawn.astype(out[name].dtype))
    for name, factor in factors.items():
        out[name] = (out[name] * factor).astype(out[name].dtype)
    return out
```

```python
from contextlib import ExitStack

import numpy as np

import concourse.bass as bass
from concourse import mybir

F32 = mybir.dt.float32
F16 = mybir.dt.float16
U8 = mybir.dt.uint8
I32 = mybir.dt.int32
ALU = mybir.AluOpType
ACT = mybir.ActivationFunctionType
AX_X = mybir.AxisListType.X

P = 128
B = 8
S = 512
D = 512
NT = S // P
NK = D // P
H = 16
DH = 32
HG = P // DH
NG = H // HG
UNITS = H * NT
R = 64
E = 8
I = 256
NI = I // P
EPS = 1e-5
WS = 256.0
HS = 128.0
MASKED = -60000.0
STRIP = S + (NT - 1) * P


def unit_of(n):
    g, r = divmod(n, NT * HG)
    i, hh = divmod(r, HG)
    return g, i, hh


def pass_a(nc, x, ctxt, maskb, g_gate, wq, bq, wk, bk, wv, bv, wo, bo, strips, ident, x1, mask_rows):
    with ExitStack() as ctx:
        def sb(name, shape, dt=F32):
            return ctx.enter_context(nc.sbuf_tensor("a_" + name, shape, dt))

        def sem(name):
            return ctx.enter_context(nc.semaphore("a_" + name))

        bank = [ctx.enter_context(nc.psum_tensor(f"a_bank{i}", [P, 512], F32)) for i in range(8)]
        PROJ = 4
        score_bank = [bank[0], bank[1], bank[2]]
        turn_bank = [bank[3], bank[4], bank[5]]
        out_bank, recip_bank = bank[6], bank[7]

        w_hi = sb("w_hi", [P, 4, NK, D], F16)
        w_lo = sb("w_lo", [P, 4, NK, D], F16)
        bias = sb("bias", [DH + 1, 4, D], F16)
        ones = sb("ones", [DH + 1, P], F16)
        b_hi, b_lo = bias[0:1], bias[DH:DH + 1]
        strip = sb("strip", [P, H, STRIP])
        idn = sb("idn", [P, P])
        q_stack = sb("q_stack", [3 * DH + 1, H, S], F16)
        k_stack = sb("k_stack", [3 * DH + 1, H, S], F16)
        xn = sb("xn", [P, NT, D])
        cn = sb("cn", [P, NT, D])
        xr = sb("xr", [P, NT, D])
        ct_hi = sb("ct_hi", [P, NK, S], F16)
        ct_lo = sb("ct_lo", [P, NK, S], F16)
        xt_hi = sb("xt_hi", [P, NK, S], F16)
        xt_lo = sb("xt_lo", [P, NK, S], F16)
        qk_hi = sb("qk_hi", [P, 4, S], F16)
        qk_lo = sb("qk_lo", [P, 4, S], F16)
        v = sb("v", [P, NT, D])
        prob = sb("prob", [P, 4, S])
        turned = sb("turned", [P, 2, HG, NT, P])
        stage = turned[:].rearrange("p s h j q -> p s (h j q)")
        recip_sb = sb("recip_sb", [P, S])
        stats = sb("stats", [P, NT, 6])
        mv = sb("mv", [P, NT, 2])
        rstd = sb("rstd", [P, 2, NT])
        power = sb("power", [P, NT])
        low = sb("low", [P, 8])
        den = sb("den", [P, 2, NT * HG])
        rden = sb("rden", [P, 2, NT * HG])
        gate = sb("gate", [P, 2])
        bstage = strip[0:DH + 1, 0:4, 0:D]
        mask_words = recip_sb[:, 0:P].bitcast(I32)
        mask8 = recip_sb[:, 0:P].bitcast(U8)
        mask_stage = ct_hi[:, 0, :]

        w_loaded = [sem(f"w_loaded{i}") for i in range(2)]
        w_free, w_split = sem("w_free"), sem("w_split")
        b_loaded, b_zeroed, b_split = sem("b_loaded"), sem("b_zeroed"), sem("b_split")
        const_loaded, const_set, strips_loaded = sem("const_loaded"), sem("const_set"), sem("strips_loaded")
        gate_ready = sem("gate_ready")
        mask_set, mask_stored, mask_loaded = sem("mask_set"), sem("mask_stored"), sem("mask_loaded")
        x_loaded, c_loaded, xr_loaded = sem("x_loaded"), sem("c_loaded"), sem("xr_loaded")
        stats_done, mv_done, rstd_done, pow_done, xn_ready = (sem("stats_done"), sem("mv_done"), sem("rstd_done"),
                                                              sem("pow_done"), sem("xn_ready"))
        job_done, hi_done, lo_done, sum_done = sem("job_done"), sem("hi_done"), sem("lo_done"), sem("sum_done")
        stacked = [sem(f"stacked{g}") for g in range(NG)]
        x1_stored = sem("x1_stored")
        scored, biased, exped, turned_done = sem("scored"), sem("biased"), sem("exped"), sem("turned_done")
        kept_act, kept_dve = sem("kept_act"), sem("kept_dve")
        summed, recip_done, spread, recip_kept, normed = (sem("summed"), sem("recip_done"), sem("spread"),
                                                          sem("recip_kept"), sem("normed"))
        o_hi_done, o_lo_done = sem("o_hi_done"), sem("o_lo_done")

        STK = 16 * 2 * 3 * HG
        J_CT, J_XT, J_QK, J_V, J_O = 0, NK, 2 * NK, 2 * NK + 2 * NG, 2 * NK + 2 * NG + NT
        JOBS = J_O + NT
        HI, LO = J_O, J_V
        q_scale = 1.0 / (WS * DH ** 0.5)
        normal = recip_sb

        block = ctx.enter_context(nc.Block())

        @block.sync
        def _(sp):
            for n, w in enumerate((bq, bk, bv, bo)):
                for row in (0, DH):
                    sp.dma_start(bstage[row:row + 1, n, :], w.rearrange("(a n) -> a n", a=1)).then_inc(b_loaded, 16)
            sp.dma_start(idn[:], ident).then_inc(const_loaded, 16)
            sp.dma_start(gate[:, 0:1], g_gate.rearrange("(a n) -> a n", a=1).broadcast_to([P, 1])).then_inc(const_loaded, 16)
            for b in range(B):
                sp.dma_start(mask_words[b * H:(b + 1) * H, :], maskb[b:b + 1, :].broadcast_to([H, S // 4])).then_inc(const_loaded, 16)
            for n, w in enumerate((wq, wk, wv, wo)):
                if n >= 2:
                    sp.wait_ge(w_split, n - 1)
                sp.dma_start(stage[:, n % 2, :].rearrange("p (k n) -> p k n", k=NK),
                             w.rearrange("(k p) n -> p k n", p=P)).then_inc(w_loaded[n % 2], 16)
            sp.wait_ge(mask_set, 1)
            sp.dma_start(mask_rows, mask_stage).then_inc(mask_stored, 16)
            sp.wait_ge(mask_stored, 16)
            sp.wait_ge(b_split, 3)
            sp.dma_start(strip[:], strips).then_inc(strips_loaded, 16)
            with sp.Fori(0, B) as b:
                sp.wait_ge(job_done, b * JOBS + NK)
                sp.dma_start(cn[:], ctxt[bass.ds(b * 1, 1), :, :].rearrange("a (t p) n -> p (a t) n", p=P)).then_inc(c_loaded, 16)
                sp.wait_ge(job_done, b * JOBS + 2 * NK)
                sp.dma_start(xn[:], x[bass.ds(b * 1, 1), :, :].rearrange("a (t p) n -> p (a t) n", p=P)).then_inc(x_loaded, 16)
                sp.wait_ge(scored, b * UNITS + UNITS)
                sp.dma_start(k_stack[3 * DH:3 * DH + 1, :, :],
                             mask_rows.rearrange("(b h) n -> b h n", h=H)[bass.ds(b * 1, 1), :, :]).then_inc(mask_loaded, 16)
                sp.wait_ge(x1_stored, b * 16 * NT + 16 * NT)
                sp.dma_start(xr[:], x[bass.ds(b * 1, 1), :, :].rearrange("a (t p) n -> p (a t) n", p=P)).then_inc(xr_loaded, 16)
                for g in range(NG):
                    for part, stack in enumerate((q_stack, k_stack)):
                        slot = 2 * (g % 2) + part
                        job = J_QK + 2 * g + part
                        sp.wait_ge(lo_done, b * LO + job + 1)
                        for row, src in enumerate((qk_hi, qk_lo, qk_hi) if part == 0 else (qk_hi, qk_hi, qk_lo)):
                            for hh in range(HG):
                                sp.dma_start(stack[row * DH:(row + 1) * DH, g * HG + hh, :],
                                             src[hh * DH:(hh + 1) * DH, slot, :]).then_inc(stacked[g], 16)
                for t in range(NT):
                    sp.wait_ge(sum_done, b * NT + NT + t + 1)
                    sp.dma_start(x1[bass.ds(b * 1, 1), t * P:(t + 1) * P, :].rearrange("a p n -> p (a n)"),
                                 xr[:, t, :]).then_inc(x1_stored, 16)
            sp.wait_ge(x1_stored, 16 * NT * (B + 1))

        @block.gpsimd
        def _(pool):
            pool.sem_inc(job_done, JOBS)
            pool.sem_inc(scored, UNITS)
            pool.sem_inc(x1_stored, 16 * NT)
            nc.gpsimd.memset(power[:], -0.5).then_inc(const_set, 1)
            pool.wait_ge(const_loaded, 16 * (2 + B))
            nc.gpsimd.tensor_scalar(mask_stage, mask8, MASKED, None, ALU.mult).then_inc(mask_set, 1)
            pool.wait_ge(const_set, 3)
            with pool.Fori(0, B) as b:
                pool.wait_ge(mv_done, b * NT + NT)
                pool.nop(nofuse=True)
                nc.gpsimd.tensor_scalar(rstd[:, 0, :], mv[:, :, 1], EPS, None, ALU.add).then_inc(pow_done, 1)
                pool.wait_ge(pow_done, b * 1 + 1)
                nc.gpsimd.tensor_tensor(rstd[:, 1, :], rstd[:, 0, :], power[:], ALU.pow).then_inc(rstd_done, 1)
                for g in range(NG):
                    pool.wait_ge(o_hi_done, b * NG + g + 1)
                    nc.gpsimd.tensor_tensor(xt_lo[:, g, :], normal[:], xt_hi[:, g, :], ALU.subtract).then_inc(o_lo_done, 1)

        @block.scalar
        def _(act):
            act.wait_ge(const_loaded, 16 * (2 + B))
            nc.scalar.activation(gate[:, 1:2], gate[:, 0:1], ACT.Tanh).then_inc(gate_ready, 1)
            act.wait_ge(b_loaded, 128)
            act.wait_ge(b_zeroed, 1)
            nc.scalar.activation(b_hi, bstage[0:1], ACT.Copy, scale=WS).then_inc(b_split, 1)
            nc.scalar.activation(b_lo, bstage[DH:DH + 1], ACT.Copy, scale=WS).then_inc(b_split, 1)
            for n in range(4):
                act.wait_ge(w_loaded[n % 2], 16 * (n // 2 + 1))
                nc.scalar.activation(w_hi[:, n, :, :].rearrange("p k n -> p (k n)"), stage[:, n % 2, :], ACT.Copy,
                                     scale=WS).then_inc(w_free, 1)
            with act.Fori(0, B) as b:
                def high(job, out, scale=1.0):
                    act.wait_ge(job_done, b * JOBS + JOBS + job + 1)
                    nc.scalar.activation(out, bank[job % PROJ][:], ACT.Copy, scale=scale).then_inc(hi_done, 1)

                act.wait_ge(mask_stored, 16)
                for k in range(NK):
                    high(J_CT + k, ct_hi[:, k, :])
                for k in range(NK):
                    high(J_XT + k, xt_hi[:, k, :])
                for g in range(NG):
                    if g >= 2:
                        act.wait_ge(stacked[g - 2], b * STK + STK)
                    high(J_QK + 2 * g, qk_hi[:, 2 * (g % 2), :], q_scale)
                    high(J_QK + 2 * g + 1, qk_hi[:, 2 * (g % 2) + 1, :], 1.0 / WS)
                for t in range(NT):
                    high(J_V + t, v[:, t, :], 1.0 / WS)

                def keep(n):
                    act.wait_ge(turned_done, b * UNITS + n + 1)
                    nc.scalar.activation(turned[:, n // HG % 2, n % HG, :, :],
                                         turn_bank[n % 3][:].rearrange("p (j q) -> p j q", q=P), ACT.Copy).then_inc(kept_act, 1)

                for step in range(UNITS + 9):
                    if step < UNITS:
                        g, i, hh = unit_of(step)
                        act.wait_ge(biased, b * UNITS + step + 1)
                        nc.scalar.activation(prob[:, step % 4, :], prob[:, step % 4, :], ACT.Exp, scale=-1.0,
                                             bias=low[:, step % 8:step % 8 + 1],
                                             accum_out=den[:, g % 2, i * HG + hh:i * HG + hh + 1]).then_inc(exped, 1)
                    n = step - 2
                    if 0 <= n < UNITS and n % 2 == 0:
                        if n >= 2 * HG:
                            act.wait_ge(summed, b * (UNITS // HG) + n // HG - 1)
                        keep(n)
                    g, r = divmod(step - 9, NT * HG)
                    if r == NT * HG - 1 and g >= 0:
                        act.wait_ge(spread, b * NG + g + 1)
                        if g:
                            act.wait_ge(o_lo_done, b * NG + g)
                        nc.scalar.activation(recip_sb[:], recip_bank[:], ACT.Copy).then_inc(recip_kept, 1)
                        act.wait_ge(normed, b * NG + g + 1)
                        nc.scalar.activation(xt_hi[:, g, :], normal[:], ACT.Copy).then_inc(o_hi_done, 1)

        @block.vector
        def _(dve):
            dve.sem_inc(sum_done, NT)
            nc.vector.memset(bias[:], 0.0).then_inc(b_zeroed, 1)
            nc.vector.memset(ones[:], 1.0).then_inc(const_set, 1)
            nc.vector.memset(q_stack[3 * DH:3 * DH + 1, :, :], 1.0).then_inc(const_set, 1)
            dve.wait_ge(gate_ready, 1)
            nc.vector.tensor_scalar(gate[:, 0:1], gate[:, 1:2], 1.0 / WS, None, ALU.mult).then_inc(gate_ready, 1)
            dve.wait_ge(b_split, 2)
            nc.vector.scalar_tensor_tensor(out=b_lo, in0=bstage[DH:DH + 1], scalar=WS, in1=b_lo, op0=ALU.mult,
                                           op1=ALU.subtract).then_inc(b_split, 1)
            for n in range(4):
                dve.wait_ge(w_free, n + 1)
                nc.vector.scalar_tensor_tensor(out=w_lo[:, n, :, :].rearrange("p k n -> p (k n)"), in0=stage[:, n % 2, :],
                                               scalar=WS, in1=w_hi[:, n, :, :].rearrange("p k n -> p (k n)"),
                                               op0=ALU.mult, op1=ALU.subtract).then_inc(w_split, 1)
            dve.wait_ge(gate_ready, 2)
            dve.wait_ge(strips_loaded, 16)
            with dve.Fori(0, B) as b:
                def lower(job, out, hi, scale=1.0):
                    dve.wait_ge(hi_done, b * HI + job + 1)
                    nc.vector.scalar_tensor_tensor(out=out, in0=bank[job % PROJ][:], scalar=scale, in1=hi, op0=ALU.mult,
                                                   op1=ALU.subtract).then_inc(lo_done, 1)

                dve.wait_ge(x_loaded, b * 16 + 16)
                for t in range(NT):
                    nc.vector.bn_stats(stats[:, t, :], xn[:, t, :]).then_inc(stats_done, 1)
                for t in range(NT):
                    dve.wait_ge(stats_done, b * NT + t + 1)
                    dve.nop(nofuse=True)
                    nc.vector.bn_aggr(mv[:, t, :], stats[:, t, :]).then_inc(mv_done, 1)
                for k in range(NK):
                    lower(J_CT + k, ct_lo[:, k, :], ct_hi[:, k, :])
                dve.wait_ge(mv_done, b * NT + NT)
                dve.wait_ge(rstd_done, b * 1 + 1)
                for t in range(NT):
                    nc.vector.tensor_scalar(xn[:, t, :], xn[:, t, :], mv[:, t, 0:1], rstd[:, 1, t:t + 1], ALU.subtract,
                                            ALU.mult).then_inc(xn_ready, 1)
                for k in range(NK):
                    lower(J_XT + k, xt_lo[:, k, :], xt_hi[:, k, :])
                for g in range(NG):
                    lower(J_QK + 2 * g, qk_lo[:, 2 * (g % 2), :], qk_hi[:, 2 * (g % 2), :], q_scale)
                    lower(J_QK + 2 * g + 1, qk_lo[:, 2 * (g % 2) + 1, :], qk_hi[:, 2 * (g % 2) + 1, :], 1.0 / WS)

                for step in range(UNITS + 9):
                    if step < UNITS:
                        g, i, hh = unit_of(step)
                        dve.wait_ge(scored, b * UNITS + UNITS + step + 1)
                        if step >= 4:
                            dve.wait_ge(turned_done, b * UNITS + step - 3)
                        at = (NT - 1 - i) * P
                        dve.nop(nofuse=True)
                        nc.vector.tensor_tensor_reduce(out=prob[:, step % 4, :], in0=score_bank[step % 3][:],
                                                       in1=strip[:, g * HG + hh, at:at + S], scale=-1.0, scalar=3e38,
                                                       op0=ALU.add, op1=ALU.min,
                                                       accum_out=low[:, step % 8:step % 8 + 1]).then_inc(biased, 1)
                    n = step - 2
                    if 0 <= n < UNITS and n % 2 == 1:
                        if n >= 2 * HG:
                            dve.wait_ge(summed, b * (UNITS // HG) + n // HG - 1)
                        dve.wait_ge(turned_done, b * UNITS + n + 1)
                        nc.vector.tensor_copy(turned[:, n // HG % 2, n % HG, :, :],
                                              turn_bank[n % 3][:].rearrange("p (j q) -> p j q", q=P)).then_inc(kept_dve, 1)
                    g, r = divmod(step - 4, NT * HG)
                    if r == NT * HG - 1 and g >= 0:
                        dve.wait_ge(exped, b * UNITS + (g + 1) * NT * HG)
                        nc.vector.reciprocal(rden[:, g % 2, :], den[:, g % 2, :]).then_inc(recip_done, 1)
                    g, r = divmod(step - 9, NT * HG)
                    if r == NT * HG - 1 and g >= 0:
                        dve.wait_ge(summed, b * (UNITS // HG) + (g + 1) * NT)
                        dve.wait_ge(recip_kept, b * NG + g + 1)
                        nc.vector.tensor_tensor(normal[:], out_bank[:], recip_sb[:], ALU.mult).then_inc(normed, 1)
                dve.wait_ge(xr_loaded, b * 16 + 16)
                for t in range(NT):
                    dve.wait_ge(job_done, b * JOBS + JOBS + J_O + t + 1)
                    nc.vector.scalar_tensor_tensor(out=xr[:, t, :], in0=bank[(J_O + t) % PROJ][:], scalar=gate[:, 0:1],
                                                   in1=xr[:, t, :], op0=ALU.mult, op1=ALU.add).then_inc(sum_done, 1)

        @block.tensor
        def _(pe):
            mm = nc.tensor.matmul
            pe.wait_ge(const_loaded, 16 * (2 + B))
            pe.wait_ge(const_set, 3)
            pe.wait_ge(b_split, 3)
            with pe.Fori(0, B) as b:
                def transpose(job, src, k):
                    for t in range(NT):
                        last = nc.tensor.transpose(bank[job % PROJ][:, t * P:(t + 1) * P], src[:, t, k * P:(k + 1) * P], idn[:])
                    last.then_inc(job_done, 1)

                def product(job, pairs, both):
                    for n, ((lh, ll), (rh, rl)) in enumerate(pairs):
                        mm(bank[job % PROJ][:], lh, rh, start=(n == 0), stop=False)
                        mm(bank[job % PROJ][:], lh, rl, start=False, stop=False)
                        mm(bank[job % PROJ][:], ll, rh, start=False, stop=False)
                    mm(bank[job % PROJ][:], *both, start=False, stop=True).then_inc(job_done, 1)

                def cols(m, n, k, j):
                    return (m[:, n, k, j * P:(j + 1) * P])

                pe.wait_ge(c_loaded, b * 16 + 16)
                for k in range(NK):
                    pe.wait_ge(sum_done, b * NT + k + 1)
                    transpose(J_CT + k, cn, k)
                pe.wait_ge(xn_ready, b * NT + NT)
                for k in range(NK):
                    pe.wait_ge(lo_done, b * LO + J_CT + k + 1)
                    transpose(J_XT + k, xn, k)
                pe.wait_ge(w_split, 4)
                for g in range(NG):
                    for part, (h, l) in enumerate(((xt_hi, xt_lo), (ct_hi, ct_lo))):
                        job = J_QK + 2 * g + part
                        pe.wait_ge(lo_done, b * LO + (J_QK if g < 2 else job - PROJ + 1))
                        product(job, [((cols(w_hi, part, k, g), cols(w_lo, part, k, g)), (h[:, k, :], l[:, k, :]))
                                      for k in range(NK)],
                                (bias[:, part, g * P:(g + 1) * P], ones[:].unsqueeze(1).broadcast_to([DH + 1, NT, P])))
                for t in range(NT):
                    pe.wait_ge(lo_done, b * LO + J_V - PROJ + t + 1)
                    product(J_V + t, [((ct_hi[:, k, t * P:(t + 1) * P], ct_lo[:, k, t * P:(t + 1) * P]),
                                       (w_hi[:, 2, k, :], w_lo[:, 2, k, :])) for k in range(NK)],
                            (ones[:], bias[:, 2, :]))
                pe.wait_ge(hi_done, b * HI + HI)
                pe.wait_ge(mask_loaded, b * 16 + 16)

                for step in range(UNITS + 9):
                    if step < UNITS:
                        g, i, hh = unit_of(step)
                        if step % (NT * HG) == 0:
                            pe.wait_ge(stacked[g], b * STK + STK)
                        if step >= 3:
                            pe.wait_ge(biased, b * UNITS + step - 2)
                        h = g * HG + hh
                        mm(score_bank[step % 3][:], q_stack[:, h, i * P:(i + 1) * P], k_stack[:, h, :], start=True,
                           stop=True).then_inc(scored, 1)
                    n = step - 2
                    if 0 <= n < UNITS:
                        pe.wait_ge(exped, b * UNITS + n + 1)
                        if n >= 3:
                            pe.wait_ge((kept_act, kept_dve)[(n - 3) % 2], b * (UNITS // 2) + (n - 3) // 2 + 1)
                        for j in range(NT):
                            last = nc.tensor.transpose(turn_bank[n % 3][:, j * P:(j + 1) * P],
                                                       prob[:, n % 4, j * P:(j + 1) * P], idn[:])
                        last.then_inc(turned_done, 1)
                    m = step - 5
                    if m >= 0 and m % HG == HG - 1 and m < UNITS:
                        quad = m // HG
                        g, i = divmod(quad, NT)
                        pe.wait_ge(kept_act, b * (UNITS // 2) + (quad + 1) * HG // 2)
                        pe.wait_ge(kept_dve, b * (UNITS // 2) + (quad + 1) * HG // 2)
                        if i == 0 and g > 0:
                            pe.wait_ge(normed, b * NG + g)
                        for j in range(NT):
                            for hh in range(HG):
                                c = (g * HG + hh) * DH
                                last = mm(out_bank[hh * DH:(hh + 1) * DH, i * P:(i + 1) * P], v[:, j, c:c + DH],
                                          turned[:, quad % 2, hh, j, :], start=(j == 0), stop=(j == NT - 1),
                                          tile_position=(0, hh * DH))
                        last.then_inc(summed, 1)
                        if i == NT - 1:
                            pe.wait_ge(recip_done, b * NG + g + 1)
                            for t in range(NT):
                                for hh in range(HG):
                                    c = t * HG + hh
                                    last = mm(recip_bank[hh * DH:(hh + 1) * DH, t * P:(t + 1) * P],
                                              rden[:, g % 2, c:c + 1].broadcast_to([P, DH]), idn[:], start=True,
                                              stop=True, tile_position=(0, hh * DH))
                            last.then_inc(spread, 1)
                pe.wait_ge(o_lo_done, b * NG + NG)
                for t in range(NT):
                    product(J_O + t, [((xt_hi[:, k, t * P:(t + 1) * P], xt_lo[:, k, t * P:(t + 1) * P]),
                                       (w_hi[:, 3, k, :], w_lo[:, 3, k, :])) for k in range(NK)],
                            (ones[:], bias[:, 3, :]))


def pass_b(nc, x1, w_norm, wq, wkva, wkvb, wo, cos_sin, swap, causal, ident, z1):
    with ExitStack() as ctx:
        def sb(name, shape, dt=F32):
            return ctx.enter_context(nc.sbuf_tensor("b_" + name, shape, dt))

        def sem(name):
            return ctx.enter_context(nc.semaphore("b_" + name))

        bank = [ctx.enter_context(nc.psum_tensor(f"b_bank{i}", [P, 512], F32)) for i in range(8)]
        PROJ = 4
        score_bank = [bank[0], bank[1], bank[2]]
        turn_bank = [bank[3], bank[4], bank[5]]
        out_bank, recip_bank = bank[6], bank[7]

        KR = slice(R, R + DH)
        wq_hi = sb("wq_hi", [P, NK, 2 * D], F16)
        wq_lo = sb("wq_lo", [P, NK, 2 * D], F16)
        wa_hi = sb("wa_hi", [P, NK, R + DH], F16)
        wa_lo = sb("wa_lo", [P, NK, R + DH], F16)
        wb_hi = sb("wb_hi", [R, D], F16)
        wb_lo = sb("wb_lo", [R, D], F16)
        wo_hi = sb("wo_hi", [P, NG, D], F16)
        wo_lo = sb("wo_lo", [P, NG, D], F16)
        wn = sb("wn", [P, NK])
        idn = sb("idn", [P, P])
        swp = sb("swp", [P, P], F16)
        rot = sb("rot", [P, 4, S])
        tri = sb("tri", [P, STRIP])
        q_stack = sb("q_stack", [P, H, S], F16)
        k_stack = sb("k_stack", [P, H, S], F16)
        k_stack2 = sb("k_stack2", [2 * DH, H, S], F16)
        z = sb("z", [P, NT, D])
        hn = sb("hn", [P, NT, D])
        ht_hi = sb("ht_hi", [P, NK, S], F16)
        ht_lo = sb("ht_lo", [P, NK, S], F16)
        lat_hi = sb("lat_hi", [R + DH, S], F16)
        lat_lo = sb("lat_lo", [R + DH, S], F16)
        kr_hi = sb("kr_hi", [R + DH, S], F16)
        kr_lo = sb("kr_lo", [R + DH, S], F16)
        kn_hi = sb("kn_hi", [P, 2, S], F16)
        kn_lo = sb("kn_lo", [P, 2, S], F16)
        qn_hi = sb("qn_hi", [P, 2, S], F16)
        qn_lo = sb("qn_lo", [P, 2, S], F16)
        qu_hi = sb("qu_hi", [P, 2, S], F16)
        qu_lo = sb("qu_lo", [P, 2, S], F16)
        qr_hi = sb("qr_hi", [P, 2, S], F16)
        qr_lo = sb("qr_lo", [P, 2, S], F16)
        rc = sb("rc", [P, 2, S])
        rs = sb("rs", [P, 2, S])
        v = sb("v", [P, NT, D])
        prob = sb("prob", [P, 4, S])
        turned = sb("turned", [P, 2, HG, NT, P])
        stage = turned[:].rearrange("p s h j q -> p s (h j q)")
        recip_sb = sb("recip_sb", [P, S])
        stats = sb("stats", [P, NT, 6])
        mv = sb("mv", [P, NT, 2])
        small = sb("small", [P, 6, NT])
        power = sb("power", [P, NT])
        low = sb("low", [P, 8])
        den = sb("den", [P, 2, NT * HG])
        rden = sb("rden", [P, 2, NT * HG])

        w_loaded = [sem(f"w_loaded{i}") for i in range(2)]
        w_free, w_split, const_loaded, const_set = sem("w_free"), sem("w_split"), sem("const_loaded"), sem("const_set")
        x_loaded, stats_done, mv_done, small_done, z_ready, h_ready = (
            sem("x_loaded"), sem("stats_done"), sem("mv_done"), sem("small_done"), sem("z_ready"), sem("h_ready"))
        job_done, hi_done, left = sem("job_done"), sem("hi_done"), sem("left")
        rot_in, rot_sum, rot_hi, rot_lo = sem("rot_in"), sem("rot_sum"), sem("rot_hi"), sem("rot_lo")
        kr_stacked = sem("kr_stacked")
        k_stacked = [sem(f"k_stacked{g}") for g in range(NG)]
        q_stacked = [sem(f"q_stacked{g}") for g in range(NG)]
        z1_stored = sem("z1_stored")
        scored, biased, exped, turned_done = sem("scored"), sem("biased"), sem("exped"), sem("turned_done")
        kept_act, kept_dve = sem("kept_act"), sem("kept_dve")
        summed, recip_done, spread, recip_kept, normed = (sem("summed"), sem("recip_done"), sem("spread"),
                                                          sem("recip_kept"), sem("normed"))
        o_hi_done, o_lo_done = sem("o_hi_done"), sem("o_lo_done")

        J_HT, J_LAT, J_KSWAP, J_K, J_V = 0, NK, NK + 1, NK + 2, NK + 2 + NG
        J_Q = J_V + NT
        J_O = J_Q + 3 * NG
        JOBS = J_O + NT
        SPLIT = ([J_HT + k for k in range(NK)] + [J_LAT] + [J_K + g for g in range(NG)]
                 + [J_Q + 3 * g + n for g in range(NG) for n in (0, 1)])
        HI = len(SPLIT)
        RI = 1 + NG
        NS = 6
        KS, QS, KRS = 16 * 3 * HG, 16 * 4 * HG, 16 * 3
        scale_nope = 1.0 / (WS * 8.0)

        loads = [(wa_hi[:], wa_lo[:], wkva.rearrange("(k p) n -> p k n", p=P), P, NK, R + DH),
                 (wb_hi[:], wb_lo[:], wkvb, R, 1, D),
                 (wq_hi[:, :, 0:D], wq_lo[:, :, 0:D], wq[:, 0:D].rearrange("(k p) n -> p k n", p=P), P, NK, D),
                 (wq_hi[:, :, D:2 * D], wq_lo[:, :, D:2 * D], wq[:, D:2 * D].rearrange("(k p) n -> p k n", p=P), P, NK, D),
                 (wo_hi[:], wo_lo[:], wo.rearrange("(g p) n -> p g n", p=P), P, NG, D)]

        def staged(n):
            _, _, src, rows, k, w = loads[n]
            a = stage[0:rows, n % 2, 0:k * w]
            return a.rearrange("p (k n) -> p k n", k=k) if len(src.shape) == 3 else a

        block = ctx.enter_context(nc.Block())

        @block.sync
        def _(sp):
            for dst, src in ((idn[:], ident), (swp[:], swap), (rot[:], cos_sin), (tri[:], causal),
                             (wn[:], w_norm)):
                sp.dma_start(dst, src).then_inc(const_loaded, 16)
            for n, (_, _, src, *_) in enumerate(loads):
                if n >= 2:
                    sp.wait_ge(w_split, n - 1)
                sp.dma_start(staged(n), src).then_inc(w_loaded[n % 2], 16)
            with sp.Fori(0, B) as b:
                sp.wait_ge(z1_stored, b * 16 * NT + 16 * NT)
                sp.dma_start(z[:], x1[bass.ds(b * 1, 1), :, :].rearrange("a (t p) n -> p (a t) n", p=P)).then_inc(x_loaded, 16)
                sp.wait_ge(rot_lo, b * RI + 1)
                for stack, row, src in ((k_stack, 1, kr_hi), (k_stack, 3, kr_hi), (k_stack2, 1, kr_lo)):
                    sp.dma_start(stack[row * DH:(row + 1) * DH, :, :],
                                 src[KR, :].unsqueeze(1).broadcast_to([DH, H, S])).then_inc(kr_stacked, 16)
                for g in range(NG):
                    sp.wait_ge(left, b * JOBS + JOBS + J_K + g + 1)
                    for stack, row, src in ((k_stack, 0, kn_hi), (k_stack, 2, kn_hi), (k_stack2, 0, kn_lo)):
                        for hh in range(HG):
                            sp.dma_start(stack[row * DH:(row + 1) * DH, g * HG + hh, :],
                                         src[hh * DH:(hh + 1) * DH, g % 2, :]).then_inc(k_stacked[g], 16)
                for g in range(NG):
                    sp.wait_ge(left, b * JOBS + JOBS + J_Q + 3 * g + 1)
                    for row, src in ((0, qn_hi), (2, qn_lo)):
                        for hh in range(HG):
                            sp.dma_start(q_stack[row * DH:(row + 1) * DH, g * HG + hh, :],
                                         src[hh * DH:(hh + 1) * DH, g % 2, :]).then_inc(q_stacked[g], 16)
                    sp.wait_ge(rot_lo, b * RI + g + 2)
                    for row, src in ((1, qr_hi), (3, qr_lo)):
                        for hh in range(HG):
                            sp.dma_start(q_stack[row * DH:(row + 1) * DH, g * HG + hh, :],
                                         src[hh * DH:(hh + 1) * DH, g % 2, :]).then_inc(q_stacked[g], 16)
                for t in range(NT):
                    sp.wait_ge(left, b * JOBS + JOBS + J_O + t + 1)
                    sp.dma_start(z1[bass.ds(b * 1, 1), t * P:(t + 1) * P, :].rearrange("a p n -> p (a n)"),
                                 z[:, t, :]).then_inc(z1_stored, 16)
            sp.wait_ge(z1_stored, 16 * NT * (B + 1))

        @block.gpsimd
        def _(pool):
            pool.sem_inc(z1_stored, 16 * NT)
            nc.gpsimd.memset(power[:], -0.5).then_inc(const_set, 1)
            pool.wait_ge(const_set, 1)
            with pool.Fori(0, B) as b:
                def add(out, a, c):
                    return nc.gpsimd.tensor_scalar(small[:, out, :], a, c, None, ALU.add)

                def two(out, a, c, op):
                    return nc.gpsimd.tensor_tensor(small[:, out, :], a, c, op)

                pool.wait_ge(mv_done, b * NT + NT)
                pool.nop(nofuse=True)
                add(0, mv[:, :, 1], EPS).then_inc(small_done, 1)
                pool.wait_ge(small_done, b * NS + 1)
                two(1, small[:, 0, :], power[:], ALU.pow).then_inc(small_done, 1)
                pool.wait_ge(small_done, b * NS + 2)
                two(2, small[:, 1, :], small[:, 1, :], ALU.mult).then_inc(small_done, 1)
                pool.wait_ge(small_done, b * NS + 3)
                two(3, small[:, 2, :], mv[:, :, 1], ALU.mult).then_inc(small_done, 1)
                pool.wait_ge(small_done, b * NS + 4)
                pool.nop(nofuse=True)
                add(4, small[:, 3, :], EPS).then_inc(small_done, 1)
                pool.wait_ge(small_done, b * NS + 5)
                two(5, small[:, 4, :], power[:], ALU.pow).then_inc(small_done, 1)
                for r in range(RI):
                    rows, hi, lo = (KR, kr_hi[KR, :], kr_lo[KR, :]) if r == 0 else (
                        slice(0, P), qr_hi[:, (r - 1) % 2, :], qr_lo[:, (r - 1) % 2, :])
                    pool.wait_ge(rot_in, b * RI + r + 1)
                    nc.gpsimd.tensor_tensor(rc[rows, r % 2, :], rc[rows, r % 2, :], rs[rows, r % 2, :], ALU.add).then_inc(rot_sum, 1)
                    pool.wait_ge(rot_hi, b * RI + r + 1)
                    nc.gpsimd.tensor_tensor(lo, rc[rows, r % 2, :], hi, ALU.subtract).then_inc(rot_lo, 1)
                for g in range(NG):
                    pool.wait_ge(o_hi_done, b * NG + g + 1)
                    nc.gpsimd.tensor_tensor(ht_lo[:, g, :], recip_sb[:], ht_hi[:, g, :], ALU.subtract).then_inc(o_lo_done, 1)

        @block.scalar
        def _(act):
            for n, (hi, *_) in enumerate(loads):
                act.wait_ge(w_loaded[n % 2], 16 * (n // 2 + 1))
                nc.scalar.activation(hi, staged(n), ACT.Copy, scale=WS).then_inc(w_free, 1)
            act.wait_ge(const_loaded, 80)
            with act.Fori(0, B) as b:
                def high(job, out, scale=1.0, rows=P):
                    act.wait_ge(job_done, b * JOBS + job + 1)
                    nc.scalar.activation(out, bank[job % PROJ][0:rows, :], ACT.Copy, scale=scale).then_inc(hi_done, 1)

                def rotated(r):
                    if r >= 3:
                        act.wait_ge(q_stacked[r - 3], b * QS + QS)
                    act.wait_ge(rot_sum, b * RI + r + 1)
                    out, src = (kr_hi[KR, :], rc[KR, 0, :]) if r == 0 else (qr_hi[:, (r - 1) % 2, :], rc[:, r % 2, :])
                    nc.scalar.activation(out, src, ACT.Copy).then_inc(rot_hi, 1)

                act.wait_ge(small_done, b * NS + NS)
                for t in range(NT):
                    act.wait_ge(z_ready, b * NT + t + 1)
                    nc.scalar.activation(hn[:, t, :], z[:, t, :], ACT.Copy, scale=small[:, 5, t:t + 1]).then_inc(h_ready, 1)
                for k in range(NK):
                    high(J_HT + k, ht_hi[:, k, :], wn[:, k:k + 1])
                high(J_LAT, lat_hi[:], 1.0 / WS, R + DH)
                for g in range(NG):
                    if g >= 2:
                        act.wait_ge(k_stacked[g - 2], b * KS + KS)
                    high(J_K + g, kn_hi[:, g % 2, :], 1.0 / WS)
                    if g == 0:
                        rotated(0)
                for g in range(NG):
                    if g >= 2:
                        act.wait_ge(q_stacked[g - 2], b * QS + QS)
                    high(J_Q + 3 * g, qn_hi[:, g % 2, :], scale_nope)
                    high(J_Q + 3 * g + 1, qu_hi[:, g % 2, :], 1.0 / WS)
                    if g:
                        rotated(g)
                rotated(NG)

                def keep(n):
                    i = unit_of(n)[1]
                    act.wait_ge(turned_done, b * UNITS + n + 1)
                    nc.scalar.activation(turned[:, n // HG % 2, n % HG, 0:i + 1, :],
                                         turn_bank[n % 3][:, 0:(i + 1) * P].rearrange("p (j q) -> p j q", q=P),
                                         ACT.Copy).then_inc(kept_act, 1)

                for step in range(UNITS + 9):
                    if step < UNITS:
                        g, i, hh = unit_of(step)
                        w = (i + 1) * P
                        act.wait_ge(biased, b * UNITS + step + 1)
                        nc.scalar.activation(prob[:, step % 4, 0:w], prob[:, step % 4, 0:w], ACT.Exp, scale=-1.0,
                                             bias=low[:, step % 8:step % 8 + 1],
                                             accum_out=den[:, g % 2, i * HG + hh:i * HG + hh + 1]).then_inc(exped, 1)
                    n = step - 2
                    if 0 <= n < UNITS and n % 2 == 0:
                        if n >= 2 * HG:
                            act.wait_ge(summed, b * (UNITS // HG) + n // HG - 1)
                        keep(n)
                    g, r = divmod(step - 9, NT * HG)
                    if r == NT * HG - 1 and g >= 0:
                        act.wait_ge(spread, b * NG + g + 1)
                        if g:
                            act.wait_ge(o_lo_done, b * NG + g)
                        nc.scalar.activation(recip_sb[:], recip_bank[:], ACT.Copy).then_inc(recip_kept, 1)
                        act.wait_ge(normed, b * NG + g + 1)
                        nc.scalar.activation(ht_hi[:, g, :], recip_sb[:], ACT.Copy).then_inc(o_hi_done, 1)

        @block.vector
        def _(dve):
            dve.sem_inc(left, JOBS)
            for n, (hi, lo, *_) in enumerate(loads):
                dve.wait_ge(w_free, n + 1)
                nc.vector.scalar_tensor_tensor(out=lo, in0=staged(n), scalar=WS, in1=hi, op0=ALU.mult,
                                               op1=ALU.subtract).then_inc(w_split, 1)
            dve.wait_ge(const_loaded, 80)
            with dve.Fori(0, B) as b:
                def lower(job, out, hi, scale=1.0, rows=P):
                    dve.wait_ge(hi_done, b * HI + SPLIT.index(job) + 1)
                    nc.vector.scalar_tensor_tensor(out=out, in0=bank[job % PROJ][0:rows, :], scalar=scale, in1=hi,
                                                   op0=ALU.mult, op1=ALU.subtract).then_inc(left, 1)

                dve.wait_ge(x_loaded, b * 16 + 16)
                for t in range(NT):
                    nc.vector.bn_stats(stats[:, t, :], z[:, t, :]).then_inc(stats_done, 1)
                for t in range(NT):
                    dve.wait_ge(stats_done, b * NT + t + 1)
                    dve.nop(nofuse=True)
                    nc.vector.bn_aggr(mv[:, t, :], stats[:, t, :]).then_inc(mv_done, 1)
                dve.wait_ge(mv_done, b * NT + NT)
                dve.wait_ge(small_done, b * NS + 2)
                for t in range(NT):
                    nc.vector.tensor_scalar(z[:, t, :], z[:, t, :], mv[:, t, 0:1], small[:, 1, t:t + 1], ALU.subtract,
                                            ALU.mult).then_inc(z_ready, 1)
                for k in range(NK):
                    lower(J_HT + k, ht_lo[:, k, :], ht_hi[:, k, :], wn[:, k:k + 1])
                dve.wait_ge(job_done, b * JOBS + J_LAT + 1)
                dve.wait_ge(hi_done, b * HI + SPLIT.index(J_LAT) + 1)
                nc.vector.tensor_tensor(rc[KR, 0, :], bank[J_LAT % PROJ][KR, :], rot[KR, 2, :], ALU.mult)
                lower(J_LAT, lat_lo[:], lat_hi[:], 1.0 / WS, R + DH)
                dve.wait_ge(job_done, b * JOBS + J_KSWAP + 1)
                nc.vector.tensor_tensor(rs[KR, 0, :], bank[J_KSWAP % PROJ][KR, :], rot[KR, 3, :], ALU.mult).then_inc(rot_in, 1)
                dve.wait_ge(rot_in, b * RI + 1)
                dve.sem_inc(left, 1)
                for g in range(NG):
                    lower(J_K + g, kn_lo[:, g % 2, :], kn_hi[:, g % 2, :], 1.0 / WS)
                for t in range(NT):
                    dve.wait_ge(job_done, b * JOBS + J_V + t + 1)
                    nc.vector.tensor_scalar(v[:, t, :], bank[(J_V + t) % PROJ][:], 1.0 / WS, None, ALU.mult).then_inc(left, 1)
                for g in range(NG):
                    r = g + 1
                    lower(J_Q + 3 * g, qn_lo[:, g % 2, :], qn_hi[:, g % 2, :], scale_nope)
                    job = J_Q + 3 * g + 1
                    if r >= 2:
                        dve.wait_ge(rot_lo, b * RI + r - 1)
                    dve.wait_ge(hi_done, b * HI + SPLIT.index(job) + 1)
                    nc.vector.tensor_tensor(rc[:, r % 2, :], bank[job % PROJ][:], rot[:, 0, :], ALU.mult)
                    lower(job, qu_lo[:, g % 2, :], qu_hi[:, g % 2, :], 1.0 / WS)
                    dve.wait_ge(job_done, b * JOBS + job + 2)
                    nc.vector.tensor_tensor(rs[:, r % 2, :], bank[(job + 1) % PROJ][:], rot[:, 1, :], ALU.mult).then_inc(rot_in, 1)
                    dve.wait_ge(rot_in, b * RI + r + 1)
                    dve.sem_inc(left, 1)

                for step in range(UNITS + 9):
                    if step < UNITS:
                        g, i, hh = unit_of(step)
                        w = (i + 1) * P
                        dve.wait_ge(scored, b * UNITS + step + 1)
                        if step >= 4:
                            dve.wait_ge(turned_done, b * UNITS + step - 3)
                        at = (NT - 1 - i) * P
                        dve.nop(nofuse=True)
                        nc.vector.tensor_tensor_reduce(out=prob[:, step % 4, 0:w], in0=score_bank[step % 3][:, 0:w],
                                                       in1=tri[:, at:at + w], scale=-1.0, scalar=3e38,
                                                       op0=ALU.add, op1=ALU.min,
                                                       accum_out=low[:, step % 8:step % 8 + 1]).then_inc(biased, 1)
                    n = step - 2
                    if 0 <= n < UNITS and n % 2 == 1:
                        i = unit_of(n)[1]
                        if n >= 2 * HG:
                            dve.wait_ge(summed, b * (UNITS // HG) + n // HG - 1)
                        dve.wait_ge(turned_done, b * UNITS + n + 1)
                        nc.vector.tensor_copy(turned[:, n // HG % 2, n % HG, 0:i + 1, :],
                                              turn_bank[n % 3][:, 0:(i + 1) * P].rearrange("p (j q) -> p j q", q=P)
                                              ).then_inc(kept_dve, 1)
                    g, r = divmod(step - 4, NT * HG)
                    if r == NT * HG - 1 and g >= 0:
                        dve.wait_ge(exped, b * UNITS + (g + 1) * NT * HG)
                        nc.vector.reciprocal(rden[:, g % 2, :], den[:, g % 2, :]).then_inc(recip_done, 1)
                    g, r = divmod(step - 9, NT * HG)
                    if r == NT * HG - 1 and g >= 0:
                        dve.wait_ge(summed, b * (UNITS // HG) + (g + 1) * NT)
                        dve.wait_ge(recip_kept, b * NG + g + 1)
                        nc.vector.tensor_tensor(recip_sb[:], out_bank[:], recip_sb[:], ALU.mult).then_inc(normed, 1)
                for t in range(NT):
                    dve.wait_ge(job_done, b * JOBS + J_O + t + 1)
                    nc.vector.scalar_tensor_tensor(out=z[:, t, :], in0=bank[(J_O + t) % PROJ][:], scalar=1.0 / WS,
                                                   in1=z[:, t, :], op0=ALU.mult, op1=ALU.add).then_inc(left, 1)

        @block.tensor
        def _(pe):
            mm = nc.tensor.matmul
            pe.wait_ge(const_loaded, 80)
            pe.wait_ge(w_split, len(loads))
            with pe.Fori(0, B) as b:
                def free(job):
                    before = job - PROJ if job >= PROJ else max(j for j in range(J_O, JOBS) if j % PROJ == job % PROJ) - JOBS
                    pe.wait_ge(left, b * JOBS + JOBS + before + 1)

                def product(job, pairs, rows=P):
                    free(job)
                    out = bank[job % PROJ][0:rows, :]
                    for n, ((lh, ll), (rh, rl)) in enumerate(pairs):
                        mm(out, lh, rh, start=(n == 0), stop=False)
                        mm(out, lh, rl, start=False, stop=False)
                        last = mm(out, ll, rh, start=False, stop=(n == len(pairs) - 1))
                    last.then_inc(job_done, 1)

                pe.wait_ge(h_ready, b * NT + NT)
                for k in range(NK):
                    free(J_HT + k)
                    for t in range(NT):
                        last = nc.tensor.transpose(bank[(J_HT + k) % PROJ][:, t * P:(t + 1) * P], hn[:, t, k * P:(k + 1) * P], idn[:])
                    last.then_inc(job_done, 1)
                hs = [(ht_hi[:, k, :], ht_lo[:, k, :]) for k in range(NK)]
                pe.wait_ge(left, b * JOBS + JOBS + J_LAT)
                product(J_LAT, [((wa_hi[:, k, :], wa_lo[:, k, :]), hs[k]) for k in range(NK)], R + DH)
                pe.wait_ge(left, b * JOBS + JOBS + J_LAT + 1)
                free(J_KSWAP)
                pe.nop(nofuse=True)
                mm(bank[J_KSWAP % PROJ][KR, :], swp[KR, R:R + DH], lat_hi[KR, :], start=True, stop=False, tile_position=(R, R))
                mm(bank[J_KSWAP % PROJ][KR, :], swp[KR, R:R + DH], lat_lo[KR, :], start=False, stop=True,
                   tile_position=(R, R)).then_inc(job_done, 1)
                for g in range(NG):
                    c = slice(g * P, (g + 1) * P)
                    product(J_K + g, [((wb_hi[:, c], wb_lo[:, c]), (lat_hi[0:R, :], lat_lo[0:R, :]))])
                for t in range(NT):
                    c = slice(t * P, (t + 1) * P)
                    product(J_V + t, [((lat_hi[0:R, c], lat_lo[0:R, c]), (wb_hi[:], wb_lo[:]))])

                def swap_q(g):
                    job = J_Q + 3 * g + 2
                    pe.wait_ge(left, b * JOBS + JOBS + job)
                    mm(bank[job % PROJ][:], swp[:], qu_hi[:, g % 2, :], start=True, stop=False)
                    mm(bank[job % PROJ][:], swp[:], qu_lo[:, g % 2, :], start=False, stop=True).then_inc(job_done, 1)

                for g in range(NG):
                    for n in range(2):
                        c = slice((2 * g + n) * P, (2 * g + n + 1) * P)
                        product(J_Q + 3 * g + n, [((wq_hi[:, k, c], wq_lo[:, k, c]), hs[k]) for k in range(NK)])
                    swap_q(g)
                pe.wait_ge(left, b * JOBS + JOBS + J_O)
                pe.wait_ge(kr_stacked, b * KRS + KRS)

                for step in range(UNITS + 9):
                    if step < UNITS:
                        g, i, hh = unit_of(step)
                        if step % (NT * HG) == 0:
                            pe.wait_ge(k_stacked[g], b * KS + KS)
                            pe.wait_ge(q_stacked[g], b * QS + QS)
                        if step >= 3:
                            pe.wait_ge(biased, b * UNITS + step - 2)
                        h, w, c = g * HG + hh, (i + 1) * P, slice(i * P, (i + 1) * P)
                        mm(score_bank[step % 3][:, 0:w], q_stack[:, h, c], k_stack[:, h, 0:w], start=True, stop=False)
                        mm(score_bank[step % 3][:, 0:w], q_stack[0:2 * DH, h, c], k_stack2[:, h, 0:w], start=False,
                           stop=True).then_inc(scored, 1)
                    n = step - 2
                    if 0 <= n < UNITS:
                        i = unit_of(n)[1]
                        pe.wait_ge(exped, b * UNITS + n + 1)
                        if n >= 3:
                            pe.wait_ge((kept_act, kept_dve)[(n - 3) % 2], b * (UNITS // 2) + (n - 3) // 2 + 1)
                        for j in range(i + 1):
                            last = nc.tensor.transpose(turn_bank[n % 3][:, j * P:(j + 1) * P],
                                                       prob[:, n % 4, j * P:(j + 1) * P], idn[:])
                        last.then_inc(turned_done, 1)
                    m = step - 5
                    if m >= 0 and m % HG == HG - 1 and m < UNITS:
                        quad = m // HG
                        g, i = divmod(quad, NT)
                        pe.wait_ge(kept_act, b * (UNITS // 2) + (quad + 1) * HG // 2)
                        pe.wait_ge(kept_dve, b * (UNITS // 2) + (quad + 1) * HG // 2)
                        if i == 0 and g > 0:
                            pe.wait_ge(normed, b * NG + g)
                        for j in range(i + 1):
                            for hh in range(HG):
                                c = (g * HG + hh) * DH
                                last = mm(out_bank[hh * DH:(hh + 1) * DH, i * P:(i + 1) * P], v[:, j, c:c + DH],
                                          turned[:, quad % 2, hh, j, :], start=(j == 0), stop=(j == i),
                                          tile_position=(0, hh * DH))
                        last.then_inc(summed, 1)
                        if i == NT - 1:
                            pe.wait_ge(recip_done, b * NG + g + 1)
                            for t in range(NT):
                                for hh in range(HG):
                                    c = t * HG + hh
                                    last = mm(recip_bank[hh * DH:(hh + 1) * DH, t * P:(t + 1) * P],
                                              rden[:, g % 2, c:c + 1].broadcast_to([P, DH]), idn[:], start=True,
                                              stop=True, tile_position=(0, hh * DH))
                            last.then_inc(spread, 1)
                pe.wait_ge(o_lo_done, b * NG + NG)
                for t in range(NT):
                    c = slice(t * P, (t + 1) * P)
                    product(J_O + t, [((ht_hi[:, k, c], ht_lo[:, k, c]), (wo_hi[:, k, :], wo_lo[:, k, :])) for k in range(NK)])


def pass_c(nc, x1, z1, g_gate, w_norm, w_route, b_route, wg, wu, wd, swg, swu, swd, ident, out):
    with ExitStack() as ctx:
        def sb(name, shape, dt=F32):
            return ctx.enter_context(nc.sbuf_tensor("c_" + name, shape, dt))

        def sem(name):
            return ctx.enter_context(nc.semaphore("c_" + name))

        bank = [ctx.enter_context(nc.psum_tensor(f"c_bank{i}", [P, 512], F32)) for i in range(8)]
        RING = 4
        X = E + 1
        NU = X * NI

        g_hi = sb("g_hi", [P, X, NK, I], F16)
        g_lo = sb("g_lo", [P, X, NK, I], F16)
        u_hi = sb("u_hi", [P, X, NK, I], F16)
        u_lo = sb("u_lo", [P, X, NK, I], F16)
        d_hi = sb("d_hi", [P, X, NI, D], F16)
        d_lo = sb("d_lo", [P, X, NI, D], F16)
        r_hi = sb("r_hi", [P, NK, E], F16)
        r_lo = sb("r_lo", [P, NK, E], F16)
        wn = sb("wn", [P, NK])
        idn = sb("idn", [P, P])
        br = sb("br", [P, E])
        gate = sb("gate", [P, 2])
        z = sb("z", [P, NT, D])
        xr = sb("xr", [P, NT, D])
        xn = sb("xn", [P, NT, D])
        xt_hi = sb("xt_hi", [P, NK, S], F16)
        xt_lo = sb("xt_lo", [P, NK, S], F16)
        cb = sb("cb", [P, E, S])
        th = sb("th", [P, 2, S])
        hid = sb("hid", [P, 3, S])
        h_hi = sb("h_hi", [P, 3, S], F16)
        h_lo = sb("h_lo", [P, 3, S], F16)
        stats = sb("stats", [P, NT, 6])
        mv = sb("mv", [P, NT, 2])
        small = sb("small", [P, 4, NT])
        power = sb("power", [P, NT])
        logit = sb("logit", [P, NT, E])
        top = sb("top", [P, NT, E])
        two = sb("two", [P, NT, E])
        rest = sb("rest", [P, NT, E])
        sel = sb("sel", [P, NT, E])
        ex = sb("ex", [P, NT, E])
        tot = sb("tot", [P, 2, NT])
        share = sb("share", [P, NT, E])
        stage = cb[:].rearrange("p (s e) n -> p s (e n)", s=4)

        w_loaded = [sem(f"w_loaded{i}") for i in range(4)]
        w_free, w_split, const_loaded, const_set, gate_ready = (sem("w_free"), sem("w_split"), sem("const_loaded"),
                                                                sem("const_set"), sem("gate_ready"))
        z_loaded, xr_loaded, stats_done, mv_done, small_done, x_ready = (
            sem("z_loaded"), sem("xr_loaded"), sem("stats_done"), sem("mv_done"), sem("small_done"), sem("x_ready"))
        job_done, hi_done, left = sem("job_done"), sem("hi_done"), sem("left")
        routed, expd, shared_out = sem("routed"), sem("expd"), sem("shared_out")
        tanhed, product_done, weighed, h_hi_done, h_lo_done, downed = (
            sem("tanhed"), sem("product_done"), sem("weighed"), sem("h_hi_done"), sem("h_lo_done"), sem("downed"))
        step_done = sem("step_done")
        two_set = sem("two_set")
        sum_done, out_ready, out_stored = sem("sum_done"), sem("out_ready"), sem("out_stored")

        J_T, J_L, J_S, J_C, J_U = 0, NK, NK + 1, NK + 1 + 2 * NI, NK + 1 + 2 * NI + E
        JOBS = J_U + 2 * (NU - NI)

        def job_of(n):
            return J_S + 2 * n if n < NI else J_U + 2 * (n - NI)

        NSM = 4
        RT = 5 + 2 * NT + 4
        LAG = 2
        DOWN = HS / (2.0 * WS * WS)

        loads = [(r_hi[:], r_lo[:], w_route.rearrange("(k p) n -> p k n", p=P), NK, E)]
        for e in range(X):
            for hi, lo, own, routed_w, k, w in ((g_hi, g_lo, swg, wg, NK, I), (u_hi, u_lo, swu, wu, NK, I),
                                                (d_hi, d_lo, swd, wd, NI, D)):
                src = own[0] if e == 0 else routed_w[e - 1]
                loads.append((hi[:, e], lo[:, e], src.rearrange("(k p) n -> p k n", p=P), k, w))

        def staged(n):
            _, _, _, k, w = loads[n]
            return stage[:, n % 4, 0:k * w].rearrange("p (k n) -> p k n", k=k)

        block = ctx.enter_context(nc.Block())

        @block.sync
        def _(sp):
            sp.dma_start(idn[:], ident).then_inc(const_loaded, 16)
            sp.dma_start(wn[:], w_norm).then_inc(const_loaded, 16)
            sp.dma_start(br[:], b_route.rearrange("(a n) -> a n", a=1).broadcast_to([P, E])).then_inc(const_loaded, 16)
            sp.dma_start(gate[:, 0:1], g_gate.rearrange("(a n) -> a n", a=1).broadcast_to([P, 1])).then_inc(const_loaded, 16)
            for n, (_, _, src, *_) in enumerate(loads):
                if n >= 4:
                    sp.wait_ge(w_split, n - 3)
                sp.dma_start(staged(n), src).then_inc(w_loaded[n % 4], 16)
            with sp.Fori(0, B) as b:
                sp.wait_ge(sum_done, b * NT + NT)
                sp.dma_start(z[:], z1[bass.ds(b * 1, 1), :, :].rearrange("a (t p) n -> p (a t) n", p=P)).then_inc(z_loaded, 16)
                sp.wait_ge(out_stored, b * 16 * NT + 16 * NT)
                sp.dma_start(xr[:], x1[bass.ds(b * 1, 1), :, :].rearrange("a (t p) n -> p (a t) n", p=P)).then_inc(xr_loaded, 16)
                for t in range(NT):
                    sp.wait_ge(out_ready, b * NT + t + 1)
                    sp.dma_start(out[bass.ds(b * 1, 1), t * P:(t + 1) * P, :].rearrange("a p n -> p (a n)"),
                                 xr[:, t, :]).then_inc(out_stored, 16)
            sp.wait_ge(out_stored, 16 * NT * (B + 1))

        @block.gpsimd
        def _(pool):
            pool.sem_inc(out_stored, 16 * NT)
            nc.gpsimd.memset(power[:], -0.5).then_inc(const_set, 1)
            pool.wait_ge(const_set, 1)
            with pool.Fori(0, B) as b:
                pool.wait_ge(mv_done, b * NT + NT)
                nc.gpsimd.tensor_tensor(small[:, 0, :], mv[:, :, 0], mv[:, :, 0], ALU.mult).then_inc(small_done, 1)
                pool.wait_ge(small_done, b * NSM + 1)
                nc.gpsimd.tensor_tensor(small[:, 1, :], small[:, 0, :], mv[:, :, 1], ALU.add).then_inc(small_done, 1)
                pool.wait_ge(small_done, b * NSM + 2)
                pool.nop(nofuse=True)
                nc.gpsimd.tensor_scalar(small[:, 2, :], small[:, 1, :], EPS, None, ALU.add).then_inc(small_done, 1)
                pool.wait_ge(small_done, b * NSM + 3)
                nc.gpsimd.tensor_tensor(small[:, 3, :], small[:, 2, :], power[:], ALU.pow).then_inc(small_done, 1)
                for n in range(NU):
                    pool.wait_ge(product_done, b * NU + n + 1)
                    if n < NI:
                        pool.nop(nofuse=True)
                        nc.gpsimd.tensor_scalar(hid[:, n % 3, :], hid[:, n % 3, :], DOWN, None, ALU.mult).then_inc(weighed, 1)
                    else:
                        if n == NI:
                            pool.wait_ge(left, b * JOBS + JOBS + J_C + E)
                        nc.gpsimd.tensor_tensor(hid[:, n % 3, :], hid[:, n % 3, :], cb[:, n // NI - 1, :], ALU.mult).then_inc(weighed, 1)

        @block.scalar
        def _(act):
            act.wait_ge(const_loaded, 64)
            nc.scalar.activation(gate[:, 1:2], gate[:, 0:1], ACT.Tanh).then_inc(gate_ready, 1)
            for n, (hi, *_) in enumerate(loads):
                act.wait_ge(w_loaded[n % 4], 16 * (n // 4 + 1))
                nc.scalar.activation(hi, staged(n), ACT.Copy, scale=WS).then_inc(w_free, 1)
            with act.Fori(0, B) as b:
                act.wait_ge(small_done, b * NSM + NSM)
                for t in range(NT):
                    nc.scalar.activation(xn[:, t, :], z[:, t, :], ACT.Copy, scale=small[:, 3, t:t + 1]).then_inc(x_ready, 1)
                for k in range(NK):
                    act.wait_ge(job_done, b * JOBS + J_T + k + 1)
                    nc.scalar.activation(xt_hi[:, k, :], bank[(J_T + k) % RING][:], ACT.Copy, scale=wn[:, k:k + 1]).then_inc(hi_done, 1)
                for n in range(NU + 1):
                    if n < NU:
                        act.wait_ge(job_done, b * JOBS + job_of(n) + 1)
                        if n >= 2:
                            act.wait_ge(product_done, b * NU + n - 1)
                        nc.scalar.activation(th[:, n % 2, :], bank[job_of(n) % RING][:], ACT.Tanh, scale=0.5 / WS).then_inc(tanhed, 1)
                    if n == NI - 1:
                        act.wait_ge(routed, b * RT + RT - 5)
                        nc.scalar.activation(ex[:], ex[:], ACT.Exp).then_inc(expd, 1)
                    if n >= 1:
                        m = n - 1
                        act.wait_ge(weighed, b * NU + m + 1)
                        if m >= 3:
                            act.wait_ge(downed, b * NU + m - 2)
                        nc.scalar.activation(h_hi[:, m % 3, :], hid[:, m % 3, :], ACT.Copy).then_inc(h_hi_done, 1)

        @block.vector
        def _(dve):
            dve.sem_inc(left, JOBS)
            dve.sem_inc(sum_done, NT)
            nc.vector.memset(two[:], -3e38).then_inc(two_set, 1)
            for n, (hi, lo, *_) in enumerate(loads):
                dve.wait_ge(w_free, n + 1)
                nc.vector.scalar_tensor_tensor(out=lo, in0=staged(n), scalar=WS, in1=hi, op0=ALU.mult,
                                               op1=ALU.subtract).then_inc(w_split, 1)
            dve.wait_ge(const_loaded, 64)
            dve.wait_ge(gate_ready, 1)
            dve.wait_ge(two_set, 1)
            with dve.Fori(0, B) as b:
                step = [0]

                def route(call):
                    call.then_inc(routed, 1)
                    step[0] += 1

                def after():
                    dve.wait_ge(routed, b * RT + step[0])
                    dve.nop(nofuse=True)

                dve.wait_ge(z_loaded, b * 16 + 16)
                for t in range(NT):
                    nc.vector.bn_stats(stats[:, t, :], z[:, t, :]).then_inc(stats_done, 1)
                for t in range(NT):
                    dve.wait_ge(stats_done, b * NT + t + 1)
                    dve.nop(nofuse=True)
                    nc.vector.bn_aggr(mv[:, t, :], stats[:, t, :]).then_inc(mv_done, 1)
                for k in range(NK):
                    dve.wait_ge(hi_done, b * NK + k + 1)
                    nc.vector.scalar_tensor_tensor(out=xt_lo[:, k, :], in0=bank[(J_T + k) % RING][:], scalar=wn[:, k:k + 1],
                                                   in1=xt_hi[:, k, :], op0=ALU.mult, op1=ALU.subtract).then_inc(left, 1)
                dve.wait_ge(job_done, b * JOBS + J_L + 1)
                route(nc.vector.scalar_tensor_tensor(out=logit[:], in0=bank[J_L % RING][:, 0:NT * E].rearrange("p (t e) -> p t e", e=E),
                                                     scalar=1.0 / WS, in1=br[:].unsqueeze(1).broadcast_to([P, NT, E]),
                                                     op0=ALU.mult, op1=ALU.add))
                after()
                dve.sem_inc(left, 1)
                for t in range(NT):
                    route(nc.vector.max(out=top[:, t, :], in_=logit[:, t, :]))
                after()
                route(nc.vector.tensor_copy(two[:, :, 0:2], top[:, :, 0:2]))
                after()
                for t in range(NT):
                    route(nc.vector.match_replace(out=rest[:, t, :], in_to_replace=two[:, t, :], in_values=logit[:, t, :],
                                                  imm_value=-1e38))
                route(nc.vector.tensor_tensor(ex[:], logit[:], top[:, :, 0:1].broadcast_to([P, NT, E]), ALU.subtract))
                after()
                route(nc.vector.tensor_tensor(sel[:], rest[:], logit[:], ALU.not_equal))
                assert step[0] == RT - 5
                after()

                def multiply(n):
                    dve.wait_ge(tanhed, b * NU + n + 1)
                    if n >= 3:
                        dve.wait_ge(h_lo_done, b * NU + n - 2)
                    nc.vector.scalar_tensor_tensor(out=hid[:, n % 3, :], in0=th[:, n % 2, :], scalar=1.0,
                                                   in1=bank[job_of(n) % RING][:], op0=ALU.add, op1=ALU.mult).then_inc(left, 1)
                    dve.wait_ge(left, b * JOBS + JOBS + job_of(n) + 1)
                    dve.wait_ge(job_done, b * JOBS + job_of(n) + 2)
                    nc.vector.tensor_tensor(hid[:, n % 3, :], hid[:, n % 3, :], bank[(job_of(n) + 1) % RING][:],
                                            ALU.mult).then_inc(product_done, 1)
                    dve.wait_ge(product_done, b * NU + n + 1)
                    dve.sem_inc(left, 1)

                def low(n):
                    dve.wait_ge(h_hi_done, b * NU + n + 1)
                    nc.vector.tensor_tensor(h_lo[:, n % 3, :], hid[:, n % 3, :], h_hi[:, n % 3, :], ALU.subtract).then_inc(h_lo_done, 1)

                multiply(0)
                multiply(1)
                low(0)
                dve.wait_ge(expd, b * 1 + 1)
                route(nc.vector.tensor_tensor(ex[:], ex[:], sel[:], ALU.mult))
                after()
                route(nc.vector.tensor_reduce(tot[:, 0, :], ex[:], AX_X, ALU.add))
                after()
                route(nc.vector.reciprocal(tot[:, 1, :], tot[:, 0, :]))
                after()
                route(nc.vector.tensor_scalar(tot[:, 0, :], tot[:, 1, :], DOWN, None, ALU.mult))
                after()
                route(nc.vector.tensor_tensor(share[:], ex[:], tot[:, 0, :].unsqueeze(2).broadcast_to([P, NT, E]), ALU.mult))
                assert step[0] == RT
                for e in range(E):
                    dve.wait_ge(job_done, b * JOBS + J_C + e + 1)
                    nc.vector.tensor_copy(cb[:, e, :], bank[(J_C + e) % RING][:]).then_inc(left, 1)
                for n in range(NI, NU + 1):
                    if n < NU:
                        multiply(n)
                    low(n - 1)
                dve.wait_ge(xr_loaded, b * 16 + 16)
                for t in range(NT):
                    dve.wait_ge(downed, b * NU + NU)
                    nc.vector.scalar_tensor_tensor(out=z[:, t, :], in0=bank[RING + t][:], scalar=1.0 / (WS * HS), in1=z[:, t, :],
                                                   op0=ALU.mult, op1=ALU.add).then_inc(step_done, 1)
                for t in range(NT):
                    dve.wait_ge(step_done, b * NT + t + 1)
                    nc.vector.scalar_tensor_tensor(out=xr[:, t, :], in0=z[:, t, :], scalar=gate[:, 1:2], in1=xr[:, t, :],
                                                   op0=ALU.mult, op1=ALU.add).then_inc(out_ready, 1)
                dve.wait_ge(out_ready, b * NT + NT)
                dve.sem_inc(sum_done, NT)

        @block.tensor
        def _(pe):
            mm = nc.tensor.matmul
            pe.wait_ge(const_loaded, 64)
            pe.wait_ge(w_split, len(loads))
            with pe.Fori(0, B) as b:
                def free(job):
                    before = job - RING if job >= RING else max(j for j in range(JOBS) if j % RING == job % RING) - JOBS
                    pe.wait_ge(left, b * JOBS + JOBS + before + 1)

                def up(n):
                    e, i = divmod(n, NI)
                    c = slice(i * P, (i + 1) * P)
                    for m, (hi, lo) in enumerate(((g_hi, g_lo), (u_hi, u_lo))):
                        job = job_of(n) + m
                        free(job)
                        for k in range(NK):
                            o = bank[job % RING][:]
                            mm(o, hi[:, e, k, c], xt_hi[:, k, :], start=(k == 0), stop=False)
                            mm(o, hi[:, e, k, c], xt_lo[:, k, :], start=False, stop=False)
                            last = mm(o, lo[:, e, k, c], xt_hi[:, k, :], start=False, stop=(k == NK - 1))
                        last.then_inc(job_done, 1)

                def down(n):
                    e, i = divmod(n, NI)
                    pe.wait_ge(h_lo_done, b * NU + n + 1)
                    for t in range(NT):
                        c = slice(t * P, (t + 1) * P)
                        o = bank[RING + t][:]
                        mm(o, h_hi[:, n % 3, c], d_hi[:, e, i, :], start=(n == 0), stop=False)
                        mm(o, h_hi[:, n % 3, c], d_lo[:, e, i, :], start=False, stop=False)
                        last = mm(o, h_lo[:, n % 3, c], d_hi[:, e, i, :], start=False, stop=(n == NU - 1))
                    last.then_inc(downed, 1)

                pe.wait_ge(x_ready, b * NT + NT)
                for k in range(NK):
                    free(J_T + k)
                    for t in range(NT):
                        last = nc.tensor.transpose(bank[(J_T + k) % RING][:, t * P:(t + 1) * P], xn[:, t, k * P:(k + 1) * P], idn[:])
                    last.then_inc(job_done, 1)
                pe.wait_ge(left, b * JOBS + JOBS + J_L)
                free(J_L)
                for t in range(NT):
                    o, c = bank[J_L % RING][:, t * E:(t + 1) * E], slice(t * P, (t + 1) * P)
                    for k in range(NK):
                        mm(o, xt_hi[:, k, c], r_hi[:, k, :], start=(k == 0), stop=False)
                        mm(o, xt_hi[:, k, c], r_lo[:, k, :], start=False, stop=False)
                        last = mm(o, xt_lo[:, k, c], r_hi[:, k, :], start=False, stop=(k == NK - 1))
                last.then_inc(job_done, 1)
                up(0)
                up(1)
                pe.wait_ge(routed, b * RT + RT)
                for e in range(E):
                    free(J_C + e)
                    for t in range(NT):
                        last = nc.tensor.transpose(bank[(J_C + e) % RING][:, t * P:(t + 1) * P],
                                                   share[:, t, e:e + 1].broadcast_to([P, P]), idn[:])
                    last.then_inc(job_done, 1)
                for n in range(NI, NU + LAG):
                    if n < NU:
                        up(n)
                    if n == LAG:
                        pe.wait_ge(sum_done, b * NT + NT)
                    down(n - LAG)


def kernel(**inputs):
    import numpy as _np
    import concourse.bacc as _bacc
    from concourse import mybir as _mybir
    from concourse.bass_utils import run_bass_kernel_spmd as _run

    nc = _bacc.Bacc("TRN2", target_bir_lowering=False, num_devices=1)
    arrays, ap = {}, {}

    def give(name, a):
        a = _np.ascontiguousarray(a)
        if a.dtype == _np.bool_:
            a = a.view(_np.int32)
        arrays["in_" + name] = a
        ap[name] = nc.dram_tensor("in_" + name, a.shape, _mybir.dt.from_np(a.dtype), kind="ExternalInput").ap()

    for name in ("x", "ctx_1024", "mask_BxS2_bf0", "g_xattn", "g_ffn") + tuple(
            "L0_xattn_" + n for n in ("Wq", "bq", "Wk", "bk", "Wv", "bv", "Wo", "bo")):
        give(name, inputs[name])
    rel = _np.asarray(inputs["L0_xattn_rel_bias"])
    far = rel.shape[1] // 2
    where = _np.clip(_np.arange(P)[:, None] - _np.arange(STRIP)[None, :] + (NT - 1) * P, -far, far) + far
    give("strips", rel[:, where].transpose(1, 0, 2))
    give("ident", _np.eye(P, dtype=_np.float32))
    wq = _np.asarray(inputs["L0_ffn_Wq"])
    give("ffn_wq", wq.reshape(D, NG, HG, 2, DH).transpose(0, 1, 3, 2, 4).reshape(D, 2 * D))
    give("ffn_wo", _np.asarray(inputs["L0_ffn_Wo"]).reshape(H, 2, DH, D)[:, 0].reshape(D, D))
    for name in ("Wkva", "Wkvb"):
        give(name, inputs["L0_ffn_" + name])
    for name in ("Wgate", "expert_bias", "Wg", "Wu", "Wd", "sWg", "sWu", "sWd"):
        give(name, inputs["L0_ffn_" + name])
    give("w_ln2", _np.asarray(inputs["L0_ffn_w_ln2"]).reshape(NK, P).T)
    give("w_ln1", _np.asarray(inputs["L0_ffn_w_ln1"]).reshape(NK, P).T)
    freqs = (1.0 / 100000.0 ** (_np.arange(0, DH, 2, dtype=_np.float32) / DH)).astype(_np.float32)
    ang = _np.outer(_np.arange(S, dtype=_np.float32), freqs).astype(_np.float32)
    cos, sin = (_np.tile(_np.repeat(f(ang).astype(_np.float32).T, 2, axis=0), (HG, 1)) for f in (_np.cos, _np.sin))
    give("cos_sin", _np.stack([cos / (8 * WS), sin / 8, cos / WS, sin], 1).astype(_np.float32))
    swap = _np.zeros((P, P), _np.float16)
    even = _np.arange(0, P, 2)
    swap[even + 1, even], swap[even, even + 1] = -1, 1
    give("swap", swap)
    give("causal", _np.where(_np.arange(STRIP)[None, :] - (NT - 1) * P <= _np.arange(P)[:, None], 0, -1e30).astype(_np.float32))
    out = nc.dram_tensor("out_0_dram", (B, S, D), F32, kind="ExternalOutput").ap()
    mask_rows = nc.dram_tensor("mask_rows", (B * H, S), F16, kind="Internal").ap()
    x1 = nc.dram_tensor("x1", (B, S, D), F32, kind="Internal").ap()
    z1 = nc.dram_tensor("z1", (B, S, D), F32, kind="Internal").ap()
    pass_a(nc, ap["x"], ap["ctx_1024"], ap["mask_BxS2_bf0"], ap["g_xattn"],
           *[ap["L0_xattn_" + n] for n in ("Wq", "bq", "Wk", "bk", "Wv", "bv", "Wo", "bo")],
           ap["strips"], ap["ident"], x1, mask_rows)
    pass_b(nc, x1, ap["w_ln1"], ap["ffn_wq"], ap["Wkva"], ap["Wkvb"], ap["ffn_wo"], ap["cos_sin"], ap["swap"],
           ap["causal"], ap["ident"], z1)
    pass_c(nc, x1, z1, ap["g_ffn"], ap["w_ln2"], *[ap[n] for n in ("Wgate", "expert_bias", "Wg", "Wu", "Wd", "sWg", "sWu", "sWd")],
           ap["ident"], out)
    r = _run(nc, [arrays], core_ids=[0])
    return r.results[0]["out_0_dram"]
```

```python
from contextlib import ExitStack

import numpy as np

import concourse.bass as bass
from concourse import mybir

F32 = mybir.dt.float32
F16 = mybir.dt.float16
U8 = mybir.dt.uint8
I32 = mybir.dt.int32
ALU = mybir.AluOpType
ACT = mybir.ActivationFunctionType
AX_X = mybir.AxisListType.X

P = 128
B = 8
S = 512
D = 512
NT = S // P
NK = D // P
H = 16
DH = 32
HG = P // DH
NG = H // HG
UNITS = H * NT
R = 64
E = 8
I = 256
NI = I // P
EPS = 1e-5
WS = 256.0
HS = 128.0
MASKED = -60000.0
STRIP = S + (NT - 1) * P
TT = B * NT
NB = 2 * TT + E
SHIFT = P.bit_length() - 1


def unit_of(n):
    g, r = divmod(n, NT * HG)
    i, hh = divmod(r, HG)
    return g, i, hh


def pass_a(nc, x, ctxt, maskb, g_gate, wq, bq, wk, bk, wv, bv, wo, bo, strips, ident, x1, mask_rows):
    with ExitStack() as ctx:
        def sb(name, shape, dt=F32):
            return ctx.enter_context(nc.sbuf_tensor("a_" + name, shape, dt))

        used = []

        def sem(name):
            used.append(ctx.enter_context(nc.semaphore("a_" + name)))
            return used[-1]

        bank = [ctx.enter_context(nc.psum_tensor(f"a_bank{i}", [P, 512], F32)) for i in range(8)]
        score_bank, turn_bank, out_bank, job_bank = bank[0:2], bank[2:4], bank[4], bank[5:8]
        RING = len(job_bank)

        w_hi = sb("w_hi", [P, 4, NK, D], F16)
        w_lo = sb("w_lo", [P, 4, NK, D], F16)
        bias = sb("bias", [DH + 1, 4, D], F16)
        ones = sb("ones", [DH + 1, P], F16)
        b_hi, b_lo = bias[0:1], bias[DH:DH + 1]
        strip = sb("strip", [P, H, STRIP])
        idn = sb("idn", [P, P])
        q_stack = sb("q_stack", [3 * DH + 1, H, S], F16)
        k_stack = sb("k_stack", [3 * DH + 1, H, S], F16)
        xn = sb("xn", [P, 2, D])
        cn = sb("cn", [P, 2, D])
        xr = sb("xr", [P, 2, D])
        ct_hi = sb("ct_hi", [P, NK, S], F16)
        ct_lo = sb("ct_lo", [P, NK, S], F16)
        xt_hi = sb("xt_hi", [P, NK, S], F16)
        xt_lo = sb("xt_lo", [P, NK, S], F16)
        o_hi = sb("o_hi", [P, NG, S], F16)
        o_lo = sb("o_lo", [P, NG, S], F16)
        qk_hi = sb("qk_hi", [P, 4, S], F16)
        qk_lo = sb("qk_lo", [P, 4, S], F16)
        v = sb("v", [P, NT, D])
        prob = sb("prob", [P, 4, S])
        turned = sb("turned", [P, 2, HG, NT, P])
        stage = turned[:].rearrange("p s h j q -> p s (h j q)")
        normal = sb("normal", [P, S])
        stats = sb("stats", [P, 2, 6])
        mv = sb("mv", [P, 2, 2])
        rstd = sb("rstd", [P, 2, 2])
        power = sb("power", [P, 1])
        low = sb("low", [P, 8])
        den = sb("den", [P, 2, NT * HG])
        rden = sb("rden", [P, 2, NT * HG])
        gate = sb("gate", [P, 2])
        bstage = strip[0:DH + 1, NG * HG - 4:NG * HG, 0:D]
        mask_words = normal[:, 0:P].bitcast(I32)
        mask8 = normal[:, 0:P].bitcast(U8)
        mask_stage = o_hi[:, 0, :]

        w_loaded = [sem(f"w_loaded{i}") for i in range(2)]
        w_free, w_split = sem("w_free"), sem("w_split")
        b_loaded, b_zeroed, b_split = sem("b_loaded"), sem("b_zeroed"), sem("b_split")
        const_loaded, ones_set, power_set, idn_loaded = sem("const_loaded"), sem("ones_set"), sem("power_set"), sem("idn_loaded")
        strips_loaded = [sem(f"strips_loaded{g}") for g in range(NG)]
        gate_ready, gate_scaled = sem("gate_ready"), sem("gate_scaled")
        mask_set, mask_stored = sem("mask_set"), sem("mask_stored")
        x_loaded = [sem(f"x_loaded{i}") for i in range(2)]
        c_loaded = [sem(f"c_loaded{i}") for i in range(2)]
        xr_loaded = [sem(f"xr_loaded{i}") for i in range(2)]
        x1_stored = [sem(f"x1_stored{i}") for i in range(2)]
        stats_done, mv_done, eps_added, rstd_done, xn_ready = (sem("stats_done"), sem("mv_done"), sem("eps_added"),
                                                               sem("rstd_done"), sem("xn_ready"))
        job_done, hi_done, left = sem("job_done"), sem("hi_done"), sem("left")
        stacked = [sem(f"stacked{g}") for g in range(NG)]
        scored, biased, exped, turned_done = sem("scored"), sem("biased"), sem("exped"), sem("turned_done")
        kept_act, kept_dve = sem("kept_act"), sem("kept_dve")
        summed, recip_done, spread_kept, normed = sem("summed"), sem("recip_done"), sem("spread_kept"), sem("normed")
        o_hi_done, o_lo_done = sem("o_hi_done"), sem("o_lo_done")

        STK = 16 * (2 * 3 * HG + 1)
        QUADS = UNITS // HG
        GS = NT * HG
        TAIL = 5
        q_scale = 1.0 / (WS * DH ** 0.5)

        CT, XT, Q, K, V, SP, O = "ct", "xt", "q", "k", "v", "spread", "o"
        own = [((Q, NG - 1), 3), ((K, NG - 1), 7)]
        ahead = [((m, t), GS // 2 + 2 * t + n) for t in range(NT) for n, m in enumerate((CT, XT))]
        for g in range(1, NG):
            own.append(((SP, g - 1), GS * g + 3))
            ahead += [((Q, g - 1), GS * g + 8), ((K, g - 1), GS * g + 15)]
        own.append(((SP, NG - 1), UNITS + 2))
        ahead += [((V, 0), UNITS), ((V, 1), UNITS + 3), ((V, 2), UNITS + 5), ((V, 3), UNITS + 6)]
        own += [((O, t), UNITS + 7 + t) for t in range(NT)]
        order = sorted(own + ahead, key=lambda j: j[1])
        rounds = {
            "first": [(m, t) for t in range(NT) for m in (CT, XT)] + [(m, g) for g in range(NG - 1) for m in (Q, K)]
                     + [(V, t) for t in range(NT)],
            "steady": [j for j, _ in order],
            "last": [j for j, _ in sorted(own, key=lambda j: j[1])],
        }
        ends = {j: s for j, s in order}
        STEPS = max(ends.values()) + 1
        split_kinds = (CT, XT, Q, K)

        def before(kind, b, count=lambda j: True):
            n = {k: sum(count(j) for j in r) for k, r in rounds.items()}
            return 0 if kind == "first" else n["first"] + n["steady"] * b

        def upto(kind, b, job):
            return before(kind, b) + rounds[kind].index(job) + 1

        def split_upto(kind, b, job):
            is_split = lambda j: j[0] in split_kinds
            r = rounds[kind]
            return before(kind, b, is_split) + sum(is_split(j) for j in r[:r.index(job) + 1])

        def bank_of(kind, job):
            return job_bank[rounds[kind].index(job) % RING]

        def ended(kind, step):
            return [j for j in rounds[kind] if ends[j] == step]

        block = ctx.enter_context(nc.Block())

        @block.sync
        def _(sp):
            def load(src, dst, loaded, b, t, freed):
                if freed:
                    sp.wait_ge(*freed)
                sp.dma_start(dst[:, t % 2, :], src[bass.ds(b * 1, 1), t * P:(t + 1) * P, :].rearrange("a p n -> p (a n)")
                             ).then_inc(loaded[t % 2], 16)

            def stack(kind, b, of, g, part):
                sp.wait_ge(left, upto(kind, b, ((Q, K)[part], g)))
                dst, slot = (q_stack, k_stack)[part], 2 * (g % 2) + part
                for row, src in enumerate(((qk_hi, qk_lo, qk_hi), (qk_hi, qk_hi, qk_lo))[part]):
                    for hh in range(HG):
                        sp.dma_start(dst[row * DH:(row + 1) * DH, g * HG + hh, :],
                                     src[hh * DH:(hh + 1) * DH, slot, :]).then_inc(stacked[g], 16)
                if part:
                    rows = mask_rows.rearrange("(b h) n -> b h n", h=H)
                    sp.dma_start(k_stack[3 * DH:3 * DH + 1, g * HG:(g + 1) * HG, :],
                                 rows[bass.ds(of * 1, 1), g * HG:(g + 1) * HG, :]).then_inc(stacked[g], 16)

            sp.dma_start(idn[:], ident).then_inc(idn_loaded, 16)
            for t in range(2):
                load(ctxt, cn, c_loaded, 0, t, None)
                load(x, xn, x_loaded, 0, t, None)
            for n, w in enumerate((bq, bk, bv, bo)):
                for row in (0, DH):
                    sp.dma_start(bstage[row:row + 1, n, :], w.rearrange("(a n) -> a n", a=1)).then_inc(b_loaded, 16)
            for n, w in enumerate((wq, wk, wv, wo)):
                if n >= 2:
                    sp.wait_ge(w_split, n - 1)
                sp.dma_start(stage[:, n % 2, :].rearrange("p (k n) -> p k n", k=NK),
                             w.rearrange("(k p) n -> p k n", p=P)).then_inc(w_loaded[n % 2], 16)
                if n == 0:
                    sp.dma_start(gate[:, 0:1], g_gate.rearrange("(a n) -> a n", a=1).broadcast_to([P, 1])).then_inc(const_loaded, 16)
                    for b in range(B):
                        sp.dma_start(mask_words[b * H:(b + 1) * H, :], maskb[b:b + 1, :].broadcast_to([H, S // 4])).then_inc(const_loaded, 16)
                if n == 1:
                    for t in range(2, NT):
                        load(ctxt, cn, c_loaded, 0, t, (job_done, upto("first", 0, (CT, t - 2))))
                        load(x, xn, x_loaded, 0, t, (job_done, upto("first", 0, (XT, t - 2))))
            sp.wait_ge(mask_set, 1)
            sp.dma_start(mask_rows, mask_stage).then_inc(mask_stored, 16)
            sp.wait_ge(mask_stored, 16)
            sp.wait_ge(b_split, 3)
            for g in range(NG):
                sp.dma_start(strip[:, g * HG:(g + 1) * HG, :], strips[:, g * HG:(g + 1) * HG, :]).then_inc(strips_loaded[g], 16)
                if g < NG - 1:
                    for part in range(2):
                        stack("first", 0, 0, g, part)

            def body(kind, b):
                more = kind == "steady"
                if more:
                    for t in range(2):
                        load(ctxt, cn, c_loaded, b + 1, t, None)
                        load(x, xn, x_loaded, b + 1, t, None)
                stack(kind, b, b, NG - 1, 0)
                if more:
                    for t in range(2, NT):
                        load(ctxt, cn, c_loaded, b + 1, t, (job_done, upto(kind, b, (CT, t - 2))))
                        load(x, xn, x_loaded, b + 1, t, (job_done, upto(kind, b, (XT, t - 2))))
                stack(kind, b, b, NG - 1, 1)
                for t in range(2):
                    load(x, xr, xr_loaded, b, t, (x1_stored[t], b * 32 + 32))
                for g in range(NG - 1 if more else 0):
                    for part in range(2):
                        stack(kind, b, b + 1, g, part)
                for t in range(NT):
                    sp.wait_ge(left, upto(kind, b, (O, t)))
                    sp.dma_start(x1[bass.ds(b * 1, 1), t * P:(t + 1) * P, :].rearrange("a p n -> p (a n)"),
                                 xr[:, t % 2, :]).then_inc(x1_stored[t % 2], 16)
                    if t < 2:
                        load(x, xr, xr_loaded, b, t + 2, (x1_stored[t], b * 32 + 48))

            with sp.Fori(0, B - 1) as b:
                body("steady", b)
            body("last", B - 1)
            for i in range(2):
                sp.wait_ge(x1_stored[i], 32 * (B + 1))

        @block.gpsimd
        def _(pool):
            for i in range(2):
                pool.sem_inc(x1_stored[i], 32)
            nc.gpsimd.memset(power[:], -0.5).then_inc(power_set, 1)
            pool.wait_ge(const_loaded, 16 * (1 + B))
            nc.gpsimd.tensor_scalar(mask_stage, mask8, MASKED, None, ALU.mult).then_inc(mask_set, 1)
            pool.wait_ge(power_set, 1)

            def deviations(b):
                for t in range(NT):
                    pool.wait_ge(mv_done, b * NT + t + 1)
                    pool.nop(nofuse=True)
                    nc.gpsimd.tensor_scalar(rstd[:, t % 2, 0:1], mv[:, t % 2, 1:2], EPS, None, ALU.add).then_inc(eps_added, 1)
                    pool.wait_ge(eps_added, b * NT + t + 1)
                    nc.gpsimd.tensor_tensor(rstd[:, t % 2, 1:2], rstd[:, t % 2, 0:1], power[:], ALU.pow).then_inc(rstd_done, 1)

            def body(kind, b):
                if kind == "steady":
                    deviations(b + 1)
                for g in range(NG):
                    pool.wait_ge(o_hi_done, b * NG + g + 1)
                    nc.gpsimd.tensor_tensor(o_lo[:, g, :], normal[:], o_hi[:, g, :], ALU.subtract).then_inc(o_lo_done, 1)

            deviations(0)
            with pool.Fori(0, B - 1) as b:
                body("steady", b)
            body("last", B - 1)

        @block.scalar
        def _(act):
            def high(kind, b, job):
                m, n = job
                if m not in split_kinds:
                    return
                act.wait_ge(job_done, upto(kind, b, job))
                src = bank_of(kind, job)[:]
                if m in (CT, XT):
                    out, src = (ct_hi if m == CT else xt_hi)[:, :, n * P:(n + 1) * P], src.rearrange("p (k q) -> p k q", q=P)
                    scale = 1.0
                else:
                    of = 0 if kind == "first" else b if n == NG - 1 else b + 1
                    if n >= 2:
                        act.wait_ge(stacked[n - 2], of * STK + STK)
                    elif kind != "first":
                        act.wait_ge(stacked[n + 2], of * STK)
                    out, scale = qk_hi[:, 2 * (n % 2) + (m == K), :], (q_scale if m == Q else 1.0 / WS)
                nc.scalar.activation(out, src, ACT.Copy, scale=scale).then_inc(hi_done, 1)

            def keep(b, n):
                act.wait_ge(turned_done, b * UNITS + n + 1)
                nc.scalar.activation(turned[:, n // HG % 2, n % HG, :, :],
                                     turn_bank[n % 2][:].rearrange("p (j q) -> p j q", q=P), ACT.Copy).then_inc(kept_act, 1)

            def body(kind, b):
                for step in range(STEPS + 1):
                    if step < UNITS:
                        g, i, hh = unit_of(step)
                        act.wait_ge(biased, b * UNITS + step + 1)
                        nc.scalar.activation(prob[:, step % 4, :], prob[:, step % 4, :], ACT.Exp, scale=-1.0,
                                             bias=low[:, step % 8:step % 8 + 1],
                                             accum_out=den[:, g % 2, i * HG + hh:i * HG + hh + 1]).then_inc(exped, 1)
                    n = step - 2
                    if 0 <= n < UNITS and n % 2 == 0:
                        if n >= 2 * HG:
                            act.wait_ge(summed, b * QUADS + n // HG - 1)
                        keep(b, n)
                    for job in ended(kind, step - 1):
                        high(kind, b, job)
                    g, off = divmod(step - GS, GS)
                    if g >= 0 and off == 6:
                        act.wait_ge(normed, b * NG + g + 1)
                        nc.scalar.activation(o_hi[:, g, :], normal[:], ACT.Copy).then_inc(o_hi_done, 1)

            act.wait_ge(b_loaded, 128)
            act.wait_ge(b_zeroed, 1)
            nc.scalar.activation(b_hi, bstage[0:1], ACT.Copy, scale=WS).then_inc(b_split, 1)
            nc.scalar.activation(b_lo, bstage[DH:DH + 1], ACT.Copy, scale=WS).then_inc(b_split, 1)

            def split(n):
                act.wait_ge(w_loaded[n % 2], 16 * (n // 2 + 1))
                nc.scalar.activation(w_hi[:, n, :, :].rearrange("p k n -> p (k n)"), stage[:, n % 2, :], ACT.Copy,
                                     scale=WS).then_inc(w_free, 1)

            for job in rounds["first"]:
                if job == (CT, 2):
                    split(0)
                if job == (Q, 0):
                    for n in range(1, 4):
                        split(n)
                    act.wait_ge(const_loaded, 16 * (1 + B))
                    nc.scalar.activation(gate[:, 1:2], gate[:, 0:1], ACT.Tanh).then_inc(gate_ready, 1)
                high("first", 0, job)
            act.wait_ge(mask_stored, 16)
            with act.Fori(0, B - 1) as b:
                body("steady", b)
            body("last", B - 1)

        @block.vector
        def _(dve):
            def leave(kind, b, job):
                m, n = job
                src = bank_of(kind, job)[:]
                if m in split_kinds:
                    dve.wait_ge(hi_done, split_upto(kind, b, job))
                    if m in (CT, XT):
                        hi, lo = (ct_hi, ct_lo) if m == CT else (xt_hi, xt_lo)
                        c = slice(n * P, (n + 1) * P)
                        hi, lo, src, scale = hi[:, :, c], lo[:, :, c], src.rearrange("p (k q) -> p k q", q=P), 1.0
                    else:
                        slot = 2 * (n % 2) + (m == K)
                        hi, lo, scale = qk_hi[:, slot, :], qk_lo[:, slot, :], (q_scale if m == Q else 1.0 / WS)
                    nc.vector.scalar_tensor_tensor(out=lo, in0=src, scalar=scale, in1=hi, op0=ALU.mult,
                                                   op1=ALU.subtract).then_inc(left, 1)
                    return
                dve.wait_ge(job_done, upto(kind, b, job))
                if m == V:
                    if kind != "first":
                        dve.wait_ge(summed, b * QUADS + QUADS)
                    nc.vector.tensor_scalar(v[:, n, :], src, 1.0 / WS, None, ALU.mult).then_inc(left, 1)
                elif m == SP:
                    if n:
                        dve.wait_ge(o_lo_done, b * NG + n)
                    nc.vector.tensor_copy(normal[:], src).then_inc(left, 1)
                else:
                    dve.wait_ge(xr_loaded[n % 2], b * 32 + 16 * (n // 2 + 1))
                    nc.vector.scalar_tensor_tensor(out=xr[:, n % 2, :], in0=src, scalar=gate[:, 0:1], in1=xr[:, n % 2, :],
                                                   op0=ALU.mult, op1=ALU.add).then_inc(left, 1)

            def moments(b, t):
                dve.wait_ge(x_loaded[t % 2], b * 32 + 16 * (t // 2 + 1))
                nc.vector.bn_stats(stats[:, t % 2, :], xn[:, t % 2, :]).then_inc(stats_done, 1)
                dve.wait_ge(stats_done, b * NT + t + 1)
                dve.nop(nofuse=True)
                nc.vector.bn_aggr(mv[:, t % 2, :], stats[:, t % 2, :]).then_inc(mv_done, 1)

            def normalise(b, t):
                dve.wait_ge(mv_done, b * NT + t + 1)
                dve.wait_ge(rstd_done, b * NT + t + 1)
                nc.vector.tensor_scalar(xn[:, t % 2, :], xn[:, t % 2, :], mv[:, t % 2, 0:1], rstd[:, t % 2, 1:2], ALU.subtract,
                                        ALU.mult).then_inc(xn_ready, 1)

            XN = {3: 0, 5: 1, 11: 2, 13: 3}

            def body(kind, b):
                for step in range(STEPS + 2):
                    if step < UNITS:
                        g, i, hh = unit_of(step)
                        if kind == "steady" and step % GS == 0:
                            dve.wait_ge(strips_loaded[g], 16)
                        dve.wait_ge(scored, b * UNITS + step + 1)
                        if step >= 4:
                            dve.wait_ge(turned_done, b * UNITS + step - 3)
                        at = (NT - 1 - i) * P
                        dve.nop(nofuse=True)
                        nc.vector.tensor_tensor_reduce(out=prob[:, step % 4, :], in0=score_bank[step % 2][:],
                                                       in1=strip[:, g * HG + hh, at:at + S], scale=-1.0, scalar=3e38,
                                                       op0=ALU.add, op1=ALU.min,
                                                       accum_out=low[:, step % 8:step % 8 + 1]).then_inc(biased, 1)
                    n = step - 2
                    if 0 <= n < UNITS and n % 2 == 1:
                        if n >= 2 * HG:
                            dve.wait_ge(summed, b * QUADS + n // HG - 1)
                        dve.wait_ge(turned_done, b * UNITS + n + 1)
                        nc.vector.tensor_copy(turned[:, n // HG % 2, n % HG, :, :],
                                              turn_bank[n % 2][:].rearrange("p (j q) -> p j q", q=P)).then_inc(kept_dve, 1)
                    g, off = divmod(step - GS, GS)
                    if g >= 0 and off == 1:
                        dve.wait_ge(exped, b * UNITS + (g + 1) * GS)
                        nc.vector.reciprocal(rden[:, g % 2, :], den[:, g % 2, :]).then_inc(recip_done, 1)
                    if g >= 0 and off == 6:
                        dve.wait_ge(summed, b * QUADS + (g + 1) * NT)
                        dve.wait_ge(left, upto(kind, b, (SP, g)))
                        nc.vector.tensor_tensor(normal[:], out_bank[:], normal[:], ALU.mult).then_inc(normed, 1)
                    if kind == "steady" and step in XN:
                        moments(b + 1, XN[step])
                    if kind == "steady" and step - 1 in XN:
                        normalise(b + 1, XN[step - 1])
                    for job in ended(kind, step - 2):
                        leave(kind, b, job)

            nc.vector.memset(bias[:], 0.0).then_inc(b_zeroed, 1)
            nc.vector.memset(ones[:], 1.0).then_inc(ones_set, 1)
            nc.vector.memset(q_stack[3 * DH:3 * DH + 1, :, :], 1.0).then_inc(ones_set, 1)
            dve.wait_ge(b_split, 2)
            nc.vector.scalar_tensor_tensor(out=b_lo, in0=bstage[DH:DH + 1], scalar=WS, in1=b_lo, op0=ALU.mult,
                                           op1=ALU.subtract).then_inc(b_split, 1)

            def split(n):
                dve.wait_ge(w_free, n + 1)
                nc.vector.scalar_tensor_tensor(out=w_lo[:, n, :, :].rearrange("p k n -> p (k n)"), in0=stage[:, n % 2, :],
                                               scalar=WS, in1=w_hi[:, n, :, :].rearrange("p k n -> p (k n)"),
                                               op0=ALU.mult, op1=ALU.subtract).then_inc(w_split, 1)

            for t in range(2):
                moments(0, t)
                normalise(0, t)
            for job in rounds["first"]:
                if job == (CT, 2):
                    split(0)
                if job[0] == CT and job[1] >= 2:
                    moments(0, job[1])
                    normalise(0, job[1])
                if job == (Q, 0):
                    for n in range(1, 4):
                        split(n)
                    dve.wait_ge(gate_ready, 1)
                    nc.vector.tensor_scalar(gate[:, 0:1], gate[:, 1:2], 1.0 / WS, None, ALU.mult).then_inc(gate_scaled, 1)
                leave("first", 0, job)
            dve.wait_ge(gate_scaled, 1)
            with dve.Fori(0, B - 1) as b:
                body("steady", b)
            body("last", B - 1)

        @block.tensor
        def _(pe):
            mm = nc.tensor.matmul

            def free(kind, b, job):
                n = rounds[kind].index(job)
                before_it = before(kind, b) + (n - RING + 1 if n >= RING else 0)
                if kind != "first" or n >= RING:
                    pe.wait_ge(left, before_it)

            def transposes(kind, b, job):
                m, t = job
                src, loaded = (cn, c_loaded) if m == CT else (xn, None)
                of = 0 if kind == "first" else b + 1
                free(kind, b, job)
                if m == CT:
                    pe.wait_ge(c_loaded[t % 2], of * 32 + 16 * (t // 2 + 1))
                else:
                    pe.wait_ge(xn_ready, of * NT + t + 1)
                for k in range(NK):
                    last = nc.tensor.transpose(bank_of(kind, job)[:, k * P:(k + 1) * P], src[:, t % 2, k * P:(k + 1) * P], idn[:])
                last.then_inc(job_done, 1)

            def product(kind, b, job, parts=range(NK)):
                m, n = job
                o, c = bank_of(kind, job)[:], slice(n * P, (n + 1) * P)
                for k in parts:
                    if k == 0:
                        free(kind, b, job)
                    if m in (Q, K):
                        w = (m == K)
                        h, l = (ct_hi, ct_lo) if w else (xt_hi, xt_lo)
                        pairs = ((w_hi[:, w, k, c], h[:, k, :]), (w_hi[:, w, k, c], l[:, k, :]), (w_lo[:, w, k, c], h[:, k, :]))
                        both = (bias[:, int(w), c], ones[:].unsqueeze(1).broadcast_to([DH + 1, NT, P]))
                    else:
                        w = 2 if m == V else 3
                        h, l = (ct_hi, ct_lo) if m == V else (o_hi, o_lo)
                        pairs = ((h[:, k, c], w_hi[:, w, k, :]), (h[:, k, c], w_lo[:, w, k, :]), (l[:, k, c], w_hi[:, w, k, :]))
                        both = (ones[:], bias[:, w, :])
                    for i, (lhs, rhs) in enumerate(pairs):
                        mm(o, lhs, rhs, start=(k == 0 and i == 0), stop=False)
                    if k == NK - 1:
                        mm(o, *both, start=False, stop=True).then_inc(job_done, 1)

            def spread(kind, b, job):
                g = job[1]
                free(kind, b, job)
                pe.wait_ge(recip_done, b * NG + g + 1)
                for t in range(NT):
                    for hh in range(HG):
                        c = t * HG + hh
                        last = mm(bank_of(kind, job)[hh * DH:(hh + 1) * DH, t * P:(t + 1) * P],
                                  rden[:, g % 2, c:c + 1].broadcast_to([P, DH]), idn[:], start=True, stop=True,
                                  tile_position=(0, hh * DH))
                last.then_inc(job_done, 1)

            def fill(kind, b, step):
                if kind == "steady" and step == GS + 2:
                    pe.wait_ge(left, upto(kind, b, (XT, NT - 1)))
                for job in rounds[kind]:
                    m, n = job
                    end = ends[job]
                    if m in (Q, K):
                        at = [end - 3, end - 2, end - 1, end] if n == NG - 1 else [end - 6, end - 4, end - 2, end]
                        if step in at:
                            product(kind, b, job, [at.index(step)])
                    elif step == end and m in (CT, XT):
                        transposes(kind, b, job)
                    elif step == end and m == V:
                        product(kind, b, job)
                    elif step == end and m == SP:
                        spread(kind, b, job)
                    elif step == end and m == O:
                        if n == 0:
                            pe.wait_ge(o_lo_done, b * NG + NG)
                        product(kind, b, job)

            def body(kind, b):
                for step in range(STEPS + 1):
                    if step < UNITS:
                        g, i, hh = unit_of(step)
                        if step % GS == 0:
                            pe.wait_ge(stacked[g], b * STK + STK)
                        if step >= 2:
                            pe.wait_ge(biased, b * UNITS + step - 1)
                        h = g * HG + hh
                        mm(score_bank[step % 2][:], q_stack[:, h, i * P:(i + 1) * P], k_stack[:, h, :], start=True,
                           stop=True).then_inc(scored, 1)
                    fill(kind, b, step)
                    n = step - 2
                    if 0 <= n < UNITS:
                        pe.wait_ge(exped, b * UNITS + n + 1)
                        if n >= 2:
                            pe.wait_ge((kept_act, kept_dve)[n % 2], b * (UNITS // 2) + (n - 2) // 2 + 1)
                        for j in range(NT):
                            last = nc.tensor.transpose(turn_bank[n % 2][:, j * P:(j + 1) * P],
                                                       prob[:, n % 4, j * P:(j + 1) * P], idn[:])
                        last.then_inc(turned_done, 1)
                    m = step - TAIL
                    if m >= 0 and m % HG == HG - 1 and m < UNITS:
                        quad = m // HG
                        g, i = divmod(quad, NT)
                        pe.wait_ge(kept_act, b * (UNITS // 2) + (quad + 1) * HG // 2)
                        pe.wait_ge(kept_dve, b * (UNITS // 2) + (quad + 1) * HG // 2)
                        if quad == 0:
                            pe.wait_ge(left, before(kind, b))
                        if i == 0 and g > 0:
                            pe.wait_ge(normed, b * NG + g)
                        for j in range(NT):
                            for hh in range(HG):
                                c = (g * HG + hh) * DH
                                last = mm(out_bank[hh * DH:(hh + 1) * DH, i * P:(i + 1) * P], v[:, j, c:c + DH],
                                          turned[:, quad % 2, hh, j, :], start=(j == 0), stop=(j == NT - 1),
                                          tile_position=(0, hh * DH))
                        last.then_inc(summed, 1)

            pe.wait_ge(idn_loaded, 16)
            pe.wait_ge(ones_set, 2)
            for job in rounds["first"]:
                if job[0] in (CT, XT):
                    transposes("first", 0, job)
                else:
                    if job == (Q, 0):
                        pe.wait_ge(b_split, 3)
                        pe.wait_ge(w_split, 4)
                        pe.wait_ge(left, 2 * NT)
                    product("first", 0, job)
            with pe.Fori(0, B - 1) as b:
                body("steady", b)
            body("last", B - 1)
    return used


def pass_b(nc, x1, w_norm, wq, wkva, wkvb, wo, cos_sin, swap, causal, ident, z1, x_sorted, used):
    with ExitStack() as ctx:
        def sb(name, shape, dt=F32):
            return ctx.enter_context(nc.sbuf_tensor("b_" + name, shape, dt))

        def sem(name):
            return ctx.enter_context(nc.semaphore("b_" + name))

        bank = [ctx.enter_context(nc.psum_tensor(f"b_bank{i}", [P, 512], F32)) for i in range(8)]
        score_bank, turn_bank, out_bank, job_bank = bank[0:2], bank[2:4], bank[4], bank[5:8]
        RING = len(job_bank)

        KR = slice(R, R + DH)
        wq_hi = sb("wq_hi", [P, NK, 2 * D], F16)
        wq_lo = sb("wq_lo", [P, NK, 2 * D], F16)
        wa_hi = sb("wa_hi", [P, NK, R + DH], F16)
        wa_lo = sb("wa_lo", [P, NK, R + DH], F16)
        wb_hi = sb("wb_hi", [R, D], F16)
        wb_lo = sb("wb_lo", [R, D], F16)
        wo_hi = sb("wo_hi", [P, NG, D], F16)
        wo_lo = sb("wo_lo", [P, NG, D], F16)
        wn = sb("wn", [P, NK])
        idn = sb("idn", [P, P])
        swp = sb("swp", [P, P], F16)
        rot = sb("rot", [P, 4, S])
        tri = sb("tri", [P, STRIP])
        q_stack = sb("q_stack", [P, H, S], F16)
        k_stack = sb("k_stack", [P, H, S], F16)
        k_stack2 = sb("k_stack2", [2 * DH, H, S], F16)
        zn = sb("zn", [P, NT, D])
        zr = sb("zr", [P, NT, D])
        zo = sb("zo", [P, 2, D])
        hn = sb("hn", [P, NT, D])
        ht_hi = sb("ht_hi", [P, NK, S], F16)
        ht_lo = sb("ht_lo", [P, NK, S], F16)
        o_hi = sb("o_hi", [P, NG, S], F16)
        o_lo = sb("o_lo", [P, NG, S], F16)
        lat_hi = sb("lat_hi", [R + DH, S], F16)
        lat_lo = sb("lat_lo", [R + DH, S], F16)
        kr_hi = sb("kr_hi", [R + DH, S], F16)
        kr_lo = sb("kr_lo", [R + DH, S], F16)
        kn_hi = sb("kn_hi", [P, S], F16)
        kn_lo = sb("kn_lo", [P, S], F16)
        qn_hi = sb("qn_hi", [P, S], F16)
        qn_lo = sb("qn_lo", [P, S], F16)
        qu_hi = sb("qu_hi", [P, S], F16)
        qu_lo = sb("qu_lo", [P, S], F16)
        qr_hi = sb("qr_hi", [P, S], F16)
        qr_lo = sb("qr_lo", [P, S], F16)
        rc = sb("rc", [P, S])
        rs = sb("rs", [P, S])
        v = sb("v", [P, NT, D])
        prob = sb("prob", [P, 4, S])
        turned = sb("turned", [P, 2, HG, NT, P])
        stage = turned[:].rearrange("p s h j q -> p s (h j q)")
        normal = sb("normal", [P, S])
        stats = sb("stats", [P, NT, 6])
        mv = sb("mv", [P, NT, 2])
        small = sb("small", [P, NT, 6])
        power = sb("power", [P, 1])
        low = sb("low", [P, 8])
        zero = sb("zero", [P, D])
        den = sb("den", [P, 2, NT * HG])
        rden = sb("rden", [P, 2, NT * HG])

        w_loaded = [sem(f"w_loaded{i}") for i in range(2)]
        w_free, w_split, const_loaded, power_set = sem("w_free"), sem("w_split"), sem("const_loaded"), sem("power_set")
        x_loaded, stats_done, mv_done, small_done, z_ready, h_ready, moved = (
            sem("x_loaded"), sem("stats_done"), sem("mv_done"), sem("small_done"), sem("z_ready"), sem("h_ready"), sem("moved"))
        job_done, hi_done, left = sem("job_done"), sem("hi_done"), sem("left")
        rot_cos, rot_sum, rot_hi, rot_lo = sem("rot_cos"), sem("rot_sum"), sem("rot_hi"), sem("rot_lo")
        k_stacked = [sem(f"k_stacked{g}") for g in range(NG)]
        qn_stacked = [sem(f"qn_stacked{g}") for g in range(NG)]
        qr_stacked = [sem(f"qr_stacked{g}") for g in range(NG)]
        z1_stored = [sem(f"z1_stored{i}") for i in range(2)]
        zero_set, zeroed = sem("zero_set"), sem("zeroed")
        scored, biased, exped, turned_done = sem("scored"), sem("biased"), sem("exped"), sem("turned_done")
        kept_act, kept_dve = sem("kept_act"), sem("kept_dve")
        summed, recip_done, normed = sem("summed"), sem("recip_done"), sem("normed")
        o_hi_done, o_lo_done = sem("o_hi_done"), sem("o_lo_done")

        QUADS = UNITS // HG
        GS = NT * HG
        TAIL = 5
        NS = 6
        STK_K, STK_Q = 16 * 3 * (HG + 1), 16 * 2 * HG
        scale_nope = 1.0 / (WS * 8.0)

        HT, LAT, KSW, K, V, QN, QR, QSW, SP, O = "ht", "lat", "kswap", "k", "v", "qn", "qr", "qswap", "spread", "o"
        G3 = NG - 1
        own = [((K, G3), 1), ((QN, G3), 5), ((QR, G3), 9), ((QSW, G3), 12)]
        ahead = [((HT, 0), 10), ((HT, 1), 11), ((HT, 2), 13), ((HT, 3), 14),
                 ((LAT, 0), GS + 5), ((KSW, 0), GS + 8), ((QN, 0), GS + 9), ((K, 0), GS + 10), ((QR, 0), GS + 14),
                 ((QSW, 0), 2 * GS + 1)]
        for g in range(1, NG - 1):
            at = GS * (g + 1)
            ahead += [((K, g), at + 4), ((QN, g), at + 8), ((QR, g), at + 12), ((QSW, g), at + 15)]
        own += [((SP, g), GS * (g + 1) + 3 - (g == G3)) for g in range(NG)]
        ahead += [((V, 0), UNITS), ((V, 1), UNITS + 3), ((V, 2), UNITS + 5), ((V, 3), UNITS + 6)]
        own += [((O, t), UNITS + 7 + t) for t in range(NT)]
        order = sorted(own + ahead, key=lambda j: j[1])
        rounds = {
            "first": [(HT, k) for k in range(NK)] + [(LAT, 0), (KSW, 0)]
                     + [(m, g) for g in range(NG - 1) for m in (K, QN, QR, QSW)] + [(V, t) for t in range(NT)],
            "steady": [j for j, _ in order],
            "last": [j for j, _ in sorted(own, key=lambda j: j[1])],
        }
        ends = {j: s for j, s in order}
        STEPS = max(ends.values()) + 1
        split_kinds = (HT, LAT, K, QN, QR)
        turns = {"first": ["k"] + list(range(NG - 1)), "steady": [G3, "k"] + list(range(NG - 1)), "last": [G3]}
        turn_step = {r: ends[(KSW, 0) if r == "k" else (QSW, r)] + 4 for r in turns["steady"]}

        def before(kind, b, count=lambda j: True):
            n = {k: sum(count(j) for j in r) for k, r in rounds.items()}
            return 0 if kind == "first" else n["first"] + n["steady"] * b

        def upto(kind, b, job):
            return before(kind, b) + rounds[kind].index(job) + 1

        def split_upto(kind, b, job):
            is_split = lambda j: j[0] in split_kinds
            r = rounds[kind]
            return before(kind, b, is_split) + sum(is_split(j) for j in r[:r.index(job) + 1])

        def turns_upto(kind, b, r):
            first = 0 if kind == "first" else len(turns["first"]) + len(turns["steady"]) * b
            return first + turns[kind].index(r) + 1

        def bank_of(kind, job):
            return job_bank[rounds[kind].index(job) % RING]

        def ended(kind, step):
            return [j for j in rounds[kind] if ends[j] == step]

        def batch_of(kind, b, g):
            return 0 if kind == "first" else b if g == G3 else b + 1

        def reuse(eng, kind, b, g, stacked, each):
            of = batch_of(kind, b, g)
            if g > 0:
                eng.wait_ge(stacked[g - 1], of * each + each)
            elif kind != "first":
                eng.wait_ge(stacked[G3], of * each)

        loads = [(wa_hi[:], wa_lo[:], wkva.rearrange("(k p) n -> p k n", p=P), P, NK, R + DH),
                 (wb_hi[:], wb_lo[:], wkvb, R, 1, D),
                 (wq_hi[:, :, 0:D], wq_lo[:, :, 0:D], wq[:, 0:D].rearrange("(k p) n -> p k n", p=P), P, NK, D),
                 (wq_hi[:, :, D:2 * D], wq_lo[:, :, D:2 * D], wq[:, D:2 * D].rearrange("(k p) n -> p k n", p=P), P, NK, D),
                 (wo_hi[:], wo_lo[:], wo.rearrange("(g p) n -> p g n", p=P), P, NG, D)]

        def staged(n):
            _, _, src, rows, k, w = loads[n]
            a = stage[0:rows, n % 2, 0:k * w]
            return a.rearrange("p (k n) -> p k n", k=k) if len(src.shape) == 3 else a

        block = ctx.enter_context(nc.Block())

        @block.sync
        def _(sp):
            def rows(stack, row, g, src, stacked, key=False):
                if key:
                    sp.dma_start(stack[row * DH:(row + 1) * DH, g * HG:(g + 1) * HG, :],
                                 src[KR, :].unsqueeze(1).broadcast_to([DH, HG, S])).then_inc(stacked[g], 16)
                    return
                for hh in range(HG):
                    sp.dma_start(stack[row * DH:(row + 1) * DH, g * HG + hh, :], src[hh * DH:(hh + 1) * DH, :]).then_inc(stacked[g], 16)

            def stack(kind, b, g):
                if g == 0:
                    sp.wait_ge(rot_lo, turns_upto(kind, b, "k"))
                    sp.nop(nofuse=True)
                sp.wait_ge(left, upto(kind, b, (K, g)))
                for to, row, src in ((k_stack, 0, kn_hi), (k_stack, 2, kn_hi), (k_stack2, 0, kn_lo)):
                    rows(to, row, g, src, k_stacked)
                for to, row, src in ((k_stack, 1, kr_hi), (k_stack, 3, kr_hi), (k_stack2, 1, kr_lo)):
                    rows(to, row, g, src, k_stacked, key=True)
                sp.wait_ge(left, upto(kind, b, (QN, g)))
                rows(q_stack, 0, g, qn_hi, qn_stacked)
                rows(q_stack, 2, g, qn_lo, qn_stacked)
                sp.wait_ge(rot_lo, turns_upto(kind, b, g))
                rows(q_stack, 1, g, qr_hi, qr_stacked)
                rows(q_stack, 3, g, qr_lo, qr_stacked)

            def load(b):
                sp.dma_start(zn[:], x1[bass.ds(b * 1, 1), :, :].rearrange("a (t p) n -> p (a t) n", p=P)).then_inc(x_loaded, 16)

            def body(kind, b):
                if kind == "steady":
                    sp.wait_ge(moved, b * NT + NT)
                    load(b + 1)
                stack(kind, b, G3)
                for g in range(NG - 1 if kind == "steady" else 0):
                    stack(kind, b, g)
                for t in range(NT):
                    sp.wait_ge(left, upto(kind, b, (O, t)))
                    sp.dma_start(z1[bass.ds(b * 1, 1), t * P:(t + 1) * P, :].rearrange("a p n -> p (a n)"),
                                 zo[:, t % 2, :]).then_inc(z1_stored[t % 2], 16)

            load(0)
            for n, (_, _, src, *_) in enumerate(loads):
                if n >= 2:
                    sp.wait_ge(w_split, n - 1)
                sp.dma_start(staged(n), src).then_inc(w_loaded[n % 2], 16)
                if n == 0:
                    for dst, src in ((idn[:], ident), (swp[:], swap), (rot[:], cos_sin), (tri[:], causal), (wn[:], w_norm)):
                        sp.dma_start(dst, src).then_inc(const_loaded, 16)
            for g in range(NG - 1):
                stack("first", 0, g)
            with sp.Fori(0, B - 1) as b:
                body("steady", b)
            body("last", B - 1)
            for i in range(2):
                sp.wait_ge(z1_stored[i], 32 * (B + 1))
            sp.wait_ge(zeroed, 16 * (B + 1))

        @block.gpsimd
        def _(pool):
            for i in range(2):
                pool.sem_inc(z1_stored[i], 32)
            nc.gpsimd.memset(power[:], -0.5).then_inc(power_set, 1)
            nc.gpsimd.memset(zero[:], 0.0).then_inc(zero_set, 1)
            for s in used:
                pool.sem_clear(s)
            pool.wait_ge(power_set, 1)

            def norms(b):
                for t in range(NT):
                    s = [small[:, t, i:i + 1] for i in range(NS)]
                    var, done = mv[:, t, 1:2], (b * NT + t) * NS
                    pool.wait_ge(mv_done, b * NT + t + 1)
                    pool.nop(nofuse=True)
                    nc.gpsimd.tensor_scalar(s[0], var, EPS, None, ALU.add).then_inc(small_done, 1)
                    pool.wait_ge(small_done, done + 1)
                    nc.gpsimd.tensor_tensor(s[1], s[0], power[:], ALU.pow).then_inc(small_done, 1)
                    pool.wait_ge(small_done, done + 2)
                    nc.gpsimd.tensor_tensor(s[2], s[1], s[1], ALU.mult).then_inc(small_done, 1)
                    pool.wait_ge(small_done, done + 3)
                    nc.gpsimd.tensor_tensor(s[3], s[2], var, ALU.mult).then_inc(small_done, 1)
                    pool.wait_ge(small_done, done + 4)
                    pool.nop(nofuse=True)
                    nc.gpsimd.tensor_scalar(s[4], s[3], EPS, None, ALU.add).then_inc(small_done, 1)
                    pool.wait_ge(small_done, done + 5)
                    nc.gpsimd.tensor_tensor(s[5], s[4], power[:], ALU.pow).then_inc(small_done, 1)

            def rotate(kind, b, r):
                part, job, hi, lo = (KR, (KSW, 0), kr_hi, kr_lo) if r == "k" else (slice(0, P), (QSW, r), qr_hi, qr_lo)
                if r == "k":
                    if kind == "first":
                        pool.wait_ge(small_done, NT * NS)
                    else:
                        pool.wait_ge(o_lo_done, b * NG + 1)
                pool.wait_ge(left, upto(kind, b, job))
                nc.gpsimd.tensor_tensor(rc[part, :], rc[part, :], rs[part, :], ALU.add).then_inc(rot_sum, 1)
                pool.wait_ge(rot_hi, turns_upto(kind, b, r))
                nc.gpsimd.tensor_tensor(lo[part, :], rc[part, :], hi[part, :], ALU.subtract).then_inc(rot_lo, 1)
                if r == "k":
                    pool.wait_ge(rot_lo, turns_upto(kind, b, r))

            def move(b, prior=None):
                for t in range(NT):
                    pool.wait_ge(z_ready, b * NT + t + 1)
                    if prior is not None:
                        pool.wait_ge(left, upto("steady", prior, (O, t)))
                    pool.nop(nofuse=True)
                    nc.gpsimd.tensor_copy(zr[:, t, :], zn[:, t, :]).then_inc(moved, 1)

            def body(kind, b):
                more = kind == "steady"
                if more:
                    norms(b + 1)
                for step in range(STEPS + 6):
                    for r in turns[kind]:
                        if turn_step[r] == step:
                            rotate(kind, b, r)
                    g, off = divmod(step - GS, GS)
                    if 0 <= g < NG and off == 6:
                        pool.wait_ge(o_hi_done, b * NG + g + 1)
                        nc.gpsimd.tensor_tensor(o_lo[:, g, :], normal[:], o_hi[:, g, :], ALU.subtract).then_inc(o_lo_done, 1)
                if more:
                    pool.wait_ge(h_ready, (b + 1) * NT + NT)
                    move(b + 1, b)

            norms(0)
            for r in turns["first"]:
                rotate("first", 0, r)
            pool.wait_ge(h_ready, NT)
            move(0)
            with pool.Fori(0, B - 1) as b:
                body("steady", b)
            body("last", B - 1)

        @block.scalar
        def _(act):
            def high(kind, b, job):
                m, n = job
                if m not in split_kinds:
                    return
                act.wait_ge(job_done, upto(kind, b, job))
                src, scale = bank_of(kind, job)[:], 1.0 / WS
                if m == HT:
                    out, scale = ht_hi[:, n, :], wn[:, n:n + 1]
                elif m == LAT:
                    out, src = lat_hi[:], src[0:R + DH]
                elif m == K:
                    reuse(act, kind, b, n, k_stacked, STK_K)
                    out = kn_hi[:]
                elif m == QN:
                    reuse(act, kind, b, n, qn_stacked, STK_Q)
                    out, scale = qn_hi[:], scale_nope
                else:
                    out = qu_hi[:]
                nc.scalar.activation(out, src, ACT.Copy, scale=scale).then_inc(hi_done, 1)

            def rotated(kind, b, r):
                if r == "k":
                    if kind != "first":
                        act.wait_ge(k_stacked[G3], b * STK_K + STK_K)
                    out, src = kr_hi[KR, :], rc[KR, :]
                else:
                    reuse(act, kind, b, r, qr_stacked, STK_Q)
                    out, src = qr_hi[:], rc[:]
                act.wait_ge(rot_sum, turns_upto(kind, b, r))
                nc.scalar.activation(out, src, ACT.Copy).then_inc(rot_hi, 1)

            def scaled(b, t):
                act.wait_ge(small_done, (b * NT + t) * NS + NS)
                act.wait_ge(z_ready, b * NT + t + 1)
                nc.scalar.activation(hn[:, t, :], zn[:, t, :], ACT.Copy, scale=small[:, t, 5:6]).then_inc(h_ready, 1)

            def clear(b):
                act.wait_ge(zeroed, b * 16 + 16)
                act.dma_start(x_sorted[bass.ds(b * (NB // B * P), NB // B * P), :].rearrange("(t p) n -> p t n", p=P),
                              zero[:].unsqueeze(1).broadcast_to([P, NB // B, D])).then_inc(zeroed, 16)

            def body(kind, b):
                clear(b)
                for step in range(STEPS + 1):
                    if step < UNITS:
                        g, i, hh = unit_of(step)
                        w = (i + 1) * P
                        act.wait_ge(biased, b * UNITS + step + 1)
                        nc.scalar.activation(prob[:, step % 4, 0:w], prob[:, step % 4, 0:w], ACT.Exp, scale=-1.0,
                                             bias=low[:, step % 8:step % 8 + 1],
                                             accum_out=den[:, g % 2, i * HG + hh:i * HG + hh + 1]).then_inc(exped, 1)
                    n = step - 2
                    if 0 <= n < UNITS and n % 2 == 0:
                        if n >= 2 * HG:
                            act.wait_ge(summed, b * QUADS + n // HG - 1)
                        i = unit_of(n)[1]
                        act.wait_ge(turned_done, b * UNITS + n + 1)
                        nc.scalar.activation(turned[:, n // HG % 2, n % HG, 0:i + 1, :],
                                             turn_bank[n % 2][:, 0:(i + 1) * P].rearrange("p (j q) -> p j q", q=P),
                                             ACT.Copy).then_inc(kept_act, 1)
                    if kind == "steady" and step in (4, 5, 7, 9):
                        scaled(b + 1, (4, 5, 7, 9).index(step))
                    for job in ended(kind, step - 1):
                        high(kind, b, job)
                    for r in turns[kind]:
                        if turn_step[r] == step:
                            rotated(kind, b, r)
                    g, off = divmod(step - GS, GS)
                    if 0 <= g < NG and off == 6:
                        act.wait_ge(normed, b * NG + g + 1)
                        nc.scalar.activation(o_hi[:, g, :], normal[:], ACT.Copy).then_inc(o_hi_done, 1)

            def split(n):
                act.wait_ge(w_loaded[n % 2], 16 * (n // 2 + 1))
                nc.scalar.activation(loads[n][0], staged(n), ACT.Copy, scale=WS).then_inc(w_free, 1)

            act.sem_inc(zeroed, 16)
            act.wait_ge(zero_set, 1)
            split(0)
            split(1)
            act.wait_ge(const_loaded, 80)
            for t in range(NT):
                scaled(0, t)
            for job in rounds["first"]:
                if job == (LAT, 0):
                    for n in range(2, len(loads)):
                        split(n)
                high("first", 0, job)
                if job[0] == KSW or job[0] == QSW:
                    rotated("first", 0, "k" if job[0] == KSW else job[1])
            with act.Fori(0, B - 1) as b:
                body("steady", b)
            body("last", B - 1)

        @block.vector
        def _(dve):
            def leave(kind, b, job):
                m, n = job
                src, scale, r = bank_of(kind, job)[:], 1.0 / WS, turns[kind]
                if m in split_kinds:
                    dve.wait_ge(hi_done, split_upto(kind, b, job))
                    if m in (LAT, QR):
                        which = "k" if m == LAT else n
                        part, table = (KR, 2) if m == LAT else (slice(0, P), 0)
                        if kind != "first" or r.index(which):
                            dve.wait_ge(rot_lo, turns_upto(kind, b, which) - 1)
                        nc.vector.tensor_tensor(rc[part, :], src[part], rot[part, table, :], ALU.mult).then_inc(rot_cos, 1)
                    if m == HT:
                        hi, lo, scale = ht_hi[:, n, :], ht_lo[:, n, :], wn[:, n:n + 1]
                    elif m == LAT:
                        hi, lo, src = lat_hi[:], lat_lo[:], src[0:R + DH]
                    elif m == K:
                        hi, lo = kn_hi[:], kn_lo[:]
                    elif m == QN:
                        hi, lo, scale = qn_hi[:], qn_lo[:], scale_nope
                    else:
                        hi, lo = qu_hi[:], qu_lo[:]
                    nc.vector.scalar_tensor_tensor(out=lo, in0=src, scalar=scale, in1=hi, op0=ALU.mult,
                                                   op1=ALU.subtract).then_inc(left, 1)
                    return
                dve.wait_ge(job_done, upto(kind, b, job))
                if m == KSW or m == QSW:
                    part, table = (KR, 3) if m == KSW else (slice(0, P), 1)
                    dve.wait_ge(rot_cos, turns_upto(kind, b, "k" if m == KSW else n))
                    nc.vector.tensor_tensor(rs[part, :], src[part], rot[part, table, :], ALU.mult).then_inc(left, 1)
                elif m == V:
                    if kind != "first":
                        dve.wait_ge(summed, b * QUADS + QUADS)
                    nc.vector.tensor_scalar(v[:, n, :], src, 1.0 / WS, None, ALU.mult).then_inc(left, 1)
                elif m == SP:
                    if n:
                        dve.wait_ge(o_lo_done, b * NG + n)
                    nc.vector.tensor_copy(normal[:], src).then_inc(left, 1)
                else:
                    dve.wait_ge(z1_stored[n % 2], b * 32 + 32 + 16 * (n // 2))
                    dve.wait_ge(moved, b * NT + n + 1)
                    nc.vector.scalar_tensor_tensor(out=zo[:, n % 2, :], in0=src, scalar=1.0 / WS, in1=zr[:, n, :],
                                                   op0=ALU.mult, op1=ALU.add).then_inc(left, 1)

            def moments(b, t):
                dve.wait_ge(x_loaded, b * 16 + 16)
                nc.vector.bn_stats(stats[:, t, :], zn[:, t, :]).then_inc(stats_done, 1)
                dve.wait_ge(stats_done, b * NT + t + 1)
                dve.nop(nofuse=True)
                nc.vector.bn_aggr(mv[:, t, :], stats[:, t, :]).then_inc(mv_done, 1)

            def normalise(b, t):
                dve.wait_ge(mv_done, b * NT + t + 1)
                dve.wait_ge(small_done, (b * NT + t) * NS + 2)
                nc.vector.tensor_scalar(zn[:, t, :], zn[:, t, :], mv[:, t, 0:1], small[:, t, 1:2], ALU.subtract,
                                        ALU.mult).then_inc(z_ready, 1)

            def body(kind, b):
                for step in range(STEPS + 2):
                    if step < UNITS:
                        g, i, hh = unit_of(step)
                        w = (i + 1) * P
                        dve.wait_ge(scored, b * UNITS + step + 1)
                        if step >= 4:
                            dve.wait_ge(turned_done, b * UNITS + step - 3)
                        at = (NT - 1 - i) * P
                        dve.nop(nofuse=True)
                        nc.vector.tensor_tensor_reduce(out=prob[:, step % 4, 0:w], in0=score_bank[step % 2][:, 0:w],
                                                       in1=tri[:, at:at + w], scale=-1.0, scalar=3e38,
                                                       op0=ALU.add, op1=ALU.min,
                                                       accum_out=low[:, step % 8:step % 8 + 1]).then_inc(biased, 1)
                    n = step - 2
                    if 0 <= n < UNITS and n % 2 == 1:
                        i = unit_of(n)[1]
                        if n >= 2 * HG:
                            dve.wait_ge(summed, b * QUADS + n // HG - 1)
                        dve.wait_ge(turned_done, b * UNITS + n + 1)
                        nc.vector.tensor_copy(turned[:, n // HG % 2, n % HG, 0:i + 1, :],
                                              turn_bank[n % 2][:, 0:(i + 1) * P].rearrange("p (j q) -> p j q", q=P)
                                              ).then_inc(kept_dve, 1)
                    g, off = divmod(step - GS, GS)
                    if 0 <= g < NG and off == 1:
                        dve.wait_ge(exped, b * UNITS + (g + 1) * GS)
                        nc.vector.reciprocal(rden[:, g % 2, :], den[:, g % 2, :]).then_inc(recip_done, 1)
                    if 0 <= g < NG and off == 6:
                        dve.wait_ge(summed, b * QUADS + (g + 1) * NT)
                        dve.wait_ge(left, upto(kind, b, (SP, g)))
                        nc.vector.tensor_tensor(normal[:], out_bank[:], normal[:], ALU.mult).then_inc(normed, 1)
                    if kind == "steady" and step in (1, 3, 5, 7):
                        moments(b + 1, step // 2)
                    if kind == "steady" and step in (3, 5, 7, 8):
                        normalise(b + 1, (3, 5, 7, 8).index(step))
                    for job in ended(kind, step - 2):
                        leave(kind, b, job)

            def split(n):
                dve.wait_ge(w_free, n + 1)
                nc.vector.scalar_tensor_tensor(out=loads[n][1], in0=staged(n), scalar=WS, in1=loads[n][0], op0=ALU.mult,
                                               op1=ALU.subtract).then_inc(w_split, 1)

            for t in range(NT):
                moments(0, t)
            for t in range(NT):
                normalise(0, t)
            split(0)
            split(1)
            dve.wait_ge(const_loaded, 80)
            for job in rounds["first"]:
                if job == (LAT, 0):
                    for n in range(2, len(loads)):
                        split(n)
                leave("first", 0, job)
            with dve.Fori(0, B - 1) as b:
                body("steady", b)
            body("last", B - 1)

        @block.tensor
        def _(pe):
            mm = nc.tensor.matmul

            def free(kind, b, job):
                n = rounds[kind].index(job)
                if kind != "first" or n >= RING:
                    pe.wait_ge(left, before(kind, b) + (n - RING + 1 if n >= RING else 0))

            def chain(o, pairs, begins, ends_it):
                for n, ((lh, ll), (rh, rl)) in enumerate(pairs):
                    mm(o, lh, rh, start=(begins and n == 0), stop=False)
                    mm(o, lh, rl, start=False, stop=False)
                    last = mm(o, ll, rh, start=False, stop=(ends_it and n == len(pairs) - 1))
                return last

            def run(kind, b, job, parts=range(NK)):
                m, n = job
                o = bank_of(kind, job)
                parts = list(parts)
                if parts[0] == 0:
                    free(kind, b, job)
                if m == HT:
                    of = 0 if kind == "first" else b + 1
                    pe.wait_ge(h_ready, of * NT + NT)
                    for t in range(NT):
                        last = nc.tensor.transpose(o[:, t * P:(t + 1) * P], hn[:, t, n * P:(n + 1) * P], idn[:])
                elif m in (LAT, QN, QR):
                    if m == LAT and parts[0] == 0:
                        pe.wait_ge(left, upto(kind, b, (HT, NK - 1)))
                    c = slice(0, R + DH) if m == LAT else slice((2 * n + (m == QR)) * P, (2 * n + (m == QR) + 1) * P)
                    wh, wl = (wa_hi, wa_lo) if m == LAT else (wq_hi, wq_lo)
                    o = o[0:R + DH] if m == LAT else o[:]
                    last = chain(o, [((wh[:, k, c], wl[:, k, c]), (ht_hi[:, k, :], ht_lo[:, k, :])) for k in parts],
                                 parts[0] == 0, parts[-1] == NK - 1)
                elif m == KSW:
                    pe.wait_ge(left, upto(kind, b, (LAT, 0)))
                    pe.nop(nofuse=True)
                    mm(o[KR, :], swp[KR, R:R + DH], lat_hi[KR, :], start=True, stop=False, tile_position=(R, R))
                    last = mm(o[KR, :], swp[KR, R:R + DH], lat_lo[KR, :], start=False, stop=True, tile_position=(R, R))
                elif m == QSW:
                    pe.wait_ge(left, upto(kind, b, (QR, n)))
                    mm(o[:], swp[:], qu_hi[:], start=True, stop=False)
                    last = mm(o[:], swp[:], qu_lo[:], start=False, stop=True)
                elif m == K:
                    c = slice(n * P, (n + 1) * P)
                    last = chain(o[:], [((wb_hi[:, c], wb_lo[:, c]), (lat_hi[0:R, :], lat_lo[0:R, :]))], True, True)
                elif m == V:
                    c = slice(n * P, (n + 1) * P)
                    last = chain(o[:], [((lat_hi[0:R, c], lat_lo[0:R, c]), (wb_hi[:], wb_lo[:]))], True, True)
                elif m == SP:
                    pe.wait_ge(recip_done, b * NG + n + 1)
                    for t in range(NT):
                        for hh in range(HG):
                            c = t * HG + hh
                            last = mm(o[hh * DH:(hh + 1) * DH, t * P:(t + 1) * P],
                                      rden[:, n % 2, c:c + 1].broadcast_to([P, DH]), idn[:], start=True, stop=True,
                                      tile_position=(0, hh * DH))
                else:
                    if n == 0:
                        pe.wait_ge(o_lo_done, b * NG + NG)
                    c = slice(n * P, (n + 1) * P)
                    last = chain(o[:], [((o_hi[:, k, c], o_lo[:, k, c]), (wo_hi[:, k, :], wo_lo[:, k, :])) for k in range(NK)],
                                 True, True)
                if m not in (LAT, QN, QR) or parts[-1] == NK - 1:
                    last.then_inc(job_done, 1)

            def fill(kind, b, step):
                for job in rounds[kind]:
                    end = ends[job]
                    if job[0] in (LAT, QN, QR):
                        if end - NK < step <= end:
                            run(kind, b, job, [step - end + NK - 1])
                    elif step == end:
                        run(kind, b, job)

            def body(kind, b):
                for step in range(STEPS + 1):
                    if step < UNITS:
                        g, i, hh = unit_of(step)
                        if step % GS == 0:
                            pe.wait_ge(k_stacked[g], b * STK_K + STK_K)
                            pe.wait_ge(qn_stacked[g], b * STK_Q + STK_Q)
                            pe.wait_ge(qr_stacked[g], b * STK_Q + STK_Q)
                        if step >= 2:
                            pe.wait_ge(biased, b * UNITS + step - 1)
                        h, w, c = g * HG + hh, (i + 1) * P, slice(i * P, (i + 1) * P)
                        mm(score_bank[step % 2][:, 0:w], q_stack[:, h, c], k_stack[:, h, 0:w], start=True, stop=False)
                        mm(score_bank[step % 2][:, 0:w], q_stack[0:2 * DH, h, c], k_stack2[:, h, 0:w], start=False,
                           stop=True).then_inc(scored, 1)
                    fill(kind, b, step)
                    n = step - 2
                    if 0 <= n < UNITS:
                        pe.wait_ge(exped, b * UNITS + n + 1)
                        if n >= 2:
                            pe.wait_ge((kept_act, kept_dve)[n % 2], b * (UNITS // 2) + (n - 2) // 2 + 1)
                        for j in range(unit_of(n)[1] + 1):
                            last = nc.tensor.transpose(turn_bank[n % 2][:, j * P:(j + 1) * P],
                                                       prob[:, n % 4, j * P:(j + 1) * P], idn[:])
                        last.then_inc(turned_done, 1)
                    m = step - TAIL
                    if m >= 0 and m % HG == HG - 1 and m < UNITS:
                        quad = m // HG
                        g, i = divmod(quad, NT)
                        pe.wait_ge(kept_act, b * (UNITS // 2) + (quad + 1) * HG // 2)
                        pe.wait_ge(kept_dve, b * (UNITS // 2) + (quad + 1) * HG // 2)
                        if quad == 0:
                            pe.wait_ge(left, before(kind, b))
                        if i == 0 and g > 0:
                            pe.wait_ge(normed, b * NG + g)
                        for j in range(i + 1):
                            for hh in range(HG):
                                c = (g * HG + hh) * DH
                                last = mm(out_bank[hh * DH:(hh + 1) * DH, i * P:(i + 1) * P], v[:, j, c:c + DH],
                                          turned[:, quad % 2, hh, j, :], start=(j == 0), stop=(j == i),
                                          tile_position=(0, hh * DH))
                        last.then_inc(summed, 1)

            pe.wait_ge(const_loaded, 80)
            for job in rounds["first"]:
                if job == (LAT, 0):
                    pe.wait_ge(w_split, len(loads))
                run("first", 0, job)
            with pe.Fori(0, B - 1) as b:
                body("steady", b)
            body("last", B - 1)


class Count:

    def __init__(self, turn, c, size):
        self.turn, self.c, self.size = turn, c, size
        self.n = c if isinstance(turn, int) else turn * size + c
        self.slot = c % size
        self.use = c // size if isinstance(turn, int) else turn + c // size

    def back(self, steps):
        return Count(self.turn, self.c - steps, self.size)

    def within(self, low, high):
        return isinstance(self.turn, int) and low <= self.c <= high


def pass_c(nc, x1, z1, g_gate, w_norm, w_route, b_route, wg, wu, wd, swg, swu, swd, ident, earlier, starts, before_e,
           xn_rows, x_sorted, y_sorted, base_rows, out):
    with ExitStack() as ctx:
        def sb(name, shape, dt=F32):
            return ctx.enter_context(nc.sbuf_tensor("c_" + name, shape, dt))

        def sem(name):
            return ctx.enter_context(nc.semaphore("c_" + name))

        bank = [ctx.enter_context(nc.psum_tensor(f"c_bank{i}", [P, 512], F32)) for i in range(8)]
        turn_bank, up_bank, hid_bank, down_bank = bank[0:2], bank[2:4], bank[4:6], bank[6:8]
        X = E + 1

        gu_hi = sb("gu_hi", [P, X * NK, 2 * I], F16)
        gu_lo = sb("gu_lo", [P, X * NK, 2 * I], F16)
        d_hi = sb("d_hi", [P, X * NI, D], F16)
        d_lo = sb("d_lo", [P, X * NI, D], F16)
        r_hi = sb("r_hi", [P, NK, E], F16)
        r_lo = sb("r_lo", [P, NK, E], F16)
        stage = sb("stage", [P, 3, NK * I])
        r_stage = sb("r_stage", [P, NK, E])
        wn = sb("wn", [P, D])
        idn = sb("idn", [P, P])
        before_p = sb("before_p", [P, P], F16)
        ones = sb("ones", [P, P], F16)
        before_x = sb("before_x", [P, E, E])
        start_row = sb("start_row", [P, NB])
        br = sb("br", [P, E])
        gate = sb("gate", [P, 2])
        z = sb("z", [P, 2, NT, D])
        xn = sb("xn", [P, 2, NT, D])
        zf, xf = z[:].rearrange("p a t n -> p (a t) n"), xn[:].rearrange("p a t n -> p (a t) n")
        x_in, z_in, x1_in, y_out = zf[:, 0:4], zf[:, 4:8], xf[:, 0:4], xf[:, 4:8]
        y_first, y_second, sums = zf[:, 0:4], zf[:, 4:8], xf[:, 0:4]
        xt_hi = sb("xt_hi", [P, 2, NK, P], F16)
        xt_lo = sb("xt_lo", [P, 2, NK, P], F16)
        th = sb("th", [P, 2, I])
        hid = sb("hid", [P, 2, I])
        h_hi = sb("h_hi", [P, 2, NI, P], F16)
        h_lo = sb("h_lo", [P, 2, NI, P], F16)
        stats = sb("stats", [P, NT, 6])
        mv = sb("mv", [P, NT, 2])
        small = sb("small", [P, 4, NT])
        power = sb("power", [P, NT])
        logit = sb("logit", [P, NT, E])
        top = sb("top", [P, NT, E])
        two = sb("two", [P, NT, E])
        rest = sb("rest", [P, NT, E])
        sel = sb("sel", [P, NT, E])
        ex = sb("ex", [P, NT, E])
        tot = sb("tot", [P, 2, NT])
        share = sb("share", [P, TT, E])
        chosen = sb("chosen", [P, TT, E], F16)
        count = sb("count", [P, E])
        count_i = sb("count_i", [P, 2, E], I32)
        padded = sb("padded", [P, E])
        lesser = sb("lesser", [P, E, E])
        start = sb("start", [P, 2, E])
        row = sb("row", [P, TT, E])
        place = sb("place", [P, 4, TT])
        place_i = sb("place_i", [P, TT, 2], I32)
        hit = sb("hit", [P, TT, E])
        weight = sb("weight", [P, 2, TT])
        started = sb("started", [P, NB, E])
        block_x = sb("block_x", [P, NB])
        block_i = sb("block_i", [P, NB], I32)
        index = sb("index", [P, 4, 2], I32)

        w_loaded = [sem(f"w_loaded{i}") for i in range(3)]
        w_hi_done, w_split, r_loaded, r_split, const_loaded, const_set, gate_ready, two_set = (
            sem("w_hi_done"), sem("w_split"), sem("r_loaded"), sem("r_split"), sem("const_loaded"), sem("const_set"),
            sem("gate_ready"), sem("two_set"))
        z_loaded = [sem(f"z_loaded{i}") for i in range(2)]
        xn_stored = [sem(f"xn_stored{i}") for i in range(2)]
        stats_done, mv_done, small_done, x_ready = sem("stats_done"), sem("mv_done"), sem("small_done"), sem("x_ready")
        routed, expd, ranked, table_ready = sem("routed"), sem("expd"), sem("ranked"), sem("table_ready")
        counted = sem("counted")
        rows_loaded, x1_loaded, z1_loaded, y_stored, scattered = (
            [sem(f"{n}{i}") for i in range(4)] for n in ("rows_loaded", "x1_loaded", "z1_loaded", "y_stored", "scattered"))
        turned, split_hi, split_lo, multiplied_up = sem("turned"), sem("split_hi"), sem("split_lo"), sem("multiplied_up")
        tanhed, half_done, hidden, hid_turned, h_hi_done, h_lo_done, downed, summed, y_ready = (
            sem("tanhed"), sem("half_done"), sem("hidden"), sem("hid_turned"), sem("h_hi_done"), sem("h_lo_done"), sem("downed"),
            sem("summed"), sem("y_ready"))
        base_ready = sem("base_ready")
        index_ready = sem("index_ready")
        gathered, out_stored = ([sem(f"{n}{i}") for i in range(4)] for n in ("gathered", "out_stored"))
        first_added, added = sem("first_added"), sem("added")

        NSM = 4
        AHEAD = 4
        DOWN = HS / (2.0 * WS * WS)
        RT = 2 * NT + 9
        z_rows = z1.rearrange("b (t p) n -> (b t) p n", p=P)
        x1_rows = x1.rearrange("b (t p) n -> (b t) p n", p=P)
        out_rows = out.rearrange("b (t p) n -> (b t) p n", p=P)
        xn_tiles = xn_rows.rearrange("(t p) n -> t p n", p=P)
        base_tiles = base_rows.rearrange("(t p) n -> t p n", p=P)
        xs_tiles = x_sorted.rearrange("(t p) n -> t p n", p=P)
        ys_tiles = y_sorted.rearrange("(t p) n -> t p n", p=P)

        def tile(rows, j):
            return rows[bass.ds(j * 1, 1), :, :].rearrange("a p n -> p (a n)")

        SHARED, ROUTED = ("shared", TT, 0), ("routed", NB, TT)

        def over(eng, steps, call):
            call(Count(0, 0, 4))
            with eng.Fori(0, (steps - 4) // 4) as i:
                for u in range(4):
                    call(Count(i, 1 + u, 4))
            for j in range(steps - 3, steps + 1):
                call(Count(0, j, 4))

        def split_views(e, part):
            if part == 2:
                return (d_hi[:, bass.ds(e * NI, NI), :], d_lo[:, bass.ds(e * NI, NI), :],
                        stage[:, 2].rearrange("p (k n) -> p k n", k=NI))
            c = slice(part * I, (part + 1) * I)
            return (gu_hi[:, bass.ds(e * NK, NK), c], gu_lo[:, bass.ds(e * NK, NK), c],
                    stage[:, part].rearrange("p (k n) -> p k n", k=NK))

        def batches(eng, call):
            call(Count(0, 0, 2))
            with eng.Fori(0, (B - 2) // 2) as i:
                for u in range(2):
                    call(Count(i, 1 + u, 2))
            call(Count(0, B - 1, 2))
            call(Count(0, B, 2))

        block = ctx.enter_context(nc.Block())

        @block.sync
        def _(sp):
            for i in range(4):
                sp.sem_inc(y_stored[i], 16)
                sp.sem_inc(out_stored[i], 16)
            for i in range(2):
                sp.sem_inc(xn_stored[i], 16)

            def weights(e, sources, first=False):
                for part in range(3):
                    if not first:
                        sp.wait_ge(w_split, e * 3 + (part - 2))
                    sp.dma_start(split_views(0, part)[2], sources[part]).then_inc(w_loaded[part], 16)

            def prepare(at):
                b, u = at.n, at.slot
                if at.within(B, B):
                    return
                if not at.within(0, 1):
                    sp.wait_ge(x_ready, b * NT - NT)
                sp.dma_start(z[:, u], z1[bass.ds(b * 1, 1), :, :].rearrange("a (t p) n -> p (a t) n", p=P)).then_inc(z_loaded[u], 16)
                weights(b + 1, [wg[bass.ds(b * 1, 1)].rearrange("a (k p) n -> p (a k) n", p=P),
                                wu[bass.ds(b * 1, 1)].rearrange("a (k p) n -> p (a k) n", p=P),
                                wd[bass.ds(b * 1, 1)].rearrange("a (k p) n -> p (a k) n", p=P)])
                sp.wait_ge(x_ready, b * NT + NT)
                sp.dma_start(xn_rows[bass.ds(b * S, S), :].rearrange("(t p) n -> p t n", p=P), xn[:, u]).then_inc(xn_stored[u], 16)

            for dst, src in ((idn[:], ident), (wn[:], w_norm.rearrange("(a n) -> a n", a=1).broadcast_to([P, D])),
                             (br[:], b_route.rearrange("(a n) -> a n", a=1).broadcast_to([P, E])),
                             (gate[:, 0:1], g_gate.rearrange("(a n) -> a n", a=1).broadcast_to([P, 1])),
                             (before_p[:], earlier), (start_row[:], starts), (before_x[:], before_e)):
                sp.dma_start(dst, src).then_inc(const_loaded, 16)
            sp.dma_start(r_stage[:], w_route.rearrange("(k p) n -> p k n", p=P)).then_inc(r_loaded, 16)
            weights(0, [swg[0].rearrange("(k p) n -> p k n", p=P), swu[0].rearrange("(k p) n -> p k n", p=P),
                        swd[0].rearrange("(k p) n -> p k n", p=P)], first=True)
            batches(sp, prepare)

            for i in range(2):
                sp.wait_ge(xn_stored[i], 16 + 16 * (B // 2))
            sp.wait_ge(turned, AHEAD + TT)

            def blocks(kind):
                name, n, base = kind
                ready = base_ready if name == "shared" else y_ready

                def load(at):
                    j, u = at.n, at.slot
                    if name == "routed" or not at.within(0, 3):
                        sp.wait_ge(turned, j + (AHEAD + TT + base - 3))
                        sp.nop(nofuse=True)
                    if name == "shared":
                        if not at.within(0, 3):
                            sp.wait_ge(scattered[u], at.use * 32)
                            sp.nop(nofuse=True)
                            sp.wait_ge(base_ready, j + (AHEAD - 3))
                            sp.nop(nofuse=True)
                        sp.dma_start(x_in[:, u], tile(xn_tiles, j)).then_inc(rows_loaded[u], 16)
                        sp.dma_start(z_in[:, u], tile(z_rows, j)).then_inc(z1_loaded[u], 16)
                        sp.dma_start(x1_in[:, u], tile(x1_rows, j)).then_inc(x1_loaded[u], 16)
                    else:
                        sp.dma_start(x_in[:, u], tile(xs_tiles, j)).then_inc(rows_loaded[u], 16)

                def store(at):
                    sp.wait_ge(ready, at.n + (AHEAD + 1))
                    sp.dma_start(tile(base_tiles if name == "shared" else ys_tiles, at.n), y_out[:, at.slot]
                                 ).then_inc(y_stored[at.slot], 16)

                for j in range(4):
                    load(Count(0, j, 4))
                with sp.Fori(0, (n - 4) // 4) as i:
                    for u in range(4):
                        load(Count(i, 4 + u, 4))
                        store(Count(i, u, 4))
                for j in range(n - 4, n):
                    store(Count(0, j, 4))

            blocks(SHARED)
            for i in range(4):
                sp.wait_ge(scattered[i], 32 * (TT // 4))
            blocks(ROUTED)

            for i in range(4):
                sp.wait_ge(y_stored[i], 16 + 16 * ((TT + NB) // 4))
            with sp.Fori(0, TT // 4) as i:
                for u in range(4):
                    sp.wait_ge(out_stored[u], i * 16 + 16)
                    sp.dma_start(sums[:, u], tile(base_tiles, i * 4 + u)).then_inc(x1_loaded[u], 16)
            for i in range(4):
                sp.wait_ge(out_stored[i], 16 + 16 * (TT // 4))

        @block.gpsimd
        def _(pool):
            nc.gpsimd.memset(ones[:], 1.0).then_inc(const_set, 1)
            nc.gpsimd.memset(power[:], -0.5).then_inc(const_set, 1)
            pool.wait_ge(const_set, 2)
            with pool.Fori(0, B) as b:
                pool.wait_ge(mv_done, b * NT + NT)
                nc.gpsimd.tensor_tensor(small[:, 0, :], mv[:, :, 0], mv[:, :, 0], ALU.mult).then_inc(small_done, 1)
                pool.wait_ge(small_done, b * NSM + 1)
                nc.gpsimd.tensor_tensor(small[:, 1, :], small[:, 0, :], mv[:, :, 1], ALU.add).then_inc(small_done, 1)
                pool.wait_ge(small_done, b * NSM + 2)
                pool.nop(nofuse=True)
                nc.gpsimd.tensor_scalar(small[:, 2, :], small[:, 1, :], EPS, None, ALU.add).then_inc(small_done, 1)
                pool.wait_ge(small_done, b * NSM + 3)
                nc.gpsimd.tensor_tensor(small[:, 3, :], small[:, 2, :], power[:], ALU.pow).then_inc(small_done, 1)
            pool.wait_ge(table_ready, 1)
            with pool.Fori(0, TT // 4) as i:
                for u in range(4):
                    pool.wait_ge(rows_loaded[u], i * 16 + 16)
                    pool.nop(nofuse=True)
                    nc.gpsimd.tensor_copy(index[:, u, :], place_i[:, bass.ds(i * 4 + u, 1), :].rearrange("p a n -> p (a n)")
                                          ).then_inc(index_ready, 1)
                    pool.wait_ge(index_ready, i * 4 + (u + 1))
                    pool.nop(nofuse=True)
                    for c in range(2):
                        pool.indirect_dma_start(x_sorted, bass.IndirectOffsetOnAxis(index[:, u, c:c + 1], 0), x_in[:, u], None
                                                ).then_inc(scattered[u], 16)
            for i in range(4):
                pool.wait_ge(y_stored[i], 16 + 16 * ((TT + NB) // 4))
            with pool.Fori(0, TT // 4) as i:
                for u in range(4):
                    pool.wait_ge(added, i * 4 + (u + 1))
                    pool.nop(nofuse=True)
                    nc.gpsimd.tensor_copy(index[:, u, :], place_i[:, bass.ds(i * 4 + u, 1), :].rearrange("p a n -> p (a n)")
                                          ).then_inc(index_ready, 1)
                    pool.wait_ge(index_ready, i * 4 + (TT + u + 1))
                    pool.nop(nofuse=True)
                    for c, rows in enumerate((y_first, y_second)):
                        pool.indirect_dma_start(rows[:, u], None, y_sorted, bass.IndirectOffsetOnAxis(index[:, u, c:c + 1], 0)
                                                ).then_inc(gathered[u], 16)

        @block.scalar
        def _(act):
            act.sem_inc(split_hi, AHEAD)
            act.sem_inc(h_hi_done, AHEAD)
            act.sem_inc(y_ready, AHEAD)

            def high(j, u, base):
                act.wait_ge(turned, j + (AHEAD + base + 1))
                act.wait_ge(multiplied_up, j + (AHEAD + base - 1))
                nc.scalar.activation(xt_hi[:, u % 2].rearrange("p k q -> p (k q)"), turn_bank[u % 2][:], ACT.Copy).then_inc(split_hi, 1)

            def weights(e):
                for part in range(3):
                    hi, _, src = split_views(e, part)
                    act.wait_ge(w_loaded[part], e * 16 + 16)
                    nc.scalar.activation(hi, src, ACT.Copy, scale=WS).then_inc(w_hi_done, 1)

            act.wait_ge(const_loaded, 16 * 7)
            nc.scalar.activation(gate[:, 1:2], gate[:, 0:1], ACT.Tanh).then_inc(gate_ready, 1)
            act.wait_ge(r_loaded, 16)
            nc.scalar.activation(r_hi[:], r_stage[:], ACT.Copy, scale=WS).then_inc(w_hi_done, 1)
            weights(0)

            def batch(at):
                b = at.n
                if not at.within(0, 0):
                    for t in range(NT):
                        high(b * NT + (t - NT), t, 0)
                    act.wait_ge(routed, b * RT - 5)
                    nc.scalar.activation(ex[:], ex[:], ACT.Exp).then_inc(expd, 1)
                if not at.within(B, B):
                    weights(b + 1)

            batches(act, batch)

            for name, n, base in (SHARED, ROUTED):
                def step(at):
                    j, u, before = at.n, at.slot, at.back(1)
                    if at.within(0, 0):
                        high(0, 0, base + TT)
                    if not at.within(n - 1, n):
                        high(j + 1, u + 1, base + TT)
                    if not at.within(0, 0):
                        act.wait_ge(hid_turned, j + (AHEAD + base))
                        act.wait_ge(downed, j + (AHEAD + base - 2))
                        nc.scalar.activation(h_hi[:, (u + 1) % 2].rearrange("p i q -> p (i q)"), hid_bank[(u + 1) % 2][:, 0:I],
                                             ACT.Copy).then_inc(h_hi_done, 1)
                    if not at.within(n, n):
                        act.wait_ge(multiplied_up, j + (AHEAD + base + TT + 1))
                        act.wait_ge(half_done, j + (AHEAD + base - 1))
                        nc.scalar.activation(th[:, u % 2], up_bank[u % 2][:, 0:I], ACT.Tanh, scale=0.5 / WS).then_inc(tanhed, 1)
                    if name == "routed" and not at.within(0, 0):
                        act.wait_ge(downed, j + (AHEAD + base))
                        act.wait_ge(y_stored[before.slot], before.use * 16 + (16 + 4 * base))
                        nc.scalar.activation(y_out[:, before.slot], down_bank[(u + 1) % 2][:], ACT.Copy).then_inc(y_ready, 1)
                over(act, n, step)

            with act.Fori(0, TT // 4) as i:
                for u in range(4):
                    act.wait_ge(added, i * 4 + (AHEAD + u + 1))
                    act.dma_start(tile(out_rows, i * 4 + u), sums[:, u]).then_inc(out_stored[u], 16)

        @block.vector
        def _(dve):
            dve.sem_inc(split_lo, AHEAD)
            dve.sem_inc(half_done, AHEAD)
            dve.sem_inc(hidden, AHEAD)
            dve.sem_inc(h_lo_done, AHEAD)
            dve.sem_inc(base_ready, AHEAD)
            dve.sem_inc(added, AHEAD)
            nc.vector.memset(two[:], -3e38).then_inc(two_set, 1)

            def low(j, u, base):
                dve.wait_ge(split_hi, j + (AHEAD + base + 1))
                nc.vector.tensor_tensor(xt_lo[:, u % 2].rearrange("p k q -> p (k q)"), turn_bank[u % 2][:],
                                        xt_hi[:, u % 2].rearrange("p k q -> p (k q)"), ALU.subtract).then_inc(split_lo, 1)

            def weights(e):
                for part in range(3):
                    hi, lo, src = split_views(e, part)
                    dve.wait_ge(w_hi_done, e * 3 + (2 + part))
                    nc.vector.scalar_tensor_tensor(out=lo, in0=src, scalar=WS, in1=hi, op0=ALU.mult, op1=ALU.subtract
                                                   ).then_inc(w_split, 1)

            def moments(at):
                b, u = at.n, at.slot
                dve.wait_ge(z_loaded[u], at.use * 16 + 16)
                for t in range(NT):
                    nc.vector.bn_stats(stats[:, t, :], z[:, u, t, :]).then_inc(stats_done, 1)
                for t in range(NT):
                    dve.wait_ge(stats_done, b * NT + (t + 1))
                    dve.nop(nofuse=True)
                    nc.vector.bn_aggr(mv[:, t, :], stats[:, t, :]).then_inc(mv_done, 1)

            def route(b):
                step = [0]

                def did(call):
                    call.then_inc(routed, 1)
                    step[0] += 1

                def after():
                    dve.wait_ge(routed, b * RT + step[0])
                    dve.nop(nofuse=True)

                def tiles(a):
                    return a[:, bass.ds(b * NT, NT), :]

                dve.wait_ge(multiplied_up, b * NT + (AHEAD + NT))
                did(nc.vector.scalar_tensor_tensor(out=logit[:], in0=down_bank[0][:, 0:NT * E].rearrange("p (t e) -> p t e", e=E),
                                                   scalar=1.0 / WS, in1=br[:].unsqueeze(1).broadcast_to([P, NT, E]),
                                                   op0=ALU.mult, op1=ALU.add))
                after()
                for t in range(NT):
                    did(nc.vector.max(out=top[:, t, :], in_=logit[:, t, :]))
                after()
                did(nc.vector.tensor_copy(two[:, :, 0:2], top[:, :, 0:2]))
                after()
                for t in range(NT):
                    did(nc.vector.match_replace(out=rest[:, t, :], in_to_replace=two[:, t, :], in_values=logit[:, t, :],
                                                imm_value=-1e38))
                did(nc.vector.tensor_tensor(ex[:], logit[:], top[:, :, 0:1].broadcast_to([P, NT, E]), ALU.subtract))
                after()
                did(nc.vector.tensor_tensor(sel[:], rest[:], logit[:], ALU.not_equal))
                assert step[0] == RT - 5, step[0]
                after()
                did(nc.vector.tensor_copy(tiles(chosen), sel[:]))
                dve.wait_ge(expd, b * 1 + 1)
                did(nc.vector.tensor_tensor(ex[:], ex[:], sel[:], ALU.mult))
                after()
                did(nc.vector.tensor_reduce(tot[:, 0, :], ex[:], AX_X, ALU.add))
                after()
                did(nc.vector.reciprocal(tot[:, 1, :], tot[:, 0, :]))
                after()
                did(nc.vector.tensor_tensor(tiles(share), ex[:], tot[:, 1, :].unsqueeze(2).broadcast_to([P, NT, E]), ALU.mult))
                assert step[0] == RT, step[0]

            dve.wait_ge(const_loaded, 16 * 7)
            dve.wait_ge(gate_ready, 1)
            dve.wait_ge(two_set, 1)
            dve.wait_ge(w_hi_done, 1)
            nc.vector.scalar_tensor_tensor(out=r_lo[:], in0=r_stage[:], scalar=WS, in1=r_hi[:], op0=ALU.mult,
                                           op1=ALU.subtract).then_inc(r_split, 1)
            weights(0)

            def batch(at):
                b, u, last = at.n, at.slot, at.within(B, B)
                if not last:
                    moments(at)
                if not at.within(0, 0):
                    for t in range(NT):
                        low(b * NT + (t - NT), t, 0)
                if not last:
                    dve.wait_ge(small_done, b * NSM + NSM)
                    if not at.within(0, 1):
                        dve.wait_ge(xn_stored[u], at.use * 16 + 16)
                        dve.wait_ge(turned, b * NT + (AHEAD - NT))
                        dve.nop(nofuse=True)
                    for t in range(NT):
                        nc.vector.scalar_tensor_tensor(out=xn[:, u, t, :], in0=z[:, u, t, :], scalar=small[:, 3, t:t + 1],
                                                       in1=wn[:], op0=ALU.mult, op1=ALU.mult).then_inc(x_ready, 1)
                if not at.within(0, 0):
                    route(at.back(1).n)
                if not last:
                    weights(b + 1)

            batches(dve, batch)

            done = [0]

            def rank(call):
                call.then_inc(ranked, 1)
                done[0] += 1

            def after():
                dve.wait_ge(ranked, done[0])

            def all_tokens(a):
                return a.unsqueeze(2).broadcast_to([P, TT, E])

            v = nc.vector
            dve.wait_ge(counted, 1)
            rank(v.tensor_reduce(count[:], hid_bank[1][:, 0:TT * E].rearrange("p (t e) -> p e t", e=E), AX_X, ALU.add))
            after()
            rank(v.tensor_scalar(count_i[:, 0], count[:], float(P - 1), None, ALU.add))
            after()
            rank(v.tensor_scalar(count_i[:, 1], count_i[:, 0], SHIFT, SHIFT, ALU.logical_shift_right, ALU.logical_shift_left))
            after()
            rank(v.tensor_copy(padded[:], count_i[:, 1]))
            after()
            rank(v.tensor_tensor(lesser[:], before_x[:], padded[:].unsqueeze(1).broadcast_to([P, E, E]), ALU.mult))
            after()
            rank(v.tensor_reduce(start[:, 0], lesser[:], AX_X, ALU.add))
            after()
            rank(v.tensor_tensor(start[:, 1], start[:, 0], padded[:], ALU.add))
            rank(v.scalar_tensor_tensor(out=row[:], in0=hid_bank[0][:, 0:TT * E].rearrange("p (t e) -> p t e", e=E), scalar=1.0,
                                        in1=start[:, 0].unsqueeze(1).broadcast_to([P, TT, E]), op0=ALU.add, op1=ALU.add))
            after()
            rank(v.tensor_tensor(row[:], row[:], chosen[:], ALU.mult))
            after()
            rank(v.tensor_reduce(place[:, 0], row[:], AX_X, ALU.max))
            rank(v.tensor_reduce(place[:, 1], row[:], AX_X, ALU.add))
            after()
            rank(v.tensor_tensor(place[:, 2], place[:, 1], place[:, 0], ALU.subtract))
            rank(v.tensor_scalar(place_i[:, :, 0], place[:, 0], -1.0, 0.0, ALU.add, ALU.max))
            after()
            rank(v.tensor_scalar(place_i[:, :, 1], place[:, 2], -1.0, 0.0, ALU.add, ALU.max))
            rank(v.tensor_tensor(started[:], start_row[:].unsqueeze(2).broadcast_to([P, NB, E]),
                                 start[:, 1].unsqueeze(1).broadcast_to([P, NB, E]), ALU.is_ge))
            after()
            rank(v.tensor_reduce(block_x[:], started[:], AX_X, ALU.add))
            after()
            rank(v.tensor_scalar(block_i[:], block_x[:], float(E - 1), None, ALU.min))
            after()
            dve.sem_inc(table_ready, 1)
            rank(v.tensor_tensor(hit[:], row[:], all_tokens(place[:, 0]), ALU.is_equal))
            after()
            rank(v.tensor_tensor(hit[:], hit[:], share[:], ALU.mult))
            after()
            rank(v.tensor_reduce(place[:, 0], hit[:], AX_X, ALU.add))
            rank(v.tensor_tensor(row[:], share[:], hit[:], ALU.subtract))
            after()
            rank(v.tensor_reduce(place[:, 1], row[:], AX_X, ALU.add))
            after()
            rank(v.tensor_scalar(weight[:], place[:, 0:2], gate[:, 1:2], 1.0 / (WS * HS), ALU.mult, ALU.mult))

            for name, n, base in (SHARED, ROUTED):
                def step(at):
                    j, u, before = at.n, at.slot, at.back(1)
                    if at.within(0, 0):
                        low(0, 0, base + TT)
                    if not at.within(n - 1, n):
                        low(j + 1, u + 1, base + TT)
                    if not at.within(0, 0):
                        w = (u + 1) % 2
                        dve.wait_ge(h_hi_done, j + (AHEAD + base))
                        nc.vector.tensor_tensor(h_lo[:, w].rearrange("p i q -> p (i q)"), hid_bank[w][:, 0:I],
                                                h_hi[:, w].rearrange("p i q -> p (i q)"), ALU.subtract).then_inc(h_lo_done, 1)
                    if not at.within(n, n):
                        w = u % 2
                        dve.wait_ge(tanhed, j + (base + 1))
                        dve.wait_ge(hid_turned, j + (AHEAD + base - 1))
                        nc.vector.scalar_tensor_tensor(out=hid[:, w], in0=th[:, w], scalar=1.0, in1=up_bank[w][:, 0:I],
                                                       op0=ALU.add, op1=ALU.mult).then_inc(half_done, 1)
                        dve.wait_ge(half_done, j + (AHEAD + base + 1))
                        nc.vector.scalar_tensor_tensor(out=hid[:, w], in0=hid[:, w], scalar=DOWN, in1=up_bank[w][:, I:2 * I],
                                                       op0=ALU.mult, op1=ALU.mult).then_inc(hidden, 1)
                    if name == "shared" and not at.within(0, 0):
                        w = before.slot
                        dve.wait_ge(downed, j + (AHEAD + base))
                        dve.wait_ge(z1_loaded[w], before.use * 16 + 16)
                        nc.vector.scalar_tensor_tensor(out=z_in[:, w], in0=down_bank[(u + 1) % 2][:], scalar=1.0 / (WS * HS),
                                                       in1=z_in[:, w], op0=ALU.mult, op1=ALU.add).then_inc(summed, 1)
                        dve.wait_ge(x1_loaded[w], before.use * 16 + 16)
                        dve.wait_ge(y_stored[w], before.use * 16 + 16)
                        dve.wait_ge(summed, j)
                        nc.vector.scalar_tensor_tensor(out=y_out[:, w], in0=z_in[:, w], scalar=gate[:, 1:2], in1=x1_in[:, w],
                                                       op0=ALU.mult, op1=ALU.add).then_inc(base_ready, 1)
                over(dve, n, step)

            with dve.Fori(0, TT // 4) as i:
                for u in range(4):
                    dve.wait_ge(x1_loaded[u], i * 16 + (4 * TT + 16))
                    dve.wait_ge(gathered[u], i * 32 + 32)
                    for c, (rows, did) in enumerate(((y_first, first_added), (y_second, added))):
                        if c:
                            dve.wait_ge(first_added, i * 4 + (u + 1))
                        nc.vector.scalar_tensor_tensor(
                            out=sums[:, u], in0=rows[:, u],
                            scalar=weight[:, c, bass.ds(i * 4 + u, 1)],
                            in1=sums[:, u], op0=ALU.mult, op1=ALU.add).then_inc(did, 1)

        @block.tensor
        def _(pe):
            mm = nc.tensor.matmul
            for s_ in (turned, multiplied_up, hid_turned, downed):
                pe.sem_inc(s_, AHEAD)

            def turn(rows, j, u, base):
                pe.wait_ge(split_lo, j + (AHEAD + base - 1))
                for k in range(NK):
                    last = nc.tensor.transpose(turn_bank[u % 2][:, k * P:(k + 1) * P], rows[:, k * P:(k + 1) * P], idn[:])
                last.then_inc(turned, 1)

            pe.wait_ge(const_loaded, 16 * 7)
            pe.wait_ge(r_split, 1)

            def logits(j, t):
                w = t % 2
                pe.wait_ge(split_lo, j + (AHEAD + 1))
                o = down_bank[0][:, t * E:(t + 1) * E]
                for k in range(NK):
                    mm(o, xt_hi[:, w, k], r_hi[:, k, :], start=(k == 0), stop=False)
                    mm(o, xt_hi[:, w, k], r_lo[:, k, :], start=False, stop=False)
                    last = mm(o, xt_lo[:, w, k], r_hi[:, k, :], start=False, stop=(k == NK - 1))
                last.then_inc(multiplied_up, 1)

            def batch(at):
                b, u = at.n, at.slot
                if at.within(B, B):
                    return
                pe.wait_ge(x_ready, b * NT + NT)
                for t in range(NT + 1):
                    if t < NT:
                        turn(xn[:, u, t], b * NT + t, t, 0)
                    if t == 1 and not at.within(0, 0):
                        pe.wait_ge(routed, b * RT - (RT - 1))
                    if t:
                        logits(b * NT + (t - 1), t - 1)

            batches(pe, batch)

            pe.wait_ge(routed, B * RT)
            pe.wait_ge(const_set, 2)
            rows_before, counts = hid_bank[0][:, 0:TT * E], hid_bank[1][:, 0:TT * E]
            every = chosen[:].rearrange("p t e -> p (t e)")
            mm(counts, ones[:], every, start=True, stop=True)
            mm(rows_before, before_p[:], every, start=True, stop=False)
            for t in range(TT - 1):
                last = mm(rows_before[:, (t + 1) * E:].rearrange("p (t e) -> p t e", e=E), ones[:],
                          chosen[:, t:t + 1, :].broadcast_to([P, TT - 1 - t, E]), start=False, stop=(t == TT - 2))
            last.then_inc(counted, 1)

            def up(j, u, e, base):
                w = u % 2
                pe.wait_ge(split_lo, j + (AHEAD + base + TT + 1))
                pe.wait_ge(hidden, j + (AHEAD + base - 1))
                for k in range(NK):
                    def weights(a):
                        return a[:, k, :] if e is None else a[:, bass.ds(e * NK + (NK + k), 1), :].rearrange("p a n -> p (a n)")
                    mm(up_bank[w][:], xt_hi[:, w, k], weights(gu_hi), start=(k == 0), stop=False)
                    mm(up_bank[w][:], xt_hi[:, w, k], weights(gu_lo), start=False, stop=False)
                    last = mm(up_bank[w][:], xt_lo[:, w, k], weights(gu_hi), start=False, stop=(k == NK - 1))
                last.then_inc(multiplied_up, 1)

            def turn_hidden(j, u, base):
                w = u % 2
                pe.wait_ge(hidden, j + (AHEAD + base + 1))
                pe.wait_ge(h_lo_done, j + (AHEAD + base - 1))
                for i in range(NI):
                    last = nc.tensor.transpose(hid_bank[w][:, i * P:(i + 1) * P], hid[:, w, i * P:(i + 1) * P], idn[:])
                last.then_inc(hid_turned, 1)

            def down(j, u, e, base):
                w = u % 2
                pe.wait_ge(h_lo_done, j + (AHEAD + base + 1))
                pe.wait_ge(y_ready if base else base_ready, j + (AHEAD - 1))
                for i in range(NI):
                    def weights(a):
                        return a[:, i, :] if e is None else a[:, bass.ds(e * NI + (NI + i), 1), :].rearrange("p a n -> p (a n)")
                    mm(down_bank[w][:], h_hi[:, w, i], weights(d_hi), start=(i == 0), stop=False)
                    mm(down_bank[w][:], h_hi[:, w, i], weights(d_lo), start=False, stop=False)
                    last = mm(down_bank[w][:], h_lo[:, w, i], weights(d_hi), start=False, stop=(i == NI - 1))
                last.then_inc(downed, 1)

            pe.wait_ge(w_split, 3 * X)
            for name, n, base in (SHARED, ROUTED):
                def expert_of(at):
                    return pe.value_load(block_i[0:1, bass.ds(at.n, 1)], min_val=0, max_val=E - 1)

                def step(at):
                    j, u = at.n, at.slot
                    if at.within(0, 0):
                        pe.wait_ge(rows_loaded[0], 4 * base + 16)
                        turn(x_in[:, 0], 0, 0, base + TT)
                    if not at.within(n - 1, n):
                        after = at.back(-1)
                        pe.wait_ge(rows_loaded[after.slot], after.use * 16 + (4 * base + 16))
                        turn(x_in[:, after.slot], after.n, after.slot, base + TT)
                    if not at.within(0, 0):
                        turn_hidden(at.back(1).n, u + 1, base)
                    own = None
                    if not at.within(n, n):
                        if name == "routed":
                            own = expert_of(at)
                        up(j, u, own, base)
                    if not at.within(0, 0):
                        down(at.back(1).n, u + 1, expert_of(at.back(1)) if name == "routed" else None, base)

                if name == "routed":
                    pe.wait_ge(table_ready, 1)
                    pe.wait_ge(base_ready, AHEAD + TT)
                over(pe, n, step)


def kernel(**inputs):
    import numpy as _np
    import concourse.bacc as _bacc
    from concourse import mybir as _mybir
    from concourse.bass_utils import run_bass_kernel_spmd as _run

    nc = _bacc.Bacc("TRN2", target_bir_lowering=False, num_devices=1)
    arrays, ap = {}, {}

    def give(name, a):
        a = _np.ascontiguousarray(a)
        if a.dtype == _np.bool_:
            a = a.view(_np.int32)
        arrays["in_" + name] = a
        ap[name] = nc.dram_tensor("in_" + name, a.shape, _mybir.dt.from_np(a.dtype), kind="ExternalInput").ap()

    for name in ("x", "ctx_1024", "mask_BxS2_bf0", "g_xattn", "g_ffn") + tuple(
            "L0_xattn_" + n for n in ("Wq", "bq", "Wk", "bk", "Wv", "bv", "Wo", "bo")):
        give(name, inputs[name])
    rel = _np.asarray(inputs["L0_xattn_rel_bias"])
    far = rel.shape[1] // 2
    where = _np.clip(_np.arange(P)[:, None] - _np.arange(STRIP)[None, :] + (NT - 1) * P, -far, far) + far
    give("strips", rel[:, where].transpose(1, 0, 2))
    give("ident", _np.eye(P, dtype=_np.float32))
    wq = _np.asarray(inputs["L0_ffn_Wq"])
    give("ffn_wq", wq.reshape(D, NG, HG, 2, DH).transpose(0, 1, 3, 2, 4).reshape(D, 2 * D))
    give("ffn_wo", _np.asarray(inputs["L0_ffn_Wo"]).reshape(H, 2, DH, D)[:, 0].reshape(D, D))
    for name in ("Wkva", "Wkvb"):
        give(name, inputs["L0_ffn_" + name])
    for name in ("Wgate", "expert_bias", "Wg", "Wu", "Wd", "sWg", "sWu", "sWd"):
        give(name, inputs["L0_ffn_" + name])
    give("w_ln2", inputs["L0_ffn_w_ln2"])
    give("earlier", (_np.arange(P)[:, None] < _np.arange(P)[None, :]).astype(_np.float16))
    give("starts", _np.tile(_np.arange(NB, dtype=_np.float32) * P, (P, 1)))
    give("before_e", _np.tile((_np.arange(E)[None, :] < _np.arange(E)[:, None]).astype(_np.float32), (P, 1, 1)))
    give("w_ln1", _np.asarray(inputs["L0_ffn_w_ln1"]).reshape(NK, P).T)
    freqs = (1.0 / 100000.0 ** (_np.arange(0, DH, 2, dtype=_np.float32) / DH)).astype(_np.float32)
    ang = _np.outer(_np.arange(S, dtype=_np.float32), freqs).astype(_np.float32)
    cos, sin = (_np.tile(_np.repeat(f(ang).astype(_np.float32).T, 2, axis=0), (HG, 1)) for f in (_np.cos, _np.sin))
    give("cos_sin", _np.stack([cos / (8 * WS), sin / 8, cos / WS, sin], 1).astype(_np.float32))
    swap = _np.zeros((P, P), _np.float16)
    even = _np.arange(0, P, 2)
    swap[even + 1, even], swap[even, even + 1] = -1, 1
    give("swap", swap)
    give("causal", _np.where(_np.arange(STRIP)[None, :] - (NT - 1) * P <= _np.arange(P)[:, None], 0, -1e30).astype(_np.float32))
    out = nc.dram_tensor("out_0_dram", (B, S, D), F32, kind="ExternalOutput").ap()
    mask_rows = nc.dram_tensor("mask_rows", (B * H, S), F16, kind="Internal").ap()
    x1 = nc.dram_tensor("x1", (B, S, D), F32, kind="Internal").ap()
    z1 = nc.dram_tensor("z1", (B, S, D), F32, kind="Internal").ap()
    xn_rows = nc.dram_tensor("xn_rows", (B * S, D), F32, kind="Internal").ap()
    base_rows = nc.dram_tensor("base_rows", (B * S, D), F32, kind="Internal").ap()
    x_sorted = nc.dram_tensor("x_sorted", (NB * P, D), F32, kind="Internal").ap()
    y_sorted = nc.dram_tensor("y_sorted", (NB * P, D), F32, kind="Internal").ap()
    used = pass_a(nc, ap["x"], ap["ctx_1024"], ap["mask_BxS2_bf0"], ap["g_xattn"],
           *[ap["L0_xattn_" + n] for n in ("Wq", "bq", "Wk", "bk", "Wv", "bv", "Wo", "bo")],
           ap["strips"], ap["ident"], x1, mask_rows)
    pass_b(nc, x1, ap["w_ln1"], ap["ffn_wq"], ap["Wkva"], ap["Wkvb"], ap["ffn_wo"], ap["cos_sin"], ap["swap"],
           ap["causal"], ap["ident"], z1, x_sorted, used)
    pass_c(nc, x1, z1, ap["g_ffn"], ap["w_ln2"], *[ap[n] for n in ("Wgate", "expert_bias", "Wg", "Wu", "Wd", "sWg", "sWu", "sWd")],
           ap["ident"], ap["earlier"], ap["starts"], ap["before_e"], xn_rows, x_sorted, y_sorted, base_rows, out)
    r = _run(nc, [arrays], core_ids=[0])
    return r.results[0]["out_0_dram"]
```

```python
from contextlib import ExitStack

import numpy as np

import concourse.bass as bass
from concourse import mybir

F32 = mybir.dt.float32
F16 = mybir.dt.float16
U8 = mybir.dt.uint8
I32 = mybir.dt.int32
ALU = mybir.AluOpType
ACT = mybir.ActivationFunctionType
AX_X = mybir.AxisListType.X

P = 128
B = 8
S = 512
D = 512
NT = S // P
NK = D // P
H = 16
DH = 32
HG = P // DH
NG = H // HG
UNITS = H * NT
R = 64
E = 8
I = 256
NI = I // P
EPS = 1e-5
WS = 256.0
HS = 128.0
MASKED = -60000.0
STRIP = S + (NT - 1) * P
TT = B * NT
NB = 2 * TT + E
SHIFT = P.bit_length() - 1


def unit_of(n):
    g, r = divmod(n, NT * HG)
    i, hh = divmod(r, HG)
    return g, i, hh


def pass_a(nc, x, ctxt, maskb, g_gate, wq, bq, wk, bk, wv, bv, wo, bo, strips, ident, x1, mask_rows, qk_rows):
    with ExitStack() as ctx:
        def sb(name, shape, dt=F32):
            return ctx.enter_context(nc.sbuf_tensor("a_" + name, shape, dt))

        used = []

        def sem(name):
            used.append(ctx.enter_context(nc.semaphore("a_" + name)))
            return used[-1]

        bank = [ctx.enter_context(nc.psum_tensor(f"a_bank{i}", [P, 512], F32)) for i in range(8)]
        score_bank, turn_bank, out_bank, job_bank = bank[0:2], bank[2:4], bank[4], bank[5:8]
        RING = len(job_bank)

        w_hi = sb("w_hi", [P, 4, NK, D], F16)
        w_lo = sb("w_lo", [P, 4, NK, D], F16)
        bias = sb("bias", [DH + 1, 4, D], F16)
        ones = sb("ones", [DH + 1, P], F16)
        b_hi, b_lo = bias[0:1], bias[DH:DH + 1]
        strip = sb("strip", [P, H, STRIP])
        idn = sb("idn", [P, P])
        q_stack = sb("q_stack", [3 * DH + 1, H, S], F16)
        k_stack = sb("k_stack", [3 * DH + 1, H, S], F16)
        xn = sb("xn", [P, 2, D])
        cn = sb("cn", [P, 2, D])
        xr = sb("xr", [P, 2, D])
        ct_hi = sb("ct_hi", [P, NK, S], F16)
        ct_lo = sb("ct_lo", [P, NK, S], F16)
        xt_hi = sb("xt_hi", [P, NK, S], F16)
        xt_lo = sb("xt_lo", [P, NK, S], F16)
        o_hi = sb("o_hi", [P, NG, S], F16)
        o_lo = sb("o_lo", [P, NG, S], F16)
        qk_hi = sb("qk_hi", [P, 4, S], F16)
        qk_lo = sb("qk_lo", [P, 4, S], F16)
        sums = [xr[:, 0, :], xr[:, 1, :], cn[:, 0, :], cn[:, 1, :]]
        v = sb("v", [P, NT, D])
        prob = sb("prob", [P, 4, S])
        turned = sb("turned", [P, 2, HG, NT, P])
        stage = turned[:].rearrange("p s h j q -> p s (h j q)")
        normal = sb("normal", [P, S])
        stats = sb("stats", [P, 2, 6])
        mv = sb("mv", [P, 2, 2])
        rstd = sb("rstd", [P, 2, 2])
        power = sb("power", [P, 1])
        low = sb("low", [P, 8])
        den = sb("den", [P, 2, NT * HG])
        rden = sb("rden", [P, 2, NT * HG])
        gate = sb("gate", [P, 2])
        bstage = strip[0:DH + 1, NG * HG - 4:NG * HG, 0:D]
        mask_words = normal[:, 0:P].bitcast(I32)
        mask8 = normal[:, 0:P].bitcast(U8)
        mask_stage = o_hi[:, 0, :]

        w_loaded = [sem(f"w_loaded{i}") for i in range(2)]
        w_free, w_split = sem("w_free"), sem("w_split")
        b_loaded, b_zeroed, b_split = sem("b_loaded"), sem("b_zeroed"), sem("b_split")
        const_loaded, ones_set, power_set, idn_loaded = sem("const_loaded"), sem("ones_set"), sem("power_set"), sem("idn_loaded")
        strips_loaded = [sem(f"strips_loaded{g}") for g in range(NG)]
        gate_ready, gate_scaled = sem("gate_ready"), sem("gate_scaled")
        mask_set, mask_stored = sem("mask_set"), sem("mask_stored")
        x_loaded = [sem(f"x_loaded{i}") for i in range(2)]
        c_loaded = [sem(f"c_loaded{i}") for i in range(2)]
        kept = [sem(f"kept{i}") for i in range(2)]
        xr_loaded = [sem(f"xr_loaded{i}") for i in range(NT)]
        x1_stored = [sem(f"x1_stored{i}") for i in range(2)]
        stats_done, mv_done, eps_added, rstd_done, xn_ready = (sem("stats_done"), sem("mv_done"), sem("eps_added"),
                                                               sem("rstd_done"), sem("xn_ready"))
        job_done, hi_done, left = sem("job_done"), sem("hi_done"), sem("left")
        stacked = [sem(f"stacked{g}") for g in range(NG)]
        scored, biased, exped, turned_done = sem("scored"), sem("biased"), sem("exped"), sem("turned_done")
        kept_act, kept_dve = sem("kept_act"), sem("kept_dve")
        summed, recip_done, normed = sem("summed"), sem("recip_done"), sem("normed")
        o_hi_done, o_lo_done = sem("o_hi_done"), sem("o_lo_done")

        STK = 16 * 7
        QUADS = UNITS // HG
        GS = NT * HG
        LAG, TAIL = 3, 6
        q_scale = 1.0 / (WS * DH ** 0.5)

        DVE_KEEPS = [n for n in range(UNITS) if n % 4 == 3 or n % 4 == 1 and n >= 16]

        def kept_upto(eng, b, low, high):
            for kept, mine in ((kept_act, [n for n in range(UNITS) if n not in DVE_KEEPS]), (kept_dve, DVE_KEEPS)):
                if any(low <= n <= high for n in mine):
                    eng.wait_ge(kept, b * len(mine) + sum(n <= high for n in mine))

        CT, XT, Q, K, V, SP, O = "ct", "xt", "q", "k", "v", "spread", "o"
        own = [((Q, NG - 1), 3), ((K, NG - 1), 7)]
        ahead = [((XT, 0), 5), ((XT, 1), 7), ((CT, 0), 8), ((CT, 1), 10), ((XT, 2), 11), ((CT, 2), 13), ((XT, 3), 14),
                 ((CT, 3), 15)]
        for g in range(1, NG):
            own.append(((SP, g - 1), GS * g + 3))
            ahead += [((Q, g - 1), GS * g + 8), ((K, g - 1), GS * g + 15)]
        own.append(((SP, NG - 1), UNITS + 2))
        ahead += [((V, 0), UNITS), ((V, 1), UNITS + 3), ((V, 2), UNITS + 6), ((V, 3), UNITS + 7)]
        own += [((O, t), UNITS + 8 + t) for t in range(NT)]
        order = sorted(own + ahead, key=lambda j: j[1])
        rounds = {
            "first": [(m, t) for t in range(NT) for m in (CT, XT)] + [(m, g) for g in range(NG - 1) for m in (Q, K)]
                     + [(V, t) for t in range(NT)],
            "steady": [j for j, _ in order],
            "last": [j for j, _ in sorted(own, key=lambda j: j[1])],
        }
        ends = {j: s for j, s in order}
        STEPS = max(ends.values()) + 1
        split_kinds = (CT, XT, Q, K)

        def before(kind, b, count=lambda j: True):
            n = {k: sum(count(j) for j in r) for k, r in rounds.items()}
            return 0 if kind == "first" else n["first"] + n["steady"] * b

        def upto(kind, b, job):
            return before(kind, b) + rounds[kind].index(job) + 1

        def split_upto(kind, b, job):
            is_split = lambda j: j[0] in split_kinds
            r = rounds[kind]
            return before(kind, b, is_split) + sum(is_split(j) for j in r[:r.index(job) + 1])

        def bank_of(kind, job):
            return job_bank[rounds[kind].index(job) % RING]

        def ended(kind, step):
            return [j for j in rounds[kind] if ends[j] == step]

        block = ctx.enter_context(nc.Block())

        @block.sync
        def _(sp):
            def load(src, dst, loaded, b, t, freed):
                if freed:
                    sp.wait_ge(*freed)
                sp.dma_start(dst[:, t % 2, :], src[bass.ds(b * 1, 1), t * P:(t + 1) * P, :].rearrange("a p n -> p (a n)")
                             ).then_inc(loaded[t % 2], 16)

            def keep(kind, b, of, g, part):
                sp.wait_ge(left, upto(kind, b, ((Q, K)[part], g)))
                for low, src in enumerate((qk_hi, qk_lo)):
                    sp.dma_start(qk_rows[bass.ds(of * NG + g, 1), part, low].rearrange("a p n -> p (a n)"),
                                 src[:, 2 * (g % 2) + part, :]).then_inc(kept[part], 16)

            def stack(kind, b, of, g, part):
                sp.wait_ge(kept[part], of * (32 * NG) + 32 * (g + 1))
                dst = (q_stack, k_stack)[part]
                for row, low in enumerate(((0, 1, 0), (0, 0, 1))[part]):
                    sp.dma_start(dst[row * DH:(row + 1) * DH, g * HG:(g + 1) * HG, :],
                                 qk_rows[bass.ds(of * NG + g, 1), part, low].rearrange("a (h p) n -> p (a h) n", p=DH)
                                 ).then_inc(stacked[g], 16)
                if part:
                    rows = mask_rows.rearrange("(b h) n -> b h n", h=H)
                    sp.dma_start(k_stack[3 * DH:3 * DH + 1, g * HG:(g + 1) * HG, :],
                                 rows[bass.ds(of * 1, 1), g * HG:(g + 1) * HG, :]).then_inc(stacked[g], 16)

            sp.dma_start(idn[:], ident).then_inc(idn_loaded, 16)
            for t in range(2):
                load(ctxt, cn, c_loaded, 0, t, None)
                load(x, xn, x_loaded, 0, t, None)
            for n, w in enumerate((bq, bk, bv, bo)):
                for row in (0, DH):
                    sp.dma_start(bstage[row:row + 1, n, :], w.rearrange("(a n) -> a n", a=1)).then_inc(b_loaded, 16)
            for n, w in enumerate((wq, wk, wv, wo)):
                if n >= 2:
                    sp.wait_ge(w_split, n - 1)
                sp.dma_start(stage[:, n % 2, :].rearrange("p (k n) -> p k n", k=NK),
                             w.rearrange("(k p) n -> p k n", p=P)).then_inc(w_loaded[n % 2], 16)
                if n == 0:
                    sp.dma_start(gate[:, 0:1], g_gate.rearrange("(a n) -> a n", a=1).broadcast_to([P, 1])).then_inc(const_loaded, 16)
                    for b in range(B):
                        sp.dma_start(mask_words[b * H:(b + 1) * H, :], maskb[b:b + 1, :].broadcast_to([H, S // 4])).then_inc(const_loaded, 16)
                if n == 1:
                    for t in range(2, NT):
                        load(ctxt, cn, c_loaded, 0, t, (job_done, upto("first", 0, (CT, t - 2))))
                        load(x, xn, x_loaded, 0, t, (job_done, upto("first", 0, (XT, t - 2))))
            sp.wait_ge(mask_set, 1)
            sp.dma_start(mask_rows, mask_stage).then_inc(mask_stored, 16)
            sp.wait_ge(mask_stored, 16)
            sp.wait_ge(b_split, 3)
            def strips_of(g):
                sp.dma_start(strip[:, g * HG:(g + 1) * HG, :], strips[:, g * HG:(g + 1) * HG, :]).then_inc(strips_loaded[g], 16)

            strips_of(0)
            for g in range(NG - 1):
                for part in range(2):
                    keep("first", 0, 0, g, part)
                for part in range(2):
                    stack("first", 0, 0, g, part)
            for g in range(1, NG):
                strips_of(g)

            def body(kind, b):
                more = kind == "steady"
                if more:
                    for t in range(2):
                        load(ctxt, cn, c_loaded, b + 1, t, (x1_stored[t], b * 32 + 32))
                        load(x, xn, x_loaded, b + 1, t, None)
                if more:
                    load(x, xn, x_loaded, b + 1, 2, (job_done, upto(kind, b, (XT, 0))))
                keep(kind, b, b, NG - 1, 0)
                if more:
                    load(x, xn, x_loaded, b + 1, 3, (job_done, upto(kind, b, (XT, 1))))
                    for t in range(2, NT):
                        load(ctxt, cn, c_loaded, b + 1, t, (job_done, upto(kind, b, (CT, t - 2))))
                stack(kind, b, b, NG - 1, 0)
                keep(kind, b, b, NG - 1, 1)
                stack(kind, b, b, NG - 1, 1)
                for t in range(NT):
                    if t < 2:
                        sp.wait_ge(x1_stored[t], b * 32 + 32)
                    elif more:
                        sp.wait_ge(job_done, upto(kind, b, (CT, t)))
                    sp.dma_start(sums[t], x[bass.ds(b * 1, 1), t * P:(t + 1) * P, :].rearrange("a p n -> p (a n)")
                                 ).then_inc(xr_loaded[t], 16)
                for g in range(NG - 1 if more else 0):
                    for part in range(2):
                        keep(kind, b, b + 1, g, part)
                        stack(kind, b, b + 1, g, part)
                for t in range(NT):
                    sp.wait_ge(left, upto(kind, b, (O, t)))
                    sp.dma_start(x1[bass.ds(b * 1, 1), t * P:(t + 1) * P, :].rearrange("a p n -> p (a n)"),
                                 sums[t]).then_inc(x1_stored[t % 2], 16)

            with sp.Fori(0, B - 1) as b:
                body("steady", b)
            body("last", B - 1)
            for i in range(2):
                sp.wait_ge(x1_stored[i], 32 * (B + 1))

        @block.gpsimd
        def _(pool):
            for i in range(2):
                pool.sem_inc(x1_stored[i], 32)
            nc.gpsimd.memset(power[:], -0.5).then_inc(power_set, 1)
            pool.wait_ge(const_loaded, 16 * (1 + B))
            nc.gpsimd.tensor_scalar(mask_stage, mask8, MASKED, None, ALU.mult).then_inc(mask_set, 1)
            pool.wait_ge(power_set, 1)

            def deviations(b):
                for t in range(NT):
                    pool.wait_ge(mv_done, b * NT + t + 1)
                    pool.nop(nofuse=True)
                    nc.gpsimd.tensor_scalar(rstd[:, t % 2, 0:1], mv[:, t % 2, 1:2], EPS, None, ALU.add).then_inc(eps_added, 1)
                    pool.wait_ge(eps_added, b * NT + t + 1)
                    nc.gpsimd.tensor_tensor(rstd[:, t % 2, 1:2], rstd[:, t % 2, 0:1], power[:], ALU.pow).then_inc(rstd_done, 1)

            def body(kind, b):
                if kind == "steady":
                    deviations(b + 1)
                for g in range(NG):
                    pool.wait_ge(o_hi_done, b * NG + g + 1)
                    nc.gpsimd.tensor_tensor(o_lo[:, g, :], normal[:], o_hi[:, g, :], ALU.subtract).then_inc(o_lo_done, 1)

            deviations(0)
            with pool.Fori(0, B - 1) as b:
                body("steady", b)
            body("last", B - 1)

        @block.scalar
        def _(act):
            def high(kind, b, job):
                m, n = job
                if m not in split_kinds:
                    return
                act.wait_ge(job_done, upto(kind, b, job))
                src = bank_of(kind, job)[:]
                if m in (CT, XT):
                    out, src = (ct_hi if m == CT else xt_hi)[:, :, n * P:(n + 1) * P], src.rearrange("p (k q) -> p k q", q=P)
                    scale = 1.0
                else:
                    of = 0 if kind == "first" else b if n == NG - 1 else b + 1
                    if n >= 2:
                        act.wait_ge(stacked[n - 2], of * STK + STK)
                    elif kind != "first":
                        act.wait_ge(stacked[n + 2], of * STK)
                    out, scale = qk_hi[:, 2 * (n % 2) + (m == K), :], (q_scale if m == Q else 1.0 / WS)
                nc.scalar.activation(out, src, ACT.Copy, scale=scale).then_inc(hi_done, 1)

            def keep(b, n):
                act.wait_ge(turned_done, b * UNITS + n + 1)
                nc.scalar.activation(turned[:, n // HG % 2, n % HG, :, :],
                                     turn_bank[n % 2][:].rearrange("p (j q) -> p j q", q=P), ACT.Copy).then_inc(kept_act, 1)

            def body(kind, b):
                for step in range(STEPS + 1):
                    if step < UNITS:
                        g, i, hh = unit_of(step)
                        act.wait_ge(biased, b * UNITS + step + 1)
                        nc.scalar.activation(prob[:, step % 4, :], prob[:, step % 4, :], ACT.Exp, scale=-1.0,
                                             bias=low[:, step % 8:step % 8 + 1],
                                             accum_out=den[:, g % 2, i * HG + hh:i * HG + hh + 1]).then_inc(exped, 1)
                    n = step - LAG
                    if 0 <= n < UNITS and n not in DVE_KEEPS:
                        if n >= 2 * HG:
                            act.wait_ge(summed, b * QUADS + n // HG - 1)
                        keep(b, n)
                    for job in ended(kind, step - 1):
                        high(kind, b, job)
                    g, off = divmod(step - GS, GS)
                    if g >= 0 and off == 6:
                        act.wait_ge(normed, b * NG + g + 1)
                        nc.scalar.activation(o_hi[:, g, :], normal[:], ACT.Copy).then_inc(o_hi_done, 1)

            act.wait_ge(b_loaded, 128)
            act.wait_ge(b_zeroed, 1)
            nc.scalar.activation(b_hi, bstage[0:1], ACT.Copy, scale=WS).then_inc(b_split, 1)
            nc.scalar.activation(b_lo, bstage[DH:DH + 1], ACT.Copy, scale=WS).then_inc(b_split, 1)

            def split(n):
                act.wait_ge(w_loaded[n % 2], 16 * (n // 2 + 1))
                nc.scalar.activation(w_hi[:, n, :, :].rearrange("p k n -> p (k n)"), stage[:, n % 2, :], ACT.Copy,
                                     scale=WS).then_inc(w_free, 1)

            for job in rounds["first"]:
                if job == (CT, 2):
                    split(0)
                if job == (Q, 0):
                    for n in range(1, 4):
                        split(n)
                    act.wait_ge(const_loaded, 16 * (1 + B))
                    nc.scalar.activation(gate[:, 1:2], gate[:, 0:1], ACT.Tanh).then_inc(gate_ready, 1)
                high("first", 0, job)
            act.wait_ge(mask_stored, 16)
            with act.Fori(0, B - 1) as b:
                body("steady", b)
            body("last", B - 1)

        @block.vector
        def _(dve):
            def leave(kind, b, job):
                m, n = job
                src = bank_of(kind, job)[:]
                if m in split_kinds:
                    dve.wait_ge(hi_done, split_upto(kind, b, job))
                    if m in (CT, XT):
                        hi, lo = (ct_hi, ct_lo) if m == CT else (xt_hi, xt_lo)
                        c = slice(n * P, (n + 1) * P)
                        hi, lo, src, scale = hi[:, :, c], lo[:, :, c], src.rearrange("p (k q) -> p k q", q=P), 1.0
                    else:
                        slot = 2 * (n % 2) + (m == K)
                        hi, lo, scale = qk_hi[:, slot, :], qk_lo[:, slot, :], (q_scale if m == Q else 1.0 / WS)
                    nc.vector.scalar_tensor_tensor(out=lo, in0=src, scalar=scale, in1=hi, op0=ALU.mult,
                                                   op1=ALU.subtract).then_inc(left, 1)
                    return
                dve.wait_ge(job_done, upto(kind, b, job))
                if m == V:
                    if kind != "first":
                        dve.wait_ge(summed, b * QUADS + QUADS)
                    nc.vector.tensor_scalar(v[:, n, :], src, 1.0 / WS, None, ALU.mult).then_inc(left, 1)
                elif m == SP:
                    if n:
                        dve.wait_ge(o_lo_done, b * NG + n)
                    nc.vector.tensor_copy(normal[:], src).then_inc(left, 1)
                else:
                    dve.wait_ge(xr_loaded[n], b * 16 + 16)
                    nc.vector.scalar_tensor_tensor(out=sums[n], in0=src, scalar=gate[:, 0:1], in1=sums[n],
                                                   op0=ALU.mult, op1=ALU.add).then_inc(left, 1)

            def moments(b, t):
                dve.wait_ge(x_loaded[t % 2], b * 32 + 16 * (t // 2 + 1))
                nc.vector.bn_stats(stats[:, t % 2, :], xn[:, t % 2, :]).then_inc(stats_done, 1)
                dve.wait_ge(stats_done, b * NT + t + 1)
                dve.nop(nofuse=True)
                nc.vector.bn_aggr(mv[:, t % 2, :], stats[:, t % 2, :]).then_inc(mv_done, 1)

            def normalise(b, t):
                dve.wait_ge(mv_done, b * NT + t + 1)
                dve.wait_ge(rstd_done, b * NT + t + 1)
                nc.vector.tensor_scalar(xn[:, t % 2, :], xn[:, t % 2, :], mv[:, t % 2, 0:1], rstd[:, t % 2, 1:2], ALU.subtract,
                                        ALU.mult).then_inc(xn_ready, 1)

            XN = {3: 0, 5: 1, 9: 2, 12: 3}

            def body(kind, b):
                for step in range(STEPS + 2):
                    if step < UNITS:
                        g, i, hh = unit_of(step)
                        if kind == "steady" and step % GS == 0:
                            dve.wait_ge(strips_loaded[g], 16)
                        dve.wait_ge(scored, b * UNITS + step + 1)
                        if step >= 4:
                            dve.wait_ge(turned_done, b * UNITS + step - 3)
                        at = (NT - 1 - i) * P
                        dve.nop(nofuse=True)
                        nc.vector.tensor_tensor_reduce(out=prob[:, step % 4, :], in0=score_bank[step % 2][:],
                                                       in1=strip[:, g * HG + hh, at:at + S], scale=-1.0, scalar=3e38,
                                                       op0=ALU.add, op1=ALU.min,
                                                       accum_out=low[:, step % 8:step % 8 + 1]).then_inc(biased, 1)
                    n = step - LAG
                    if n in DVE_KEEPS:
                        if n >= 2 * HG:
                            dve.wait_ge(summed, b * QUADS + n // HG - 1)
                        dve.wait_ge(turned_done, b * UNITS + n + 1)
                        nc.vector.tensor_copy(turned[:, n // HG % 2, n % HG, :, :],
                                              turn_bank[n % 2][:].rearrange("p (j q) -> p j q", q=P)).then_inc(kept_dve, 1)
                    g, off = divmod(step - GS, GS)
                    if g >= 0 and off == 1:
                        dve.wait_ge(exped, b * UNITS + (g + 1) * GS)
                        nc.vector.reciprocal(rden[:, g % 2, :], den[:, g % 2, :]).then_inc(recip_done, 1)
                    if g >= 0 and off == 6:
                        dve.wait_ge(summed, b * QUADS + (g + 1) * NT)
                        dve.wait_ge(left, upto(kind, b, (SP, g)))
                        nc.vector.tensor_tensor(normal[:], out_bank[:], normal[:], ALU.mult).then_inc(normed, 1)
                    if kind == "steady" and step in XN:
                        moments(b + 1, XN[step])
                    if kind == "steady" and step - 1 in XN:
                        normalise(b + 1, XN[step - 1])
                    for job in ended(kind, step - 2):
                        leave(kind, b, job)

            nc.vector.memset(bias[:], 0.0).then_inc(b_zeroed, 1)
            nc.vector.memset(ones[:], 1.0).then_inc(ones_set, 1)
            nc.vector.memset(q_stack[3 * DH:3 * DH + 1, :, :], 1.0).then_inc(ones_set, 1)
            dve.wait_ge(b_split, 2)
            nc.vector.scalar_tensor_tensor(out=b_lo, in0=bstage[DH:DH + 1], scalar=WS, in1=b_lo, op0=ALU.mult,
                                           op1=ALU.subtract).then_inc(b_split, 1)

            def split(n):
                dve.wait_ge(w_free, n + 1)
                nc.vector.scalar_tensor_tensor(out=w_lo[:, n, :, :].rearrange("p k n -> p (k n)"), in0=stage[:, n % 2, :],
                                               scalar=WS, in1=w_hi[:, n, :, :].rearrange("p k n -> p (k n)"),
                                               op0=ALU.mult, op1=ALU.subtract).then_inc(w_split, 1)

            for t in range(2):
                moments(0, t)
                normalise(0, t)
            for job in rounds["first"]:
                if job == (CT, 2):
                    split(0)
                if job[0] == CT and job[1] >= 2:
                    moments(0, job[1])
                    normalise(0, job[1])
                if job == (Q, 0):
                    for n in range(1, 4):
                        split(n)
                    dve.wait_ge(gate_ready, 1)
                    nc.vector.tensor_scalar(gate[:, 0:1], gate[:, 1:2], 1.0 / WS, None, ALU.mult).then_inc(gate_scaled, 1)
                leave("first", 0, job)
            dve.wait_ge(gate_scaled, 1)
            with dve.Fori(0, B - 1) as b:
                body("steady", b)
            body("last", B - 1)

        @block.tensor
        def _(pe):
            mm = nc.tensor.matmul

            def free(kind, b, job):
                n = rounds[kind].index(job)
                before_it = before(kind, b) + (n - RING + 1 if n >= RING else 0)
                if kind != "first" or n >= RING:
                    pe.wait_ge(left, before_it)

            def transposes(kind, b, job):
                m, t = job
                src, loaded = (cn, c_loaded) if m == CT else (xn, None)
                of = 0 if kind == "first" else b + 1
                free(kind, b, job)
                if m == CT:
                    pe.wait_ge(c_loaded[t % 2], of * 32 + 16 * (t // 2 + 1))
                else:
                    pe.wait_ge(xn_ready, of * NT + t + 1)
                for k in range(NK):
                    last = nc.tensor.transpose(bank_of(kind, job)[:, k * P:(k + 1) * P], src[:, t % 2, k * P:(k + 1) * P], idn[:])
                last.then_inc(job_done, 1)

            def product(kind, b, job, parts=range(NK)):
                m, n = job
                o, c = bank_of(kind, job)[:], slice(n * P, (n + 1) * P)
                for k in parts:
                    if k == 0:
                        free(kind, b, job)
                    if m in (Q, K):
                        w = (m == K)
                        h, l = (ct_hi, ct_lo) if w else (xt_hi, xt_lo)
                        pairs = ((w_hi[:, w, k, c], h[:, k, :]), (w_hi[:, w, k, c], l[:, k, :]), (w_lo[:, w, k, c], h[:, k, :]))
                        both = (bias[:, int(w), c], ones[:].unsqueeze(1).broadcast_to([DH + 1, NT, P]))
                    else:
                        w = 2 if m == V else 3
                        h, l = (ct_hi, ct_lo) if m == V else (o_hi, o_lo)
                        pairs = ((h[:, k, c], w_hi[:, w, k, :]), (h[:, k, c], w_lo[:, w, k, :]), (l[:, k, c], w_hi[:, w, k, :]))
                        both = (ones[:], bias[:, w, :])
                    for i, (lhs, rhs) in enumerate(pairs):
                        mm(o, lhs, rhs, start=(k == 0 and i == 0), stop=False)
                    if k == NK - 1:
                        mm(o, *both, start=False, stop=True).then_inc(job_done, 1)

            def spread(kind, b, job):
                g = job[1]
                free(kind, b, job)
                pe.wait_ge(recip_done, b * NG + g + 1)
                for t in range(NT):
                    for hh in range(HG):
                        c = t * HG + hh
                        last = mm(bank_of(kind, job)[hh * DH:(hh + 1) * DH, t * P:(t + 1) * P],
                                  rden[:, g % 2, c:c + 1].broadcast_to([P, DH]), idn[:], start=True, stop=True,
                                  tile_position=(0, hh * DH))
                last.then_inc(job_done, 1)

            def fill(kind, b, step):
                if kind == "steady" and step == GS + 2:
                    pe.wait_ge(left, upto(kind, b, (CT, NT - 1)))
                for job in rounds[kind]:
                    m, n = job
                    end = ends[job]
                    if m in (Q, K):
                        at = [end - 3, end - 2, end - 1, end] if n == NG - 1 else [end - 6, end - 4, end - 2, end]
                        if step in at:
                            product(kind, b, job, [at.index(step)])
                    elif step == end and m in (CT, XT):
                        transposes(kind, b, job)
                    elif step == end and m == V:
                        product(kind, b, job)
                    elif step == end and m == SP:
                        spread(kind, b, job)
                    elif step == end and m == O:
                        if n == 0:
                            pe.wait_ge(o_lo_done, b * NG + NG - 1)
                            for t in range(2):
                                product(kind, b, (O, t), range(NK - 1))
                            pe.wait_ge(o_lo_done, b * NG + NG)
                        product(kind, b, job, range(NK - 1 if n < 2 else 0, NK))

            def body(kind, b):
                for step in range(STEPS + 1):
                    if step < UNITS:
                        g, i, hh = unit_of(step)
                        if step % GS == 0:
                            pe.wait_ge(stacked[g], b * STK + STK)
                        if step >= 2:
                            pe.wait_ge(biased, b * UNITS + step - 1)
                        h = g * HG + hh
                        mm(score_bank[step % 2][:], q_stack[:, h, i * P:(i + 1) * P], k_stack[:, h, :], start=True,
                           stop=True).then_inc(scored, 1)
                    fill(kind, b, step)
                    n = step - LAG
                    if 0 <= n < UNITS:
                        pe.wait_ge(exped, b * UNITS + n + 1)
                        if n >= 2:
                            kept_upto(pe, b, n - 2, n - 2)
                        for j in range(NT):
                            last = nc.tensor.transpose(turn_bank[n % 2][:, j * P:(j + 1) * P],
                                                       prob[:, n % 4, j * P:(j + 1) * P], idn[:])
                        last.then_inc(turned_done, 1)
                    m = step - TAIL
                    if m >= 0 and m % HG == HG - 1 and m < UNITS:
                        quad = m // HG
                        g, i = divmod(quad, NT)
                        kept_upto(pe, b, quad * HG, quad * HG + HG - 1)
                        if quad == 0:
                            pe.wait_ge(left, before(kind, b))
                        if i == 0 and g > 0:
                            pe.wait_ge(normed, b * NG + g)
                        for j in range(NT):
                            for hh in range(HG):
                                c = (g * HG + hh) * DH
                                last = mm(out_bank[hh * DH:(hh + 1) * DH, i * P:(i + 1) * P], v[:, j, c:c + DH],
                                          turned[:, quad % 2, hh, j, :], start=(j == 0), stop=(j == NT - 1),
                                          tile_position=(0, hh * DH))
                        last.then_inc(summed, 1)

            pe.wait_ge(idn_loaded, 16)
            pe.wait_ge(ones_set, 2)
            for job in rounds["first"]:
                if job[0] in (CT, XT):
                    transposes("first", 0, job)
                else:
                    if job == (Q, 0):
                        pe.wait_ge(b_split, 3)
                        pe.wait_ge(w_split, 4)
                        pe.wait_ge(left, 2 * NT)
                    product("first", 0, job)
            with pe.Fori(0, B - 1) as b:
                body("steady", b)
            body("last", B - 1)
    return used


def pass_b(nc, x1, w_norm, wq, wkva, wkvb, wo, cos_sin, swap, causal, ident, z1, x_sorted, qk_rows, used):
    with ExitStack() as ctx:
        def sb(name, shape, dt=F32):
            return ctx.enter_context(nc.sbuf_tensor("b_" + name, shape, dt))

        def sem(name):
            return ctx.enter_context(nc.semaphore("b_" + name))

        bank = [ctx.enter_context(nc.psum_tensor(f"b_bank{i}", [P, 512], F32)) for i in range(8)]
        score_bank, turn_bank, out_bank, job_bank = bank[0:2], bank[2:4], bank[4], bank[5:8]
        RING = len(job_bank)

        KR = slice(R, R + DH)
        wq_hi = sb("wq_hi", [P, NK, 2 * D], F16)
        wq_lo = sb("wq_lo", [P, NK, 2 * D], F16)
        wa_hi = sb("wa_hi", [P, NK, R + DH], F16)
        wa_lo = sb("wa_lo", [P, NK, R + DH], F16)
        wb_hi = sb("wb_hi", [R, D], F16)
        wb_lo = sb("wb_lo", [R, D], F16)
        wo_hi = sb("wo_hi", [P, NG, D], F16)
        wo_lo = sb("wo_lo", [P, NG, D], F16)
        wn = sb("wn", [P, NK])
        idn = sb("idn", [P, P])
        swp = sb("swp", [P, P], F16)
        rot = sb("rot", [P, 4, S])
        tri = sb("tri", [P, STRIP])
        q_stack = sb("q_stack", [P, H, S], F16)
        k_stack = sb("k_stack", [P, H, S], F16)
        k_stack2 = sb("k_stack2", [2 * DH, H, S], F16)
        zi = sb("zi", [P, NT, D])
        zn = sb("zn", [P, NT, D])
        zo = sb("zo", [P, NT, D])
        hn = sb("hn", [P, NT, D])
        ht_hi = sb("ht_hi", [P, NK, S], F16)
        ht_lo = sb("ht_lo", [P, NK, S], F16)
        o_hi = sb("o_hi", [P, NG, S], F16)
        o_lo = sb("o_lo", [P, NG, S], F16)
        lat_hi = sb("lat_hi", [R + DH, S], F16)
        lat_lo = sb("lat_lo", [R + DH, S], F16)
        kr_hi = sb("kr_hi", [R + DH, S], F16)
        kr_lo = sb("kr_lo", [R + DH, S], F16)
        kn_hi = sb("kn_hi", [P, S], F16)
        kn_lo = sb("kn_lo", [P, S], F16)
        qn_hi = sb("qn_hi", [P, S], F16)
        qn_lo = sb("qn_lo", [P, S], F16)
        qu_hi = sb("qu_hi", [P, S], F16)
        qu_lo = sb("qu_lo", [P, S], F16)
        qr_hi = sb("qr_hi", [P, S], F16)
        qr_lo = sb("qr_lo", [P, S], F16)
        rc = sb("rc", [P, S])
        rs = sb("rs", [P, S])
        v = sb("v", [P, NT, D])
        prob = sb("prob", [P, 4, S])
        turned = sb("turned", [P, 2, HG, NT, P])
        stage = turned[:].rearrange("p s h j q -> p s (h j q)")
        normal = sb("normal", [P, S])
        stats = sb("stats", [P, NT, 6])
        mv = sb("mv", [P, NT, 2])
        small = sb("small", [P, NT, 6])
        power = sb("power", [P, 1])
        low = sb("low", [P, 8])
        zero = sb("zero", [P, D])
        den = sb("den", [P, 2, NT * HG])
        rden = sb("rden", [P, 2, NT * HG])

        w_loaded = [sem(f"w_loaded{i}") for i in range(2)]
        w_free, w_split, const_loaded, power_set = sem("w_free"), sem("w_split"), sem("const_loaded"), sem("power_set")
        x_loaded, stats_done, mv_done, small_done, z_ready, h_ready, moved = (
            sem("x_loaded"), sem("stats_done"), sem("mv_done"), sem("small_done"), sem("z_ready"), sem("h_ready"), sem("moved"))
        job_done, hi_done, left = sem("job_done"), sem("hi_done"), sem("left")
        rot_cos, rot_sum, rot_hi, rot_lo = sem("rot_cos"), sem("rot_sum"), sem("rot_hi"), sem("rot_lo")
        k_stacked = [sem(f"k_stacked{g}") for g in range(NG)]
        qn_stacked = [sem(f"qn_stacked{g}") for g in range(NG)]
        qr_stacked = [sem(f"qr_stacked{g}") for g in range(NG)]
        z1_stored = [sem(f"z1_stored{i}") for i in range(NT)]
        kn_kept, qn_kept, qr_kept = sem("kn_kept"), sem("qn_kept"), sem("qr_kept")
        zero_set, zeroed = sem("zero_set"), sem("zeroed")
        scored, biased, exped, turned_done = sem("scored"), sem("biased"), sem("exped"), sem("turned_done")
        kept_act, kept_dve = sem("kept_act"), sem("kept_dve")
        summed, recip_done, normed = sem("summed"), sem("recip_done"), sem("normed")
        o_hi_done, o_lo_done = sem("o_hi_done"), sem("o_lo_done")

        QUADS = UNITS // HG
        GS = NT * HG
        LAG, TAIL = 3, 6
        NS = 6
        STK_K, STK_Q = 16 * 6, 16 * 2
        scale_nope = 1.0 / (WS * 8.0)

        DVE_KEEPS = [n for n in range(UNITS) if n % 2]

        def kept_upto(eng, b, low, high):
            for kept, mine in ((kept_act, [n for n in range(UNITS) if n not in DVE_KEEPS]), (kept_dve, DVE_KEEPS)):
                if any(low <= n <= high for n in mine):
                    eng.wait_ge(kept, b * len(mine) + sum(n <= high for n in mine))

        HT, LAT, KSW, K, V, QN, QR, QSW, SP, O = "ht", "lat", "kswap", "k", "v", "qn", "qr", "qswap", "spread", "o"
        G3 = NG - 1
        own = [((K, G3), 1), ((QN, G3), 5), ((QR, G3), 9), ((QSW, G3), 12)]
        ahead = [((HT, 0), 11), ((HT, 1), 12), ((HT, 2), 14), ((HT, 3), 15),
                 ((LAT, 0), GS + 5), ((KSW, 0), GS + 8), ((QN, 0), GS + 9), ((K, 0), GS + 10), ((QR, 0), GS + 14),
                 ((QSW, 0), 2 * GS + 1)]
        for g in range(1, NG - 1):
            at = GS * (g + 1)
            ahead += [((K, g), at + 4), ((QN, g), at + 8), ((QR, g), at + 12), ((QSW, g), at + 15)]
        own += [((SP, g), GS * (g + 1) + 3 - (g == G3)) for g in range(NG)]
        ahead += [((V, 0), UNITS), ((V, 1), UNITS + 3), ((V, 2), UNITS + 6), ((V, 3), UNITS + 7)]
        own += [((O, t), UNITS + 8 + t) for t in range(NT)]
        order = sorted(own + ahead, key=lambda j: j[1])
        rounds = {
            "first": [(HT, k) for k in range(NK)] + [(LAT, 0), (KSW, 0)]
                     + [(m, g) for g in range(NG - 1) for m in (K, QN, QR, QSW)] + [(V, t) for t in range(NT)],
            "steady": [j for j, _ in order],
            "last": [j for j, _ in sorted(own, key=lambda j: j[1])],
        }
        ends = {j: s for j, s in order}
        STEPS = max(ends.values()) + 1
        split_kinds = (HT, LAT, K, QN, QR)
        turns = {"first": ["k"] + list(range(NG - 1)), "steady": [G3, "k"] + list(range(NG - 1)), "last": [G3]}
        turn_step = {r: ends[(KSW, 0) if r == "k" else (QSW, r)] + 4 for r in turns["steady"]}

        def before(kind, b, count=lambda j: True):
            n = {k: sum(count(j) for j in r) for k, r in rounds.items()}
            return 0 if kind == "first" else n["first"] + n["steady"] * b

        def upto(kind, b, job):
            return before(kind, b) + rounds[kind].index(job) + 1

        def split_upto(kind, b, job):
            is_split = lambda j: j[0] in split_kinds
            r = rounds[kind]
            return before(kind, b, is_split) + sum(is_split(j) for j in r[:r.index(job) + 1])

        def turns_upto(kind, b, r):
            first = 0 if kind == "first" else len(turns["first"]) + len(turns["steady"]) * b
            return first + turns[kind].index(r) + 1

        def bank_of(kind, job):
            return job_bank[rounds[kind].index(job) % RING]

        def ended(kind, step):
            return [j for j in rounds[kind] if ends[j] == step]

        def batch_of(kind, b, g):
            return 0 if kind == "first" else b if g == G3 else b + 1

        def reuse(eng, kind, b, g, kept):
            if g > 0 or kind != "first":
                eng.wait_ge(kept, batch_of(kind, b, g) * (32 * NG) + 32 * g)

        loads = [(wa_hi[:], wa_lo[:], wkva.rearrange("(k p) n -> p k n", p=P), P, NK, R + DH),
                 (wb_hi[:], wb_lo[:], wkvb, R, 1, D),
                 (wq_hi[:, :, 0:D], wq_lo[:, :, 0:D], wq[:, 0:D].rearrange("(k p) n -> p k n", p=P), P, NK, D),
                 (wq_hi[:, :, D:2 * D], wq_lo[:, :, D:2 * D], wq[:, D:2 * D].rearrange("(k p) n -> p k n", p=P), P, NK, D),
                 (wo_hi[:], wo_lo[:], wo.rearrange("(g p) n -> p g n", p=P), P, NG, D)]

        def staged(n):
            _, _, src, rows, k, w = loads[n]
            a = stage[0:rows, n % 2, 0:k * w]
            return a.rearrange("p (k n) -> p k n", k=k) if len(src.shape) == 3 else a

        block = ctx.enter_context(nc.Block())

        @block.sync
        def _(sp):
            def keep(src, of, g, kind, kept):
                for low in range(2):
                    sp.dma_start(qk_rows[bass.ds(of * NG + g, 1), kind, low].rearrange("a p n -> p (a n)"), src[low][:]).then_inc(kept, 16)

            def rows(stack, row, of, g, kind, low, stacked):
                sp.dma_start(stack[row * DH:(row + 1) * DH, g * HG:(g + 1) * HG, :],
                             qk_rows[bass.ds(of * NG + g, 1), kind, low].rearrange("a (h p) n -> p (a h) n", p=DH)).then_inc(stacked[g], 16)

            def stack(kind, b, g):
                of = batch_of(kind, b, g)
                if g == 0:
                    sp.wait_ge(rot_lo, turns_upto(kind, b, "k"))
                    sp.nop(nofuse=True)
                sp.wait_ge(left, upto(kind, b, (K, g)))
                keep((kn_hi, kn_lo), of, g, 0, kn_kept)
                for to, row, src in ((k_stack, 1, kr_hi), (k_stack, 3, kr_hi), (k_stack2, 1, kr_lo)):
                    sp.dma_start(to[row * DH:(row + 1) * DH, g * HG:(g + 1) * HG, :],
                                 src[KR, :].unsqueeze(1).broadcast_to([DH, HG, S])).then_inc(k_stacked[g], 16)
                sp.wait_ge(left, upto(kind, b, (QN, g)))
                keep((qn_hi, qn_lo), of, g, 1, qn_kept)
                sp.wait_ge(kn_kept, of * (32 * NG) + 32 * (g + 1))
                for to, row, low in ((k_stack, 0, 0), (k_stack, 2, 0), (k_stack2, 0, 1)):
                    rows(to, row, of, g, 0, low, k_stacked)
                sp.wait_ge(rot_lo, turns_upto(kind, b, g))
                keep((qr_hi, qr_lo), of, g, 2, qr_kept)
                sp.wait_ge(qn_kept, of * (32 * NG) + 32 * (g + 1))
                for low in range(2):
                    rows(q_stack, 2 * low, of, g, 1, low, qn_stacked)
                sp.wait_ge(qr_kept, of * (32 * NG) + 32 * (g + 1))
                for low in range(2):
                    rows(q_stack, 2 * low + 1, of, g, 2, low, qr_stacked)

            def load(b):
                sp.dma_start(zi[:], x1[bass.ds(b * 1, 1), :, :].rearrange("a (t p) n -> p (a t) n", p=P)).then_inc(x_loaded, 16)

            def body(kind, b):
                if kind == "steady":
                    sp.wait_ge(z_ready, b * NT + NT)
                    load(b + 1)
                stack(kind, b, G3)
                for g in range(NG - 1 if kind == "steady" else 0):
                    stack(kind, b, g)
                for t in range(NT):
                    sp.wait_ge(left, upto(kind, b, (O, t)))
                    sp.dma_start(z1[bass.ds(b * 1, 1), t * P:(t + 1) * P, :].rearrange("a p n -> p (a n)"),
                                 zo[:, t, :]).then_inc(z1_stored[t], 16)

            load(0)
            def weights(n):
                src = loads[n][2]
                if n >= 2:
                    sp.wait_ge(w_split, n - 1)
                sp.dma_start(staged(n), src).then_inc(w_loaded[n % 2], 16)
                if n == 0:
                    for dst, src in ((idn[:], ident), (swp[:], swap), (rot[:], cos_sin), (tri[:], causal), (wn[:], w_norm)):
                        sp.dma_start(dst, src).then_inc(const_loaded, 16)
            for n in range(4):
                weights(n)
            for g in range(NG - 1):
                stack("first", 0, g)
                if g == 0:
                    weights(4)
            with sp.Fori(0, B - 1) as b:
                body("steady", b)
            body("last", B - 1)
            for i in range(NT):
                sp.wait_ge(z1_stored[i], 16 * (B + 1))
            sp.wait_ge(zeroed, 16 * (3 * B + 1))

        @block.gpsimd
        def _(pool):
            nc.gpsimd.memset(power[:], -0.5).then_inc(power_set, 1)
            nc.gpsimd.memset(zero[:], 0.0).then_inc(zero_set, 1)
            for s in used:
                pool.sem_clear(s)
            pool.wait_ge(power_set, 1)

            def norms(b):
                for t in range(NT):
                    s = [small[:, t, i:i + 1] for i in range(NS)]
                    var, done = mv[:, t, 1:2], (b * NT + t) * NS
                    pool.wait_ge(mv_done, b * NT + t + 1)
                    pool.nop(nofuse=True)
                    nc.gpsimd.tensor_scalar(s[0], var, EPS, None, ALU.add).then_inc(small_done, 1)
                    pool.wait_ge(small_done, done + 1)
                    nc.gpsimd.tensor_tensor(s[1], s[0], power[:], ALU.pow).then_inc(small_done, 1)
                    pool.wait_ge(small_done, done + 2)
                    nc.gpsimd.tensor_tensor(s[2], s[1], s[1], ALU.mult).then_inc(small_done, 1)
                    pool.wait_ge(small_done, done + 3)
                    nc.gpsimd.tensor_tensor(s[3], s[2], var, ALU.mult).then_inc(small_done, 1)
                    pool.wait_ge(small_done, done + 4)
                    pool.nop(nofuse=True)
                    nc.gpsimd.tensor_scalar(s[4], s[3], EPS, None, ALU.add).then_inc(small_done, 1)
                    pool.wait_ge(small_done, done + 5)
                    nc.gpsimd.tensor_tensor(s[5], s[4], power[:], ALU.pow).then_inc(small_done, 1)

            def rotate(kind, b, r):
                part, job, hi, lo = (KR, (KSW, 0), kr_hi, kr_lo) if r == "k" else (slice(0, P), (QSW, r), qr_hi, qr_lo)
                if r == "k":
                    if kind == "first":
                        pool.wait_ge(small_done, NT * NS)
                    else:
                        pool.wait_ge(o_lo_done, b * NG + 1)
                pool.wait_ge(left, upto(kind, b, job))
                nc.gpsimd.tensor_tensor(rc[part, :], rc[part, :], rs[part, :], ALU.add).then_inc(rot_sum, 1)
                pool.wait_ge(rot_hi, turns_upto(kind, b, r))
                nc.gpsimd.tensor_tensor(lo[part, :], rc[part, :], hi[part, :], ALU.subtract).then_inc(rot_lo, 1)
                if r == "k":
                    pool.wait_ge(rot_lo, turns_upto(kind, b, r))

            def body(kind, b):
                more = kind == "steady"
                if more:
                    norms(b + 1)
                for step in range(STEPS + 6):
                    for r in turns[kind]:
                        if turn_step[r] == step:
                            rotate(kind, b, r)
                    g, off = divmod(step - GS, GS)
                    if 0 <= g < NG and off == 6:
                        pool.wait_ge(o_hi_done, b * NG + g + 1)
                        nc.gpsimd.tensor_tensor(o_lo[:, g, :], normal[:], o_hi[:, g, :], ALU.subtract).then_inc(o_lo_done, 1)

            norms(0)
            for r in turns["first"]:
                rotate("first", 0, r)
            with pool.Fori(0, B - 1) as b:
                body("steady", b)
            body("last", B - 1)

        @block.scalar
        def _(act):
            def high(kind, b, job):
                m, n = job
                if m not in split_kinds:
                    return
                act.wait_ge(job_done, upto(kind, b, job))
                src, scale = bank_of(kind, job)[:], 1.0 / WS
                if m == HT:
                    out, scale = ht_hi[:, n, :], wn[:, n:n + 1]
                elif m == LAT:
                    out, src = lat_hi[:], src[0:R + DH]
                elif m == K:
                    reuse(act, kind, b, n, kn_kept)
                    out = kn_hi[:]
                elif m == QN:
                    reuse(act, kind, b, n, qn_kept)
                    out, scale = qn_hi[:], scale_nope
                else:
                    out = qu_hi[:]
                nc.scalar.activation(out, src, ACT.Copy, scale=scale).then_inc(hi_done, 1)

            def rotated(kind, b, r):
                if r == "k":
                    if kind != "first":
                        act.wait_ge(k_stacked[G3], b * STK_K + STK_K)
                    out, src = kr_hi[KR, :], rc[KR, :]
                else:
                    reuse(act, kind, b, r, qr_kept)
                    out, src = qr_hi[:], rc[:]
                act.wait_ge(rot_sum, turns_upto(kind, b, r))
                nc.scalar.activation(out, src, ACT.Copy).then_inc(rot_hi, 1)

            def scaled(b, t):
                act.wait_ge(small_done, (b * NT + t) * NS + NS)
                act.wait_ge(z_ready, b * NT + t + 1)
                nc.scalar.activation(hn[:, t, :], zn[:, t, :], ACT.Copy, scale=small[:, t, 5:6]).then_inc(h_ready, 1)

            def clear(b, part):
                n = NB // B // 3
                act.wait_ge(zeroed, b * 48 + 16 * (part + 1))
                act.dma_start(x_sorted[bass.ds(b * (3 * n * P) + part * n * P, n * P), :].rearrange("(t p) n -> p t n", p=P),
                              zero[:].unsqueeze(1).broadcast_to([P, n, D])).then_inc(zeroed, 16)

            def move(b, t):
                act.wait_ge(z1_stored[t], b * 16 + 16)
                act.wait_ge(z_ready, b * NT + t + 1)
                nc.scalar.activation(zo[:, t, :], zn[:, t, :], ACT.Copy).then_inc(moved, 1)

            def body(kind, b):
                for step in range(STEPS + 1):
                    if step in (GS // 2, GS, GS + GS // 2):
                        clear(b, step // (GS // 2) - 1)
                    if step < UNITS:
                        g, i, hh = unit_of(step)
                        w = (i + 1) * P
                        act.wait_ge(biased, b * UNITS + step + 1)
                        nc.scalar.activation(prob[:, step % 4, 0:w], prob[:, step % 4, 0:w], ACT.Exp, scale=-1.0,
                                             bias=low[:, step % 8:step % 8 + 1],
                                             accum_out=den[:, g % 2, i * HG + hh:i * HG + hh + 1]).then_inc(exped, 1)
                    n = step - LAG
                    if 0 <= n < UNITS and n not in DVE_KEEPS:
                        if n >= 2 * HG:
                            act.wait_ge(summed, b * QUADS + n // HG - 1)
                        i = unit_of(n)[1]
                        act.wait_ge(turned_done, b * UNITS + n + 1)
                        nc.scalar.activation(turned[:, n // HG % 2, n % HG, 0:i + 1, :],
                                             turn_bank[n % 2][:, 0:(i + 1) * P].rearrange("p (j q) -> p j q", q=P),
                                             ACT.Copy).then_inc(kept_act, 1)
                    if kind == "steady" and 7 <= step < 7 + NT:
                        scaled(b + 1, step - 7)
                    if 2 <= step < 2 + NT:
                        move(b, step - 2)
                    for job in ended(kind, step - 1):
                        high(kind, b, job)
                    for r in turns[kind]:
                        if turn_step[r] == step:
                            rotated(kind, b, r)
                    g, off = divmod(step - GS, GS)
                    if 0 <= g < NG and off == 6:
                        act.wait_ge(normed, b * NG + g + 1)
                        nc.scalar.activation(o_hi[:, g, :], normal[:], ACT.Copy).then_inc(o_hi_done, 1)

            def split(n):
                act.wait_ge(w_loaded[n % 2], 16 * (n // 2 + 1))
                nc.scalar.activation(loads[n][0], staged(n), ACT.Copy, scale=WS).then_inc(w_free, 1)

            act.sem_inc(zeroed, 16)
            for t in range(NT):
                act.sem_inc(z1_stored[t], 16)
            act.wait_ge(zero_set, 1)
            split(0)
            split(1)
            act.wait_ge(const_loaded, 80)
            for t in range(NT):
                scaled(0, t)
            for job in rounds["first"]:
                if job in ((QN, 0), (V, 0)):
                    for n in ((2, 3) if job == (QN, 0) else (4,)):
                        split(n)
                high("first", 0, job)
                if job[0] == KSW or job[0] == QSW:
                    rotated("first", 0, "k" if job[0] == KSW else job[1])
            with act.Fori(0, B - 1) as b:
                body("steady", b)
            body("last", B - 1)

        @block.vector
        def _(dve):
            def leave(kind, b, job):
                m, n = job
                src, scale, r = bank_of(kind, job)[:], 1.0 / WS, turns[kind]
                if m in split_kinds:
                    dve.wait_ge(hi_done, split_upto(kind, b, job))
                    if m in (LAT, QR):
                        which = "k" if m == LAT else n
                        part, table = (KR, 2) if m == LAT else (slice(0, P), 0)
                        if kind != "first" or r.index(which):
                            dve.wait_ge(rot_lo, turns_upto(kind, b, which) - 1)
                        nc.vector.tensor_tensor(rc[part, :], src[part], rot[part, table, :], ALU.mult).then_inc(rot_cos, 1)
                    if m == HT:
                        hi, lo, scale = ht_hi[:, n, :], ht_lo[:, n, :], wn[:, n:n + 1]
                    elif m == LAT:
                        hi, lo, src = lat_hi[:], lat_lo[:], src[0:R + DH]
                    elif m == K:
                        hi, lo = kn_hi[:], kn_lo[:]
                    elif m == QN:
                        hi, lo, scale = qn_hi[:], qn_lo[:], scale_nope
                    else:
                        hi, lo = qu_hi[:], qu_lo[:]
                    nc.vector.scalar_tensor_tensor(out=lo, in0=src, scalar=scale, in1=hi, op0=ALU.mult,
                                                   op1=ALU.subtract).then_inc(left, 1)
                    return
                dve.wait_ge(job_done, upto(kind, b, job))
                if m == KSW or m == QSW:
                    part, table = (KR, 3) if m == KSW else (slice(0, P), 1)
                    dve.wait_ge(rot_cos, turns_upto(kind, b, "k" if m == KSW else n))
                    nc.vector.tensor_tensor(rs[part, :], src[part], rot[part, table, :], ALU.mult).then_inc(left, 1)
                elif m == V:
                    if kind != "first":
                        dve.wait_ge(summed, b * QUADS + QUADS)
                    nc.vector.tensor_scalar(v[:, n, :], src, 1.0 / WS, None, ALU.mult).then_inc(left, 1)
                elif m == SP:
                    if n:
                        dve.wait_ge(o_lo_done, b * NG + n)
                    nc.vector.tensor_copy(normal[:], src).then_inc(left, 1)
                else:
                    dve.wait_ge(moved, b * NT + n + 1)
                    nc.vector.scalar_tensor_tensor(out=zo[:, n, :], in0=src, scalar=1.0 / WS, in1=zo[:, n, :],
                                                   op0=ALU.mult, op1=ALU.add).then_inc(left, 1)

            def moments(b, t):
                dve.wait_ge(x_loaded, b * 16 + 16)
                nc.vector.bn_stats(stats[:, t, :], zi[:, t, :]).then_inc(stats_done, 1)
                dve.wait_ge(stats_done, b * NT + t + 1)
                dve.nop(nofuse=True)
                nc.vector.bn_aggr(mv[:, t, :], stats[:, t, :]).then_inc(mv_done, 1)

            def normalise(b, t, more=True):
                dve.wait_ge(mv_done, b * NT + t + 1)
                dve.wait_ge(small_done, (b * NT + t) * NS + 2)
                if more:
                    dve.wait_ge(moved, (b - 1) * NT + t + 1)
                    dve.wait_ge(h_ready, (b - 1) * NT + t + 1)
                nc.vector.tensor_scalar(zn[:, t, :], zi[:, t, :], mv[:, t, 0:1], small[:, t, 1:2], ALU.subtract,
                                        ALU.mult).then_inc(z_ready, 1)

            def body(kind, b):
                for step in range(STEPS + 2):
                    if step < UNITS:
                        g, i, hh = unit_of(step)
                        w = (i + 1) * P
                        dve.wait_ge(scored, b * UNITS + step + 1)
                        if step >= 4:
                            dve.wait_ge(turned_done, b * UNITS + step - 3)
                        at = (NT - 1 - i) * P
                        dve.nop(nofuse=True)
                        nc.vector.tensor_tensor_reduce(out=prob[:, step % 4, 0:w], in0=score_bank[step % 2][:, 0:w],
                                                       in1=tri[:, at:at + w], scale=-1.0, scalar=3e38,
                                                       op0=ALU.add, op1=ALU.min,
                                                       accum_out=low[:, step % 8:step % 8 + 1]).then_inc(biased, 1)
                    n = step - LAG
                    if n in DVE_KEEPS:
                        i = unit_of(n)[1]
                        if n >= 2 * HG:
                            dve.wait_ge(summed, b * QUADS + n // HG - 1)
                        dve.wait_ge(turned_done, b * UNITS + n + 1)
                        nc.vector.tensor_copy(turned[:, n // HG % 2, n % HG, 0:i + 1, :],
                                              turn_bank[n % 2][:, 0:(i + 1) * P].rearrange("p (j q) -> p j q", q=P)
                                              ).then_inc(kept_dve, 1)
                    g, off = divmod(step - GS, GS)
                    if 0 <= g < NG and off == 1:
                        dve.wait_ge(exped, b * UNITS + (g + 1) * GS)
                        nc.vector.reciprocal(rden[:, g % 2, :], den[:, g % 2, :]).then_inc(recip_done, 1)
                    if 0 <= g < NG and off == 6:
                        dve.wait_ge(summed, b * QUADS + (g + 1) * NT)
                        dve.wait_ge(left, upto(kind, b, (SP, g)))
                        nc.vector.tensor_tensor(normal[:], out_bank[:], normal[:], ALU.mult).then_inc(normed, 1)
                    if kind == "steady" and 4 <= step < 4 + NT:
                        moments(b + 1, step - 4)
                    if kind == "steady" and 6 <= step < 6 + NT:
                        normalise(b + 1, step - 6)
                    for job in ended(kind, step - 2):
                        leave(kind, b, job)

            def split(n):
                dve.wait_ge(w_free, n + 1)
                nc.vector.scalar_tensor_tensor(out=loads[n][1], in0=staged(n), scalar=WS, in1=loads[n][0], op0=ALU.mult,
                                               op1=ALU.subtract).then_inc(w_split, 1)

            for t in range(NT):
                moments(0, t)
            for t in range(NT):
                normalise(0, t, more=False)
            split(0)
            split(1)
            dve.wait_ge(const_loaded, 80)
            for job in rounds["first"]:
                if job in ((QN, 0), (V, 0)):
                    for n in ((2, 3) if job == (QN, 0) else (4,)):
                        split(n)
                leave("first", 0, job)
            with dve.Fori(0, B - 1) as b:
                body("steady", b)
            body("last", B - 1)

        @block.tensor
        def _(pe):
            mm = nc.tensor.matmul

            def free(kind, b, job):
                n = rounds[kind].index(job)
                if kind != "first" or n >= RING:
                    pe.wait_ge(left, before(kind, b) + (n - RING + 1 if n >= RING else 0))

            def chain(o, pairs, begins, ends_it):
                for n, ((lh, ll), (rh, rl)) in enumerate(pairs):
                    mm(o, lh, rh, start=(begins and n == 0), stop=False)
                    mm(o, lh, rl, start=False, stop=False)
                    last = mm(o, ll, rh, start=False, stop=(ends_it and n == len(pairs) - 1))
                return last

            def run(kind, b, job, parts=range(NK)):
                m, n = job
                o = bank_of(kind, job)
                parts = list(parts)
                if parts[0] == 0:
                    free(kind, b, job)
                if m == HT:
                    of = 0 if kind == "first" else b + 1
                    pe.wait_ge(h_ready, of * NT + NT)
                    for t in range(NT):
                        last = nc.tensor.transpose(o[:, t * P:(t + 1) * P], hn[:, t, n * P:(n + 1) * P], idn[:])
                elif m in (LAT, QN, QR):
                    if m == LAT and parts[0] == 0:
                        pe.wait_ge(left, upto(kind, b, (HT, NK - 1)))
                    c = slice(0, R + DH) if m == LAT else slice((2 * n + (m == QR)) * P, (2 * n + (m == QR) + 1) * P)
                    wh, wl = (wa_hi, wa_lo) if m == LAT else (wq_hi, wq_lo)
                    o = o[0:R + DH] if m == LAT else o[:]
                    last = chain(o, [((wh[:, k, c], wl[:, k, c]), (ht_hi[:, k, :], ht_lo[:, k, :])) for k in parts],
                                 parts[0] == 0, parts[-1] == NK - 1)
                elif m == KSW:
                    pe.wait_ge(left, upto(kind, b, (LAT, 0)))
                    pe.nop(nofuse=True)
                    mm(o[KR, :], swp[KR, R:R + DH], lat_hi[KR, :], start=True, stop=False, tile_position=(R, R))
                    last = mm(o[KR, :], swp[KR, R:R + DH], lat_lo[KR, :], start=False, stop=True, tile_position=(R, R))
                elif m == QSW:
                    pe.wait_ge(left, upto(kind, b, (QR, n)))
                    mm(o[:], swp[:], qu_hi[:], start=True, stop=False)
                    last = mm(o[:], swp[:], qu_lo[:], start=False, stop=True)
                elif m == K:
                    c = slice(n * P, (n + 1) * P)
                    last = chain(o[:], [((wb_hi[:, c], wb_lo[:, c]), (lat_hi[0:R, :], lat_lo[0:R, :]))], True, True)
                elif m == V:
                    c = slice(n * P, (n + 1) * P)
                    last = chain(o[:], [((lat_hi[0:R, c], lat_lo[0:R, c]), (wb_hi[:], wb_lo[:]))], True, True)
                elif m == SP:
                    pe.wait_ge(recip_done, b * NG + n + 1)
                    for t in range(NT):
                        for hh in range(HG):
                            c = t * HG + hh
                            last = mm(o[hh * DH:(hh + 1) * DH, t * P:(t + 1) * P],
                                      rden[:, n % 2, c:c + 1].broadcast_to([P, DH]), idn[:], start=True, stop=True,
                                      tile_position=(0, hh * DH))
                else:
                    c = slice(n * P, (n + 1) * P)
                    last = chain(o[:], [((o_hi[:, k, c], o_lo[:, k, c]), (wo_hi[:, k, :], wo_lo[:, k, :])) for k in parts],
                                 parts[0] == 0, parts[-1] == NK - 1)
                if m not in (LAT, QN, QR, O) or parts[-1] == NK - 1:
                    last.then_inc(job_done, 1)

            def fill(kind, b, step):
                for job in rounds[kind]:
                    end = ends[job]
                    if job[0] in (LAT, QN, QR):
                        if end - NK < step <= end:
                            run(kind, b, job, [step - end + NK - 1])
                    elif step == end and job[0] == O:
                        if job[1] == 0:
                            pe.wait_ge(o_lo_done, b * NG + NG - 1)
                            for t in range(2):
                                run(kind, b, (O, t), range(NK - 1))
                            pe.wait_ge(o_lo_done, b * NG + NG)
                        run(kind, b, job, range(NK - 1 if job[1] < 2 else 0, NK))
                    elif step == end:
                        run(kind, b, job)

            def body(kind, b):
                for step in range(STEPS + 1):
                    if step < UNITS:
                        g, i, hh = unit_of(step)
                        if step % GS == 0:
                            pe.wait_ge(k_stacked[g], b * STK_K + STK_K)
                            pe.wait_ge(qn_stacked[g], b * STK_Q + STK_Q)
                            pe.wait_ge(qr_stacked[g], b * STK_Q + STK_Q)
                        if step >= 2:
                            pe.wait_ge(biased, b * UNITS + step - 1)
                        h, w, c = g * HG + hh, (i + 1) * P, slice(i * P, (i + 1) * P)
                        mm(score_bank[step % 2][:, 0:w], q_stack[:, h, c], k_stack[:, h, 0:w], start=True, stop=False)
                        mm(score_bank[step % 2][:, 0:w], q_stack[0:2 * DH, h, c], k_stack2[:, h, 0:w], start=False,
                           stop=True).then_inc(scored, 1)
                    fill(kind, b, step)
                    n = step - LAG
                    if 0 <= n < UNITS:
                        pe.wait_ge(exped, b * UNITS + n + 1)
                        if n >= 2:
                            kept_upto(pe, b, n - 2, n - 2)
                        for j in range(unit_of(n)[1] + 1):
                            last = nc.tensor.transpose(turn_bank[n % 2][:, j * P:(j + 1) * P],
                                                       prob[:, n % 4, j * P:(j + 1) * P], idn[:])
                        last.then_inc(turned_done, 1)
                    m = step - TAIL
                    if m >= 0 and m % HG == HG - 1 and m < UNITS:
                        quad = m // HG
                        g, i = divmod(quad, NT)
                        kept_upto(pe, b, quad * HG, quad * HG + HG - 1)
                        if quad == 0:
                            pe.wait_ge(left, before(kind, b))
                        if i == 0 and g > 0:
                            pe.wait_ge(normed, b * NG + g)
                        for j in range(i + 1):
                            for hh in range(HG):
                                c = (g * HG + hh) * DH
                                last = mm(out_bank[hh * DH:(hh + 1) * DH, i * P:(i + 1) * P], v[:, j, c:c + DH],
                                          turned[:, quad % 2, hh, j, :], start=(j == 0), stop=(j == i),
                                          tile_position=(0, hh * DH))
                        last.then_inc(summed, 1)

            pe.wait_ge(const_loaded, 80)
            for job in rounds["first"]:
                needed = {(LAT, 0): 1, (K, 0): 2, (QN, 0): 4}
                if job in needed:
                    pe.wait_ge(w_split, needed[job])
                run("first", 0, job)
            pe.wait_ge(w_split, len(loads))
            with pe.Fori(0, B - 1) as b:
                body("steady", b)
            body("last", B - 1)


class Count:

    def __init__(self, turn, c, size):
        self.turn, self.c, self.size = turn, c, size
        self.n = c if isinstance(turn, int) else turn * size + c
        self.slot = c % size
        self.use = c // size if isinstance(turn, int) else turn + c // size

    def back(self, steps):
        return Count(self.turn, self.c - steps, self.size)

    def within(self, low, high):
        return isinstance(self.turn, int) and low <= self.c <= high


def pass_c(nc, x1, z1, g_gate, w_norm, w_route, b_route, wg, wu, wd, swg, swu, swd, ident, earlier, starts, before_e,
           xn_rows, x_sorted, y_sorted, base_rows, out):
    with ExitStack() as ctx:
        def sb(name, shape, dt=F32):
            return ctx.enter_context(nc.sbuf_tensor("c_" + name, shape, dt))

        def sem(name):
            return ctx.enter_context(nc.semaphore("c_" + name))

        bank = [ctx.enter_context(nc.psum_tensor(f"c_bank{i}", [P, 512], F32)) for i in range(8)]
        turn_bank, up_bank, hid_bank, down_bank = bank[0:2], bank[2:4], bank[4:6], bank[6:8]
        X = E + 1

        gu_hi = sb("gu_hi", [P, X * NK, 2 * I], F16)
        gu_lo = sb("gu_lo", [P, X * NK, 2 * I], F16)
        d_hi = sb("d_hi", [P, X * NI, D], F16)
        d_lo = sb("d_lo", [P, X * NI, D], F16)
        r_hi = sb("r_hi", [P, NK, E], F16)
        r_lo = sb("r_lo", [P, NK, E], F16)
        stage = sb("stage", [P, 3, NK * I])
        r_stage = sb("r_stage", [P, NK, E])
        wn = sb("wn", [P, D])
        idn = sb("idn", [P, P])
        before_p = sb("before_p", [P, P], F16)
        ones = sb("ones", [P, P], F16)
        before_x = sb("before_x", [P, E, E])
        start_row = sb("start_row", [P, NB])
        br = sb("br", [P, E])
        gate = sb("gate", [P, 2])
        z = sb("z", [P, 2, NT, D])
        xn = sb("xn", [P, 2, NT, D])
        zf, xf = z[:].rearrange("p a t n -> p (a t) n"), xn[:].rearrange("p a t n -> p (a t) n")
        x_in, z_in, x1_in, y_out = zf[:, 0:4], zf[:, 4:8], xf[:, 0:4], xf[:, 4:8]
        y_first, y_second, sums = zf[:, 0:4], zf[:, 4:8], xf[:, 0:4]
        xt_hi = sb("xt_hi", [P, 2, NK, P], F16)
        xt_lo = sb("xt_lo", [P, 2, NK, P], F16)
        th = sb("th", [P, 2, I])
        hid = sb("hid", [P, 2, I])
        h_hi = sb("h_hi", [P, 2, NI, P], F16)
        h_lo = sb("h_lo", [P, 2, NI, P], F16)
        squares = hid_bank + up_bank
        small = sb("small", [P, 2, 3, NT])
        power = sb("power", [P, NT])
        logit = sb("logit", [P, NT, E])
        top = sb("top", [P, NT, E])
        two = sb("two", [P, NT, E])
        rest = sb("rest", [P, NT, E])
        sel = sb("sel", [P, NT, E])
        ex = sb("ex", [P, NT, E])
        tot = sb("tot", [P, 2, NT])
        share = sb("share", [P, TT, E])
        chosen = sb("chosen", [P, TT, E], F16)
        count = sb("count", [P, E])
        count_i = sb("count_i", [P, 2, E], I32)
        padded = sb("padded", [P, E])
        lesser = sb("lesser", [P, E, E])
        start = sb("start", [P, 2, E])
        row = sb("row", [P, TT, E])
        place = sb("place", [P, 4, TT])
        place_i = sb("place_i", [P, TT, 2], I32)
        hit = sb("hit", [P, TT, E])
        weight = sb("weight", [P, 2, TT])
        started = sb("started", [P, NB, E])
        block_x = sb("block_x", [P, NB])
        block_i = sb("block_i", [P, NB], I32)
        index = sb("index", [P, 4, 2], I32)

        w_loaded = [sem(f"w_loaded{i}") for i in range(3)]
        w_hi_done, w_split, r_loaded, r_split, const_loaded, const_set, gate_ready, two_set = (
            sem("w_hi_done"), sem("w_split"), sem("r_loaded"), sem("r_split"), sem("const_loaded"), sem("const_set"),
            sem("gate_ready"), sem("two_set"))
        z_loaded = [sem(f"z_loaded{i}") for i in range(2)]
        xn_stored = [sem(f"xn_stored{i}") for i in range(2)]
        summed_up, small_done, x_ready = sem("summed_up"), sem("small_done"), sem("x_ready")
        routed, expd, ranked, table_ready = sem("routed"), sem("expd"), sem("ranked"), sem("table_ready")
        counted = sem("counted")
        rows_loaded, x1_loaded, z1_loaded, y_stored, scattered = (
            [sem(f"{n}{i}") for i in range(4)] for n in ("rows_loaded", "x1_loaded", "z1_loaded", "y_stored", "scattered"))
        turned, split_hi, split_lo, multiplied_up = sem("turned"), sem("split_hi"), sem("split_lo"), sem("multiplied_up")
        tanhed, half_done, hidden, hid_turned, h_hi_done, h_lo_done, downed, summed, y_ready = (
            sem("tanhed"), sem("half_done"), sem("hidden"), sem("hid_turned"), sem("h_hi_done"), sem("h_lo_done"), sem("downed"),
            sem("summed"), sem("y_ready"))
        base_ready = sem("base_ready")
        index_ready = sem("index_ready")
        gathered, out_stored = ([sem(f"{n}{i}") for i in range(4)] for n in ("gathered", "out_stored"))
        first_added, added = sem("first_added"), sem("added")

        NSM = 2
        AHEAD = 4
        DOWN = HS / (2.0 * WS * WS)
        RT = 2 * NT + 9
        z_rows = z1.rearrange("b (t p) n -> (b t) p n", p=P)
        x1_rows = x1.rearrange("b (t p) n -> (b t) p n", p=P)
        out_rows = out.rearrange("b (t p) n -> (b t) p n", p=P)
        xn_tiles = xn_rows.rearrange("(t p) n -> t p n", p=P)
        base_tiles = base_rows.rearrange("(t p) n -> t p n", p=P)
        xs_tiles = x_sorted.rearrange("(t p) n -> t p n", p=P)
        ys_tiles = y_sorted.rearrange("(t p) n -> t p n", p=P)

        def tile(rows, j):
            return rows[bass.ds(j * 1, 1), :, :].rearrange("a p n -> p (a n)")

        SHARED, ROUTED = ("shared", TT, 0), ("routed", NB, TT)

        def over(eng, steps, call):
            call(Count(0, 0, 4))
            with eng.Fori(0, (steps - 4) // 4) as i:
                for u in range(4):
                    call(Count(i, 1 + u, 4))
            for j in range(steps - 3, steps + 1):
                call(Count(0, j, 4))

        def split_views(e, part):
            if part == 2:
                return (d_hi[:, bass.ds(e * NI, NI), :], d_lo[:, bass.ds(e * NI, NI), :],
                        stage[:, 2].rearrange("p (k n) -> p k n", k=NI))
            c = slice(part * I, (part + 1) * I)
            return (gu_hi[:, bass.ds(e * NK, NK), c], gu_lo[:, bass.ds(e * NK, NK), c],
                    stage[:, part].rearrange("p (k n) -> p k n", k=NK))

        def batches(eng, call):
            call(Count(0, 0, 2))
            with eng.Fori(0, (B - 2) // 2) as i:
                for u in range(2):
                    call(Count(i, 1 + u, 2))
            call(Count(0, B - 1, 2))
            call(Count(0, B, 2))

        block = ctx.enter_context(nc.Block())

        @block.sync
        def _(sp):
            for i in range(4):
                sp.sem_inc(y_stored[i], 16)
                sp.sem_inc(out_stored[i], 16)
            for i in range(2):
                sp.sem_inc(xn_stored[i], 16)

            def weights(e, sources, first=False):
                for part in range(3):
                    if not first:
                        sp.wait_ge(w_split, e * 3 + (part - 2))
                    sp.dma_start(split_views(0, part)[2], sources[part]).then_inc(w_loaded[part], 16)

            def load(at):
                sp.dma_start(z[:, at.slot], z1[bass.ds(at.n * 1, 1), :, :].rearrange("a (t p) n -> p (a t) n", p=P)
                             ).then_inc(z_loaded[at.slot], 16)

            def prepare(at):
                b, u = at.n, at.slot
                if at.within(B, B):
                    return
                if not at.within(B - 1, B - 1):
                    if not at.within(0, 0):
                        sp.wait_ge(x_ready, b * NT)
                    load(at.back(-1))
                weights(b + 1, [wg[bass.ds(b * 1, 1)].rearrange("a (k p) n -> p (a k) n", p=P),
                                wu[bass.ds(b * 1, 1)].rearrange("a (k p) n -> p (a k) n", p=P),
                                wd[bass.ds(b * 1, 1)].rearrange("a (k p) n -> p (a k) n", p=P)])
                sp.wait_ge(x_ready, b * NT + NT)
                sp.dma_start(xn_rows[bass.ds(b * S, S), :].rearrange("(t p) n -> p t n", p=P), xn[:, u]).then_inc(xn_stored[u], 16)

            load(Count(0, 0, 2))
            for dst, src in ((idn[:], ident), (wn[:], w_norm.rearrange("(a n) -> a n", a=1).broadcast_to([P, D])),
                             (br[:], b_route.rearrange("(a n) -> a n", a=1).broadcast_to([P, E])),
                             (gate[:, 0:1], g_gate.rearrange("(a n) -> a n", a=1).broadcast_to([P, 1])),
                             (before_p[:], earlier), (start_row[:], starts), (before_x[:], before_e)):
                sp.dma_start(dst, src).then_inc(const_loaded, 16)
            sp.dma_start(r_stage[:], w_route.rearrange("(k p) n -> p k n", p=P)).then_inc(r_loaded, 16)
            weights(0, [swg[0].rearrange("(k p) n -> p k n", p=P), swu[0].rearrange("(k p) n -> p k n", p=P),
                        swd[0].rearrange("(k p) n -> p k n", p=P)], first=True)
            batches(sp, prepare)

            for i in range(2):
                sp.wait_ge(xn_stored[i], 16 + 16 * (B // 2))
            sp.wait_ge(turned, AHEAD + TT)

            def blocks(kind):
                name, n, base = kind
                ready = base_ready if name == "shared" else y_ready

                def load(at):
                    j, u = at.n, at.slot
                    if name == "routed" or not at.within(0, 3):
                        sp.wait_ge(turned, j + (AHEAD + TT + base - 3))
                        sp.nop(nofuse=True)
                    if name == "shared":
                        if not at.within(0, 3):
                            sp.wait_ge(scattered[u], at.use * 32)
                            sp.nop(nofuse=True)
                            sp.wait_ge(base_ready, j + (AHEAD - 3))
                            sp.nop(nofuse=True)
                        sp.dma_start(x_in[:, u], tile(xn_tiles, j)).then_inc(rows_loaded[u], 16)
                        sp.dma_start(z_in[:, u], tile(z_rows, j)).then_inc(z1_loaded[u], 16)
                        sp.dma_start(x1_in[:, u], tile(x1_rows, j)).then_inc(x1_loaded[u], 16)
                    else:
                        sp.dma_start(x_in[:, u], tile(xs_tiles, j)).then_inc(rows_loaded[u], 16)

                def store(at):
                    sp.wait_ge(ready, at.n + (AHEAD + 1))
                    sp.dma_start(tile(base_tiles if name == "shared" else ys_tiles, at.n), y_out[:, at.slot]
                                 ).then_inc(y_stored[at.slot], 16)

                for j in range(4):
                    load(Count(0, j, 4))
                with sp.Fori(0, (n - 4) // 4) as i:
                    for u in range(4):
                        load(Count(i, 4 + u, 4))
                        store(Count(i, u, 4))
                for j in range(n - 4, n):
                    store(Count(0, j, 4))

            blocks(SHARED)
            for i in range(4):
                sp.wait_ge(scattered[i], 32 * (TT // 4))
            blocks(ROUTED)

            for i in range(4):
                sp.wait_ge(y_stored[i], 16 + 16 * ((TT + NB) // 4))
            with sp.Fori(0, TT // 4) as i:
                for u in range(4):
                    sp.wait_ge(out_stored[u], i * 16 + 16)
                    sp.dma_start(sums[:, u], tile(base_tiles, i * 4 + u)).then_inc(x1_loaded[u], 16)
            for i in range(4):
                sp.wait_ge(out_stored[i], 16 + 16 * (TT // 4))

        @block.gpsimd
        def _(pool):
            nc.gpsimd.memset(ones[:], 1.0).then_inc(const_set, 1)
            nc.gpsimd.memset(power[:], -0.5).then_inc(const_set, 1)
            pool.wait_ge(const_set, 2)
            with pool.Fori(0, B // 2) as i:
                for u in range(2):
                    b, s = Count(i, u, 2).n, small[:, u]
                    pool.wait_ge(summed_up, b * NT + NT)
                    pool.nop(nofuse=True)
                    nc.gpsimd.tensor_scalar(s[:, 1, :], s[:, 0, :], 1.0 / D, EPS, ALU.mult, ALU.add).then_inc(small_done, 1)
                    pool.wait_ge(small_done, b * NSM + 1)
                    nc.gpsimd.tensor_tensor(s[:, 2, :], s[:, 1, :], power[:], ALU.pow).then_inc(small_done, 1)
            pool.wait_ge(table_ready, 1)
            with pool.Fori(0, TT // 4) as i:
                for u in range(4):
                    pool.wait_ge(rows_loaded[u], i * 16 + 16)
                    pool.nop(nofuse=True)
                    nc.gpsimd.tensor_copy(index[:, u, :], place_i[:, bass.ds(i * 4 + u, 1), :].rearrange("p a n -> p (a n)")
                                          ).then_inc(index_ready, 1)
                    pool.wait_ge(index_ready, i * 4 + (u + 1))
                    pool.nop(nofuse=True)
                    for c in range(2):
                        pool.indirect_dma_start(x_sorted, bass.IndirectOffsetOnAxis(index[:, u, c:c + 1], 0), x_in[:, u], None
                                                ).then_inc(scattered[u], 16)
            for i in range(4):
                pool.wait_ge(y_stored[i], 16 + 16 * ((TT + NB) // 4))
            with pool.Fori(0, TT // 4) as i:
                for u in range(4):
                    pool.wait_ge(added, i * 4 + (u + 1))
                    pool.nop(nofuse=True)
                    nc.gpsimd.tensor_copy(index[:, u, :], place_i[:, bass.ds(i * 4 + u, 1), :].rearrange("p a n -> p (a n)")
                                          ).then_inc(index_ready, 1)
                    pool.wait_ge(index_ready, i * 4 + (TT + u + 1))
                    pool.nop(nofuse=True)
                    for c, rows in enumerate((y_first, y_second)):
                        pool.indirect_dma_start(rows[:, u], None, y_sorted, bass.IndirectOffsetOnAxis(index[:, u, c:c + 1], 0)
                                                ).then_inc(gathered[u], 16)

        @block.scalar
        def _(act):
            act.sem_inc(split_hi, AHEAD)
            act.sem_inc(h_hi_done, AHEAD)
            act.sem_inc(y_ready, AHEAD)

            def high(j, u, base):
                act.wait_ge(turned, j + (AHEAD + base + 1))
                act.wait_ge(multiplied_up, j + (AHEAD + base - 1))
                nc.scalar.activation(xt_hi[:, u % 2].rearrange("p k q -> p (k q)"), turn_bank[u % 2][:], ACT.Copy).then_inc(split_hi, 1)

            def weights(e, parts=range(3)):
                for part in parts:
                    hi, _, src = split_views(e, part)
                    act.wait_ge(w_loaded[part], e * 16 + 16)
                    nc.scalar.activation(hi, src, ACT.Copy, scale=WS).then_inc(w_hi_done, 1)

            act.wait_ge(const_loaded, 16 * 7)
            nc.scalar.activation(gate[:, 1:2], gate[:, 0:1], ACT.Tanh).then_inc(gate_ready, 1)
            act.wait_ge(r_loaded, 16)
            nc.scalar.activation(r_hi[:], r_stage[:], ACT.Copy, scale=WS).then_inc(w_hi_done, 1)
            weights(0)

            def square(at):
                b, u = at.n, at.slot
                act.wait_ge(z_loaded[u], at.use * 16 + 16)
                if not at.within(0, 0):
                    act.wait_ge(summed_up, b * NT)
                if not at.within(0, 1):
                    act.wait_ge(x_ready, b * NT - NT)
                for t in range(NT):
                    nc.scalar.activation(squares[t][:], z[:, u, t, :], ACT.Square, accum_out=small[:, u, 0, t:t + 1]
                                         ).then_inc(summed_up, 1)

            def batch(at):
                b = at.n
                if at.within(0, 0):
                    square(at)
                else:
                    for t in range(NT):
                        high(b * NT + (t - NT), t, 0)
                        if t < 3:
                            weights(b, [t])
                if not at.within(B - 1, B):
                    square(at.back(-1))
                if not at.within(0, 0):
                    act.wait_ge(routed, b * RT - 5)
                    nc.scalar.activation(ex[:], ex[:], ACT.Exp).then_inc(expd, 1)

            batches(act, batch)

            for name, n, base in (SHARED, ROUTED):
                def step(at):
                    j, u, before = at.n, at.slot, at.back(1)
                    if at.within(0, 0):
                        high(0, 0, base + TT)
                    if not at.within(n - 1, n):
                        high(j + 1, u + 1, base + TT)
                    if not at.within(0, 0):
                        act.wait_ge(hid_turned, j + (AHEAD + base))
                        act.wait_ge(downed, j + (AHEAD + base - 2))
                        nc.scalar.activation(h_hi[:, (u + 1) % 2].rearrange("p i q -> p (i q)"), hid_bank[(u + 1) % 2][:, 0:I],
                                             ACT.Copy).then_inc(h_hi_done, 1)
                    if not at.within(n, n):
                        act.wait_ge(multiplied_up, j + (AHEAD + base + TT + 1))
                        act.wait_ge(half_done, j + (AHEAD + base - 1))
                        nc.scalar.activation(th[:, u % 2], up_bank[u % 2][:, 0:I], ACT.Tanh, scale=0.5 / WS).then_inc(tanhed, 1)
                    if name == "routed" and not at.within(0, 0):
                        act.wait_ge(downed, j + (AHEAD + base))
                        act.wait_ge(y_stored[before.slot], before.use * 16 + (16 + 4 * base))
                        nc.scalar.activation(y_out[:, before.slot], down_bank[(u + 1) % 2][:], ACT.Copy).then_inc(y_ready, 1)
                over(act, n, step)

            with act.Fori(0, TT // 4) as i:
                for u in range(4):
                    act.wait_ge(added, i * 4 + (AHEAD + u + 1))
                    act.dma_start(tile(out_rows, i * 4 + u), sums[:, u]).then_inc(out_stored[u], 16)

        @block.vector
        def _(dve):
            dve.sem_inc(split_lo, AHEAD)
            dve.sem_inc(half_done, AHEAD)
            dve.sem_inc(hidden, AHEAD)
            dve.sem_inc(h_lo_done, AHEAD)
            dve.sem_inc(base_ready, AHEAD)
            dve.sem_inc(added, AHEAD)
            nc.vector.memset(two[:], -3e38).then_inc(two_set, 1)

            def low(j, u, base):
                dve.wait_ge(split_hi, j + (AHEAD + base + 1))
                nc.vector.tensor_tensor(xt_lo[:, u % 2].rearrange("p k q -> p (k q)"), turn_bank[u % 2][:],
                                        xt_hi[:, u % 2].rearrange("p k q -> p (k q)"), ALU.subtract).then_inc(split_lo, 1)

            def weights(e, parts=range(3)):
                for part in parts:
                    hi, lo, src = split_views(e, part)
                    dve.wait_ge(w_hi_done, e * 3 + (2 + part))
                    nc.vector.scalar_tensor_tensor(out=lo, in0=src, scalar=WS, in1=hi, op0=ALU.mult, op1=ALU.subtract
                                                   ).then_inc(w_split, 1)

            def route(b):
                step = [0]

                def did(call):
                    call.then_inc(routed, 1)
                    step[0] += 1

                def after():
                    dve.wait_ge(routed, b * RT + step[0])
                    dve.nop(nofuse=True)

                def tiles(a):
                    return a[:, bass.ds(b * NT, NT), :]

                dve.wait_ge(multiplied_up, b * NT + (AHEAD + NT))
                did(nc.vector.scalar_tensor_tensor(out=logit[:], in0=down_bank[0][:, 0:NT * E].rearrange("p (t e) -> p t e", e=E),
                                                   scalar=1.0 / WS, in1=br[:].unsqueeze(1).broadcast_to([P, NT, E]),
                                                   op0=ALU.mult, op1=ALU.add))
                after()
                for t in range(NT):
                    did(nc.vector.max(out=top[:, t, :], in_=logit[:, t, :]))
                after()
                did(nc.vector.tensor_copy(two[:, :, 0:2], top[:, :, 0:2]))
                after()
                for t in range(NT):
                    did(nc.vector.match_replace(out=rest[:, t, :], in_to_replace=two[:, t, :], in_values=logit[:, t, :],
                                                imm_value=-1e38))
                did(nc.vector.tensor_tensor(ex[:], logit[:], top[:, :, 0:1].broadcast_to([P, NT, E]), ALU.subtract))
                after()
                did(nc.vector.tensor_tensor(sel[:], rest[:], logit[:], ALU.not_equal))
                assert step[0] == RT - 5, step[0]
                after()
                did(nc.vector.tensor_copy(tiles(chosen), sel[:]))
                dve.wait_ge(expd, b * 1 + 1)
                did(nc.vector.tensor_tensor(ex[:], ex[:], sel[:], ALU.mult))
                after()
                did(nc.vector.tensor_reduce(tot[:, 0, :], ex[:], AX_X, ALU.add))
                after()
                did(nc.vector.reciprocal(tot[:, 1, :], tot[:, 0, :]))
                after()
                did(nc.vector.tensor_tensor(tiles(share), ex[:], tot[:, 1, :].unsqueeze(2).broadcast_to([P, NT, E]), ALU.mult))
                assert step[0] == RT, step[0]

            dve.wait_ge(const_loaded, 16 * 7)
            dve.wait_ge(gate_ready, 1)
            dve.wait_ge(two_set, 1)
            dve.wait_ge(w_hi_done, 1)
            nc.vector.scalar_tensor_tensor(out=r_lo[:], in0=r_stage[:], scalar=WS, in1=r_hi[:], op0=ALU.mult,
                                           op1=ALU.subtract).then_inc(r_split, 1)
            weights(0)

            def batch(at):
                b, u, last = at.n, at.slot, at.within(B, B)
                if not at.within(0, 0):
                    for t in range(NT):
                        low(b * NT + (t - NT), t, 0)
                        if t < 3:
                            weights(b, [t])
                if not last:
                    dve.wait_ge(small_done, b * NSM + NSM)
                    if not at.within(0, 1):
                        dve.wait_ge(xn_stored[u], at.use * 16 + 16)
                        dve.wait_ge(turned, b * NT + (AHEAD - NT))
                        dve.nop(nofuse=True)
                    for t in range(NT):
                        nc.vector.scalar_tensor_tensor(out=xn[:, u, t, :], in0=z[:, u, t, :], scalar=small[:, u, 2, t:t + 1],
                                                       in1=wn[:], op0=ALU.mult, op1=ALU.mult).then_inc(x_ready, 1)
                if not at.within(0, 0):
                    route(at.back(1).n)

            batches(dve, batch)

            done = [0]

            def rank(call):
                call.then_inc(ranked, 1)
                done[0] += 1

            def after():
                dve.wait_ge(ranked, done[0])

            def all_tokens(a):
                return a.unsqueeze(2).broadcast_to([P, TT, E])

            v = nc.vector
            dve.wait_ge(counted, 1)
            rank(v.tensor_reduce(count[:], hid_bank[1][:, 0:TT * E].rearrange("p (t e) -> p e t", e=E), AX_X, ALU.add))
            after()
            rank(v.tensor_scalar(count_i[:, 0], count[:], float(P - 1), None, ALU.add))
            after()
            rank(v.tensor_scalar(count_i[:, 1], count_i[:, 0], SHIFT, SHIFT, ALU.logical_shift_right, ALU.logical_shift_left))
            after()
            rank(v.tensor_copy(padded[:], count_i[:, 1]))
            after()
            rank(v.tensor_tensor(lesser[:], before_x[:], padded[:].unsqueeze(1).broadcast_to([P, E, E]), ALU.mult))
            after()
            rank(v.tensor_reduce(start[:, 0], lesser[:], AX_X, ALU.add))
            after()
            rank(v.tensor_tensor(start[:, 1], start[:, 0], padded[:], ALU.add))
            rank(v.scalar_tensor_tensor(out=row[:], in0=hid_bank[0][:, 0:TT * E].rearrange("p (t e) -> p t e", e=E), scalar=1.0,
                                        in1=start[:, 0].unsqueeze(1).broadcast_to([P, TT, E]), op0=ALU.add, op1=ALU.add))
            after()
            rank(v.tensor_tensor(row[:], row[:], chosen[:], ALU.mult))
            after()
            rank(v.tensor_reduce(place[:, 0], row[:], AX_X, ALU.max))
            rank(v.tensor_reduce(place[:, 1], row[:], AX_X, ALU.add))
            after()
            rank(v.tensor_tensor(place[:, 2], place[:, 1], place[:, 0], ALU.subtract))
            rank(v.tensor_scalar(place_i[:, :, 0], place[:, 0], -1.0, 0.0, ALU.add, ALU.max))
            after()
            rank(v.tensor_scalar(place_i[:, :, 1], place[:, 2], -1.0, 0.0, ALU.add, ALU.max))
            rank(v.tensor_tensor(started[:], start_row[:].unsqueeze(2).broadcast_to([P, NB, E]),
                                 start[:, 1].unsqueeze(1).broadcast_to([P, NB, E]), ALU.is_ge))
            after()
            rank(v.tensor_reduce(block_x[:], started[:], AX_X, ALU.add))
            after()
            rank(v.tensor_scalar(block_i[:], block_x[:], float(E - 1), None, ALU.min))
            after()
            dve.sem_inc(table_ready, 1)
            rank(v.tensor_tensor(hit[:], row[:], all_tokens(place[:, 0]), ALU.is_equal))
            after()
            rank(v.tensor_tensor(hit[:], hit[:], share[:], ALU.mult))
            after()
            rank(v.tensor_reduce(place[:, 0], hit[:], AX_X, ALU.add))
            rank(v.tensor_tensor(row[:], share[:], hit[:], ALU.subtract))
            after()
            rank(v.tensor_reduce(place[:, 1], row[:], AX_X, ALU.add))
            after()
            rank(v.tensor_scalar(weight[:], place[:, 0:2], gate[:, 1:2], 1.0 / (WS * HS), ALU.mult, ALU.mult))

            for name, n, base in (SHARED, ROUTED):
                def step(at):
                    j, u, before = at.n, at.slot, at.back(1)
                    if at.within(0, 0):
                        low(0, 0, base + TT)
                    if not at.within(n - 1, n):
                        low(j + 1, u + 1, base + TT)
                    if not at.within(0, 0):
                        w = (u + 1) % 2
                        dve.wait_ge(h_hi_done, j + (AHEAD + base))
                        nc.vector.tensor_tensor(h_lo[:, w].rearrange("p i q -> p (i q)"), hid_bank[w][:, 0:I],
                                                h_hi[:, w].rearrange("p i q -> p (i q)"), ALU.subtract).then_inc(h_lo_done, 1)
                    if not at.within(n, n):
                        w = u % 2
                        dve.wait_ge(tanhed, j + (base + 1))
                        dve.wait_ge(hid_turned, j + (AHEAD + base - 1))
                        nc.vector.scalar_tensor_tensor(out=hid[:, w], in0=th[:, w], scalar=1.0, in1=up_bank[w][:, 0:I],
                                                       op0=ALU.add, op1=ALU.mult).then_inc(half_done, 1)
                        dve.wait_ge(half_done, j + (AHEAD + base + 1))
                        nc.vector.scalar_tensor_tensor(out=hid[:, w], in0=hid[:, w], scalar=DOWN, in1=up_bank[w][:, I:2 * I],
                                                       op0=ALU.mult, op1=ALU.mult).then_inc(hidden, 1)
                    if name == "shared" and not at.within(0, 0):
                        w = before.slot
                        dve.wait_ge(downed, j + (AHEAD + base))
                        dve.wait_ge(z1_loaded[w], before.use * 16 + 16)
                        nc.vector.scalar_tensor_tensor(out=z_in[:, w], in0=down_bank[(u + 1) % 2][:], scalar=1.0 / (WS * HS),
                                                       in1=z_in[:, w], op0=ALU.mult, op1=ALU.add).then_inc(summed, 1)
                        dve.wait_ge(x1_loaded[w], before.use * 16 + 16)
                        dve.wait_ge(y_stored[w], before.use * 16 + 16)
                        dve.wait_ge(summed, j)
                        nc.vector.scalar_tensor_tensor(out=y_out[:, w], in0=z_in[:, w], scalar=gate[:, 1:2], in1=x1_in[:, w],
                                                       op0=ALU.mult, op1=ALU.add).then_inc(base_ready, 1)
                over(dve, n, step)

            with dve.Fori(0, TT // 4) as i:
                for u in range(4):
                    dve.wait_ge(x1_loaded[u], i * 16 + (4 * TT + 16))
                    dve.wait_ge(gathered[u], i * 32 + 32)
                    for c, (rows, did) in enumerate(((y_first, first_added), (y_second, added))):
                        if c:
                            dve.wait_ge(first_added, i * 4 + (u + 1))
                        nc.vector.scalar_tensor_tensor(
                            out=sums[:, u], in0=rows[:, u],
                            scalar=weight[:, c, bass.ds(i * 4 + u, 1)],
                            in1=sums[:, u], op0=ALU.mult, op1=ALU.add).then_inc(did, 1)

        @block.tensor
        def _(pe):
            mm = nc.tensor.matmul
            for s_ in (turned, multiplied_up, hid_turned, downed):
                pe.sem_inc(s_, AHEAD)

            def turn(rows, j, u, base):
                pe.wait_ge(split_lo, j + (AHEAD + base - 1))
                for k in range(NK):
                    last = nc.tensor.transpose(turn_bank[u % 2][:, k * P:(k + 1) * P], rows[:, k * P:(k + 1) * P], idn[:])
                last.then_inc(turned, 1)

            pe.wait_ge(const_loaded, 16 * 7)
            pe.wait_ge(r_split, 1)

            def logits(j, t):
                w = t % 2
                pe.wait_ge(split_lo, j + (AHEAD + 1))
                o = down_bank[0][:, t * E:(t + 1) * E]
                for k in range(NK):
                    mm(o, xt_hi[:, w, k], r_hi[:, k, :], start=(k == 0), stop=False)
                    mm(o, xt_hi[:, w, k], r_lo[:, k, :], start=False, stop=False)
                    last = mm(o, xt_lo[:, w, k], r_hi[:, k, :], start=False, stop=(k == NK - 1))
                last.then_inc(multiplied_up, 1)

            def batch(at):
                b, u = at.n, at.slot
                if at.within(B, B):
                    return
                pe.wait_ge(x_ready, b * NT + NT)
                for t in range(NT + 1):
                    if t < NT:
                        turn(xn[:, u, t], b * NT + t, t, 0)
                    if t == 1 and not at.within(0, 0):
                        pe.wait_ge(routed, b * RT - (RT - 1))
                    if t:
                        logits(b * NT + (t - 1), t - 1)

            batches(pe, batch)

            pe.wait_ge(routed, B * RT)
            pe.wait_ge(const_set, 2)
            rows_before, counts = hid_bank[0][:, 0:TT * E], hid_bank[1][:, 0:TT * E]
            every = chosen[:].rearrange("p t e -> p (t e)")
            mm(counts, ones[:], every, start=True, stop=True)
            mm(rows_before, before_p[:], every, start=True, stop=False)
            for t in range(TT - 1):
                last = mm(rows_before[:, (t + 1) * E:].rearrange("p (t e) -> p t e", e=E), ones[:],
                          chosen[:, t:t + 1, :].broadcast_to([P, TT - 1 - t, E]), start=False, stop=(t == TT - 2))
            last.then_inc(counted, 1)

            def up(j, u, e, base):
                w = u % 2
                pe.wait_ge(split_lo, j + (AHEAD + base + TT + 1))
                pe.wait_ge(hidden, j + (AHEAD + base - 1))
                for k in range(NK):
                    def weights(a):
                        return a[:, k, :] if e is None else a[:, bass.ds(e * NK + (NK + k), 1), :].rearrange("p a n -> p (a n)")
                    mm(up_bank[w][:], xt_hi[:, w, k], weights(gu_hi), start=(k == 0), stop=False)
                    mm(up_bank[w][:], xt_hi[:, w, k], weights(gu_lo), start=False, stop=False)
                    last = mm(up_bank[w][:], xt_lo[:, w, k], weights(gu_hi), start=False, stop=(k == NK - 1))
                last.then_inc(multiplied_up, 1)

            def turn_hidden(j, u, base):
                w = u % 2
                pe.wait_ge(hidden, j + (AHEAD + base + 1))
                pe.wait_ge(h_lo_done, j + (AHEAD + base - 1))
                for i in range(NI):
                    last = nc.tensor.transpose(hid_bank[w][:, i * P:(i + 1) * P], hid[:, w, i * P:(i + 1) * P], idn[:])
                last.then_inc(hid_turned, 1)

            def down(j, u, e, base):
                w = u % 2
                pe.wait_ge(h_lo_done, j + (AHEAD + base + 1))
                pe.wait_ge(y_ready if base else base_ready, j + (AHEAD - 1))
                for i in range(NI):
                    def weights(a):
                        return a[:, i, :] if e is None else a[:, bass.ds(e * NI + (NI + i), 1), :].rearrange("p a n -> p (a n)")
                    mm(down_bank[w][:], h_hi[:, w, i], weights(d_hi), start=(i == 0), stop=False)
                    mm(down_bank[w][:], h_hi[:, w, i], weights(d_lo), start=False, stop=False)
                    last = mm(down_bank[w][:], h_lo[:, w, i], weights(d_hi), start=False, stop=(i == NI - 1))
                last.then_inc(downed, 1)

            pe.wait_ge(w_split, 3 * X)
            for name, n, base in (SHARED, ROUTED):
                def expert_of(at):
                    return pe.value_load(block_i[0:1, bass.ds(at.n, 1)], min_val=0, max_val=E - 1)

                def step(at):
                    j, u = at.n, at.slot
                    own = earlier_x = None
                    if name == "routed":
                        if not at.within(n, n):
                            own = expert_of(at)
                        if not at.within(0, 0):
                            earlier_x = expert_of(at.back(1))
                    if at.within(0, 0):
                        pe.wait_ge(rows_loaded[0], 4 * base + 16)
                        turn(x_in[:, 0], 0, 0, base + TT)
                    if not at.within(n - 1, n):
                        after = at.back(-1)
                        pe.wait_ge(rows_loaded[after.slot], after.use * 16 + (4 * base + 16))
                        turn(x_in[:, after.slot], after.n, after.slot, base + TT)
                    if not at.within(0, 0):
                        turn_hidden(at.back(1).n, u + 1, base)
                    if not at.within(n, n):
                        up(j, u, own, base)
                    if not at.within(0, 0):
                        down(at.back(1).n, u + 1, earlier_x, base)

                if name == "routed":
                    pe.wait_ge(table_ready, 1)
                    pe.wait_ge(base_ready, AHEAD + TT)
                over(pe, n, step)


def kernel(**inputs):
    import numpy as _np
    import concourse.bacc as _bacc
    from concourse import mybir as _mybir
    from concourse.bass_utils import run_bass_kernel_spmd as _run

    nc = _bacc.Bacc("TRN2", target_bir_lowering=False, num_devices=1)
    arrays, ap = {}, {}

    def give(name, a):
        a = _np.ascontiguousarray(a)
        if a.dtype == _np.bool_:
            a = a.view(_np.int32)
        arrays["in_" + name] = a
        ap[name] = nc.dram_tensor("in_" + name, a.shape, _mybir.dt.from_np(a.dtype), kind="ExternalInput").ap()

    for name in ("x", "ctx_1024", "mask_BxS2_bf0", "g_xattn", "g_ffn") + tuple(
            "L0_xattn_" + n for n in ("Wq", "bq", "Wk", "bk", "Wv", "bv", "Wo", "bo")):
        give(name, inputs[name])
    rel = _np.asarray(inputs["L0_xattn_rel_bias"])
    far = rel.shape[1] // 2
    where = _np.clip(_np.arange(P)[:, None] - _np.arange(STRIP)[None, :] + (NT - 1) * P, -far, far) + far
    give("strips", rel[:, where].transpose(1, 0, 2))
    give("ident", _np.eye(P, dtype=_np.float32))
    wq = _np.asarray(inputs["L0_ffn_Wq"])
    give("ffn_wq", wq.reshape(D, NG, HG, 2, DH).transpose(0, 1, 3, 2, 4).reshape(D, 2 * D))
    give("ffn_wo", _np.asarray(inputs["L0_ffn_Wo"]).reshape(H, 2, DH, D)[:, 0].reshape(D, D))
    for name in ("Wkva", "Wkvb"):
        give(name, inputs["L0_ffn_" + name])
    for name in ("Wgate", "expert_bias", "Wg", "Wu", "Wd", "sWg", "sWu", "sWd"):
        give(name, inputs["L0_ffn_" + name])
    give("w_ln2", inputs["L0_ffn_w_ln2"])
    give("earlier", (_np.arange(P)[:, None] < _np.arange(P)[None, :]).astype(_np.float16))
    give("starts", _np.tile(_np.arange(NB, dtype=_np.float32) * P, (P, 1)))
    give("before_e", _np.tile((_np.arange(E)[None, :] < _np.arange(E)[:, None]).astype(_np.float32), (P, 1, 1)))
    give("w_ln1", _np.asarray(inputs["L0_ffn_w_ln1"]).reshape(NK, P).T)
    freqs = (1.0 / 100000.0 ** (_np.arange(0, DH, 2, dtype=_np.float32) / DH)).astype(_np.float32)
    ang = _np.outer(_np.arange(S, dtype=_np.float32), freqs).astype(_np.float32)
    cos, sin = (_np.tile(_np.repeat(f(ang).astype(_np.float32).T, 2, axis=0), (HG, 1)) for f in (_np.cos, _np.sin))
    give("cos_sin", _np.stack([cos / (8 * WS), sin / 8, cos / WS, sin], 1).astype(_np.float32))
    swap = _np.zeros((P, P), _np.float16)
    even = _np.arange(0, P, 2)
    swap[even + 1, even], swap[even, even + 1] = -1, 1
    give("swap", swap)
    give("causal", _np.where(_np.arange(STRIP)[None, :] - (NT - 1) * P <= _np.arange(P)[:, None], 0, -1e30).astype(_np.float32))
    out = nc.dram_tensor("out_0_dram", (B, S, D), F32, kind="ExternalOutput").ap()
    mask_rows = nc.dram_tensor("mask_rows", (B * H, S), F16, kind="Internal").ap()
    qk_rows = [nc.dram_tensor(f"qk_rows{i}", (B * NG, 2 + i, 2, P, S), F16, kind="Internal").ap() for i in range(2)]
    x1 = nc.dram_tensor("x1", (B, S, D), F32, kind="Internal").ap()
    z1 = nc.dram_tensor("z1", (B, S, D), F32, kind="Internal").ap()
    xn_rows = nc.dram_tensor("xn_rows", (B * S, D), F32, kind="Internal").ap()
    base_rows = nc.dram_tensor("base_rows", (B * S, D), F32, kind="Internal").ap()
    x_sorted = nc.dram_tensor("x_sorted", (NB * P, D), F32, kind="Internal").ap()
    y_sorted = nc.dram_tensor("y_sorted", (NB * P, D), F32, kind="Internal").ap()
    used = pass_a(nc, ap["x"], ap["ctx_1024"], ap["mask_BxS2_bf0"], ap["g_xattn"],
           *[ap["L0_xattn_" + n] for n in ("Wq", "bq", "Wk", "bk", "Wv", "bv", "Wo", "bo")],
           ap["strips"], ap["ident"], x1, mask_rows, qk_rows[0])
    pass_b(nc, x1, ap["w_ln1"], ap["ffn_wq"], ap["Wkva"], ap["Wkvb"], ap["ffn_wo"], ap["cos_sin"], ap["swap"],
           ap["causal"], ap["ident"], z1, x_sorted, qk_rows[1], used)
    pass_c(nc, x1, z1, ap["g_ffn"], ap["w_ln2"], *[ap[n] for n in ("Wgate", "expert_bias", "Wg", "Wu", "Wd", "sWg", "sWu", "sWd")],
           ap["ident"], ap["earlier"], ap["starts"], ap["before_e"], xn_rows, x_sorted, y_sorted, base_rows, out)
    r = _run(nc, [arrays], core_ids=[0])
    return r.results[0]["out_0_dram"]
```
